# Optimizing a Trainium2 kernel written in Bass

```python
import numpy as np
import jax
import jax.numpy as jnp

def _softmax(x, axis=-1):
    return jax.nn.softmax(x, axis=axis)

def _gelu(x):
    return jax.nn.gelu(x, approximate=True)

def _silu(x):
    return jax.nn.silu(x)

def _sigmoid(x):
    return jax.nn.sigmoid(x)

def _layernorm(x, axis=-1, eps=1e-05):
    m = jnp.mean(x, axis=axis, keepdims=True)
    v = jnp.var(x, axis=axis, keepdims=True)
    return (x - m) / jnp.sqrt(v + eps)

def _scatter_add(tgt, idx, src, axis=0):
    return tgt.at[idx].add(src)

def _segment_sum(src, seg, n):
    return jax.ops.segment_sum(src, seg, n)
kernel_name = 'mk_seq_preln_d2_jaxref_r8_ed7764'

def setup_inputs(seed: int=0):
    np.random.seed(seed)
    _w = jnp.asarray

    def _L0_attn_setup():
        import math
        import jax, jax.numpy as jnp
        import numpy as np
        BLOCK = 64

        def build_slope_tensor(n_heads):

            def p2(n):
                start = 2.0 ** (-2.0 ** (-(math.log2(n) - 3)))
                return [start * start ** i for i in range(n)]
            if math.log2(n_heads).is_integer():
                s = p2(n_heads)
            else:
                closest = 2 ** math.floor(math.log2(n_heads))
                s = p2(closest) + p2(2 * closest)[0::2][:n_heads - closest]
            return jnp.asarray(np.array(s, dtype=np.float32))

        def lightning_attn(q, k, v, slopes, block=BLOCK):
            B, H, N, d = q.shape
            nc = N // block
            i = jnp.arange(block, dtype=q.dtype)
            diff = i[:, None] - i[None, :]
            intra_decay = jnp.where(diff >= 0, jnp.exp(-slopes[:, None, None] * diff), 0.0)
            q_decay = jnp.exp(-slopes[:, None] * i[None, :])
            k_decay = jnp.exp(-slopes[:, None] * (block - i[None, :]))
            blk_decay = jnp.exp(-slopes * block)

            def to_chunks(t):
                return t.reshape(B, H, nc, block, d).transpose(2, 0, 1, 3, 4)
            qc, kc, vc = (to_chunks(q), to_chunks(k), to_chunks(v))

            def body(S, xs):
                qb, kb, vb = xs
                scores = jnp.einsum('bhid,bhjd->bhij', qb, kb) * intra_decay[None]
                o_intra = jnp.einsum('bhij,bhjd->bhid', scores, vb)
                o_inter = jnp.einsum('bhid,bhde->bhie', qb * q_decay[None, :, :, None], S)
                S_new = blk_decay[None, :, None, None] * S + jnp.einsum('bhjd,bhje->bhde', kb * k_decay[None, :, :, None], vb)
                return (S_new, o_intra + o_inter)
            S0 = jnp.zeros((B, H, d, d), dtype=q.dtype)
            _, o = jax.lax.scan(body, S0, (qc, kc, vc))
            return o.transpose(1, 2, 0, 3, 4).reshape(B, H, N, d)
        key = jax.random.key(seed)
        k1, k2, k3 = jax.random.split(key, 3)
        dim, num_heads = (256, 16)
        B, N = (2, 512)
        x = jax.random.normal(k1, (B, N, dim), dtype=jnp.float32)
        Wqkv = jax.random.normal(k2, (dim, 3 * dim), dtype=jnp.float32) / math.sqrt(dim)
        bqkv = jnp.zeros((3 * dim,), dtype=jnp.float32)
        Wout = jax.random.normal(k3, (dim, dim), dtype=jnp.float32) / math.sqrt(dim)
        bout = jnp.zeros((dim,), dtype=jnp.float32)
        slopes = build_slope_tensor(num_heads)
        return {'x': x, 'Wqkv': Wqkv, 'bqkv': bqkv, 'Wout': Wout, 'bout': bout, 'slopes': slopes}
    _L0_attn_in = _L0_attn_setup()

    def _L0_ffn_setup():
        import jax, jax.numpy as jnp
        import numpy as np
        NUM_EXPERTS = 64
        TOP_K = 8
        HIDDEN = 256
        FFN = 96
        BATCH, SEQ = (1, 256)
        CAP_FACTOR = 2

        def _moe_forward(hidden_states, gate_w, w_gate, w_up, w_down):
            B, S, D = hidden_states.shape
            E = gate_w.shape[0]
            x = hidden_states.reshape(-1, D)
            N = x.shape[0]
            P = N * TOP_K
            C = CAP_FACTOR * P // E
            logits = x @ gate_w.T
            probs = jax.nn.softmax(logits, axis=-1)
            scores, idx = jax.lax.top_k(probs, TOP_K)
            flat_e = idx.reshape(-1)
            order = jnp.argsort(flat_e)
            e_sorted = flat_e[order]
            tok_sorted = order // TOP_K
            s_sorted = scores.reshape(-1)[order]
            counts = jnp.bincount(e_sorted, length=E)
            starts = jnp.cumsum(counts) - counts
            pos = jnp.arange(P) - starts[e_sorted]
            valid = pos < C
            safe_pos = jnp.minimum(pos, C - 1)
            xbuf = jnp.zeros((E, C, D), dtype=x.dtype).at[e_sorted, pos].set(x[tok_sorted], mode='drop')
            g = jnp.einsum('ecd,efd->ecf', xbuf, w_gate)
            u = jnp.einsum('ecd,efd->ecf', xbuf, w_up)
            y = jnp.einsum('ecf,edf->ecd', jax.nn.silu(g) * u, w_down)
            y_pair = y[e_sorted, safe_pos] * (s_sorted * valid)[:, None]
            out = jnp.zeros((N, D), dtype=x.dtype).at[tok_sorted].add(y_pair)
            return out.reshape(B, S, D)
        key = jax.random.key(seed)
        k1, k2, k3, k4, k5 = jax.random.split(key, 5)
        hidden_states = jax.random.normal(k1, (BATCH, SEQ, HIDDEN), dtype=jnp.float32)
        gate_w = jax.random.normal(k2, (NUM_EXPERTS, HIDDEN), dtype=jnp.float32) * 0.02
        w_gate = jax.random.normal(k3, (NUM_EXPERTS, FFN, HIDDEN), dtype=jnp.float32) * 0.02
        w_up = jax.random.normal(k4, (NUM_EXPERTS, FFN, HIDDEN), dtype=jnp.float32) * 0.02
        w_down = jax.random.normal(k5, (NUM_EXPERTS, HIDDEN, FFN), dtype=jnp.float32) * 0.02
        return {'hidden_states': hidden_states, 'gate_w': gate_w, 'w_gate': w_gate, 'w_up': w_up, 'w_down': w_down}
    _L0_ffn_in = _L0_ffn_setup()

    def _L1_attn_setup():
        import jax, jax.numpy as jnp
        import numpy as np
        B, N, H = (2, 512, 256)
        NH, HD = (16, 128)
        BLK = 32
        EPS = 1e-06

        def _lightning_attn(x, slope_rate, w_qkv, w_gate, w_out, norm_w):
            b, n, _ = x.shape
            h, d = (NH, HD)
            nb = n // BLK
            qkv = jax.nn.silu(jnp.einsum('bnf,of->bno', x, w_qkv))
            qkv = qkv.reshape(b, n, h, 3 * d)
            q, k, v = jnp.split(qkv, 3, axis=-1)
            q = q.transpose(0, 2, 1, 3)
            k = k.transpose(0, 2, 1, 3)
            v = v.transpose(0, 2, 1, 3)
            s = slope_rate.astype(jnp.float32)
            arr = jnp.arange(1, BLK + 1, dtype=jnp.float32)
            q_decay = jnp.exp(-s * arr[:, None])
            k_decay = jnp.exp(-s * (BLK - arr)[:, None])
            idx = arr[:, None] - arr[None, :]
            diag_decay = jnp.where(idx >= 0, jnp.exp(-s * idx), 0.0)
            block_decay = jnp.exp(-s * BLK)
            qb = q.reshape(b, h, nb, BLK, d).transpose(2, 0, 1, 3, 4)
            kb = k.reshape(b, h, nb, BLK, d).transpose(2, 0, 1, 3, 4)
            vb = v.reshape(b, h, nb, BLK, d).transpose(2, 0, 1, 3, 4)

            def step(kv, blk):
                qi, ki, vi = blk
                o_inter = jnp.einsum('bhmd,bhde->bhme', qi * q_decay, kv)
                qk = jnp.einsum('bhmd,bhnd->bhmn', qi, ki) * diag_decay
                o_intra = jnp.einsum('bhmn,bhne->bhme', qk, vi)
                kv_new = block_decay * kv + jnp.einsum('bhmd,bhme->bhde', ki * k_decay, vi)
                return (kv_new, o_inter + o_intra)
            kv0 = jnp.zeros((b, h, d, d), dtype=jnp.float32)
            _, out = jax.lax.scan(step, kv0, (qb, kb, vb))
            out = out.transpose(1, 2, 0, 3, 4).reshape(b, h, n, d)
            out = out.transpose(0, 2, 1, 3).reshape(b, n, h * d)
            var = jnp.mean(out * out, axis=-1, keepdims=True)
            out = norm_w * (out * jax.lax.rsqrt(var + EPS))
            gate = jax.nn.sigmoid(jnp.einsum('bnf,of->bno', x, w_gate))
            return jnp.einsum('bno,fo->bnf', gate * out, w_out)
        key = jax.random.key(seed)
        ks = jax.random.split(key, 5)
        scale = 0.02
        x = jax.random.normal(ks[0], (B, N, H), dtype=jnp.float32)
        slopes = (1.0 / 2.0 ** (8.0 * np.arange(1, NH + 1) / NH)).astype(np.float32)
        slope_rate = jnp.asarray(slopes).reshape(NH, 1, 1)
        w_qkv = jax.random.normal(ks[1], (3 * NH * HD, H), dtype=jnp.float32) * scale
        w_gate = jax.random.normal(ks[2], (NH * HD, H), dtype=jnp.float32) * scale
        w_out = jax.random.normal(ks[3], (H, NH * HD), dtype=jnp.float32) * scale
        norm_w = jnp.ones((NH * HD,), dtype=jnp.float32)
        return {'hidden_states': x, 'slope_rate': slope_rate, 'w_qkv': w_qkv, 'w_gate': w_gate, 'w_out': w_out, 'norm_w': norm_w}
    _L1_attn_in = _L1_attn_setup()

    def _L1_ffn_setup():
        import jax, jax.numpy as jnp
        import numpy as np
        DIM_IN = 256
        DIM_HIDDEN = 1024
        key = jax.random.key(seed)
        k_x, k_g, k_u, k_d = jax.random.split(key, 4)
        s_in = 1.0 / np.sqrt(DIM_IN)
        s_hid = 1.0 / np.sqrt(DIM_HIDDEN)
        x = jax.random.normal(k_x, (4, 256, DIM_IN), dtype=jnp.float32)
        w_gate = jax.random.uniform(k_g, (DIM_HIDDEN, DIM_IN), jnp.float32, -s_in, s_in)
        w_up = jax.random.uniform(k_u, (DIM_HIDDEN, DIM_IN), jnp.float32, -s_in, s_in)
        w_down = jax.random.uniform(k_d, (DIM_IN, DIM_HIDDEN), jnp.float32, -s_hid, s_hid)
        return {'x': x, 'w_gate': w_gate, 'w_up': w_up, 'w_down': w_down}
    _L1_ffn_in = _L1_ffn_setup()
    _d = {'L0_attn_x': _L0_attn_in['x'], 'L0_attn_Wqkv': _L0_attn_in['Wqkv'], 'L0_attn_bqkv': _L0_attn_in['bqkv'], 'L0_attn_Wout': _L0_attn_in['Wout'], 'L0_attn_bout': _L0_attn_in['bout'], 'L0_attn_slopes': _L0_attn_in['slopes'], 'L0_ffn_gate_w': _L0_ffn_in['gate_w'], 'L0_ffn_w_gate': _L0_ffn_in['w_gate'], 'L0_ffn_w_up': _L0_ffn_in['w_up'], 'L0_ffn_w_down': _L0_ffn_in['w_down'], 'L1_attn_slope_rate': _L1_attn_in['slope_rate'], 'L1_attn_w_qkv': _L1_attn_in['w_qkv'], 'L1_attn_w_gate': _L1_attn_in['w_gate'], 'L1_attn_w_out': _L1_attn_in['w_out'], 'L1_attn_norm_w': _L1_attn_in['norm_w'], 'L1_ffn_w_gate': _L1_ffn_in['w_gate'], 'L1_ffn_w_up': _L1_ffn_in['w_up'], 'L1_ffn_w_down': _L1_ffn_in['w_down']}
    _x0 = _d['L0_attn_x']
    _d['L0_attn_x'] = jax.random.normal(jax.random.fold_in(jax.random.key(seed), 1), (8, 256, 256), dtype=_x0.dtype)
    del _x0
    return _d

def reference(L0_attn_x, L0_attn_Wqkv, L0_attn_bqkv, L0_attn_Wout, L0_attn_bout, L0_attn_slopes, L0_ffn_gate_w, L0_ffn_w_gate, L0_ffn_w_up, L0_ffn_w_down, L1_attn_slope_rate, L1_attn_w_qkv, L1_attn_w_gate, L1_attn_w_out, L1_attn_norm_w, L1_ffn_w_gate, L1_ffn_w_up, L1_ffn_w_down):

    def _L0_attn_ref(x, Wqkv, bqkv, Wout, bout, slopes):
        import math
        import jax, jax.numpy as jnp
        import numpy as np
        BLOCK = 64

        def build_slope_tensor(n_heads):

            def p2(n):
                start = 2.0 ** (-2.0 ** (-(math.log2(n) - 3)))
                return [start * start ** i for i in range(n)]
            if math.log2(n_heads).is_integer():
                s = p2(n_heads)
            else:
                closest = 2 ** math.floor(math.log2(n_heads))
                s = p2(closest) + p2(2 * closest)[0::2][:n_heads - closest]
            return jnp.asarray(np.array(s, dtype=np.float32))

        def lightning_attn(q, k, v, slopes, block=BLOCK):
            B, H, N, d = q.shape
            nc = N // block
            i = jnp.arange(block, dtype=q.dtype)
            diff = i[:, None] - i[None, :]
            intra_decay = jnp.where(diff >= 0, jnp.exp(-slopes[:, None, None] * diff), 0.0)
            q_decay = jnp.exp(-slopes[:, None] * i[None, :])
            k_decay = jnp.exp(-slopes[:, None] * (block - i[None, :]))
            blk_decay = jnp.exp(-slopes * block)

            def to_chunks(t):
                return t.reshape(B, H, nc, block, d).transpose(2, 0, 1, 3, 4)
            qc, kc, vc = (to_chunks(q), to_chunks(k), to_chunks(v))

            def body(S, xs):
                qb, kb, vb = xs
                scores = jnp.einsum('bhid,bhjd->bhij', qb, kb) * intra_decay[None]
                o_intra = jnp.einsum('bhij,bhjd->bhid', scores, vb)
                o_inter = jnp.einsum('bhid,bhde->bhie', qb * q_decay[None, :, :, None], S)
                S_new = blk_decay[None, :, None, None] * S + jnp.einsum('bhjd,bhje->bhde', kb * k_decay[None, :, :, None], vb)
                return (S_new, o_intra + o_inter)
            S0 = jnp.zeros((B, H, d, d), dtype=q.dtype)
            _, o = jax.lax.scan(body, S0, (qc, kc, vc))
            return o.transpose(1, 2, 0, 3, 4).reshape(B, H, N, d)
        B, N, C = x.shape
        H = slopes.shape[0]
        hd = C // H
        qkv = (x @ Wqkv + bqkv).reshape(B, N, 3, H, hd)
        qkv = qkv.transpose(2, 0, 3, 1, 4)
        q, k, v = (qkv[0], qkv[1], qkv[2])
        attn = lightning_attn(q, k, v, slopes)
        out = attn.transpose(0, 2, 1, 3).reshape(B, N, C)
        return out @ Wout + bout

    def _L0_ffn_ref(hidden_states, gate_w, w_gate, w_up, w_down):
        import jax, jax.numpy as jnp
        import numpy as np
        NUM_EXPERTS = 64
        TOP_K = 8
        HIDDEN = 256
        FFN = 96
        BATCH, SEQ = (1, 256)
        CAP_FACTOR = 2

        def _moe_forward(hidden_states, gate_w, w_gate, w_up, w_down):
            B, S, D = hidden_states.shape
            E = gate_w.shape[0]
            x = hidden_states.reshape(-1, D)
            N = x.shape[0]
            P = N * TOP_K
            C = CAP_FACTOR * P // E
            logits = x @ gate_w.T
            probs = jax.nn.softmax(logits, axis=-1)
            scores, idx = jax.lax.top_k(probs, TOP_K)
            flat_e = idx.reshape(-1)
            order = jnp.argsort(flat_e)
            e_sorted = flat_e[order]
            tok_sorted = order // TOP_K
            s_sorted = scores.reshape(-1)[order]
            counts = jnp.bincount(e_sorted, length=E)
            starts = jnp.cumsum(counts) - counts
            pos = jnp.arange(P) - starts[e_sorted]
            valid = pos < C
            safe_pos = jnp.minimum(pos, C - 1)
            xbuf = jnp.zeros((E, C, D), dtype=x.dtype).at[e_sorted, pos].set(x[tok_sorted], mode='drop')
            g = jnp.einsum('ecd,efd->ecf', xbuf, w_gate)
            u = jnp.einsum('ecd,efd->ecf', xbuf, w_up)
            y = jnp.einsum('ecf,edf->ecd', jax.nn.silu(g) * u, w_down)
            y_pair = y[e_sorted, safe_pos] * (s_sorted * valid)[:, None]
            out = jnp.zeros((N, D), dtype=x.dtype).at[tok_sorted].add(y_pair)
            return out.reshape(B, S, D)
        return _moe_forward(hidden_states, gate_w, w_gate, w_up, w_down)

    def _L1_attn_ref(hidden_states, slope_rate, w_qkv, w_gate, w_out, norm_w):
        import jax, jax.numpy as jnp
        import numpy as np
        B, N, H = (2, 512, 256)
        NH, HD = (16, 128)
        BLK = 32
        EPS = 1e-06

        def _lightning_attn(x, slope_rate, w_qkv, w_gate, w_out, norm_w):
            b, n, _ = x.shape
            h, d = (NH, HD)
            nb = n // BLK
            qkv = jax.nn.silu(jnp.einsum('bnf,of->bno', x, w_qkv))
            qkv = qkv.reshape(b, n, h, 3 * d)
            q, k, v = jnp.split(qkv, 3, axis=-1)
            q = q.transpose(0, 2, 1, 3)
            k = k.transpose(0, 2, 1, 3)
            v = v.transpose(0, 2, 1, 3)
            s = slope_rate.astype(jnp.float32)
            arr = jnp.arange(1, BLK + 1, dtype=jnp.float32)
            q_decay = jnp.exp(-s * arr[:, None])
            k_decay = jnp.exp(-s * (BLK - arr)[:, None])
            idx = arr[:, None] - arr[None, :]
            diag_decay = jnp.where(idx >= 0, jnp.exp(-s * idx), 0.0)
            block_decay = jnp.exp(-s * BLK)
            qb = q.reshape(b, h, nb, BLK, d).transpose(2, 0, 1, 3, 4)
            kb = k.reshape(b, h, nb, BLK, d).transpose(2, 0, 1, 3, 4)
            vb = v.reshape(b, h, nb, BLK, d).transpose(2, 0, 1, 3, 4)

            def step(kv, blk):
                qi, ki, vi = blk
                o_inter = jnp.einsum('bhmd,bhde->bhme', qi * q_decay, kv)
                qk = jnp.einsum('bhmd,bhnd->bhmn', qi, ki) * diag_decay
                o_intra = jnp.einsum('bhmn,bhne->bhme', qk, vi)
                kv_new = block_decay * kv + jnp.einsum('bhmd,bhme->bhde', ki * k_decay, vi)
                return (kv_new, o_inter + o_intra)
            kv0 = jnp.zeros((b, h, d, d), dtype=jnp.float32)
            _, out = jax.lax.scan(step, kv0, (qb, kb, vb))
            out = out.transpose(1, 2, 0, 3, 4).reshape(b, h, n, d)
            out = out.transpose(0, 2, 1, 3).reshape(b, n, h * d)
            var = jnp.mean(out * out, axis=-1, keepdims=True)
            out = norm_w * (out * jax.lax.rsqrt(var + EPS))
            gate = jax.nn.sigmoid(jnp.einsum('bnf,of->bno', x, w_gate))
            return jnp.einsum('bno,fo->bnf', gate * out, w_out)
        return _lightning_attn(hidden_states, slope_rate, w_qkv, w_gate, w_out, norm_w)

    def _L1_ffn_ref(x, w_gate, w_up, w_down):
        import jax, jax.numpy as jnp
        import numpy as np
        DIM_IN = 256
        DIM_HIDDEN = 1024
        gate = jnp.einsum('bsd,hd->bsh', x, w_gate)
        up = jnp.einsum('bsd,hd->bsh', x, w_up)
        gated = jax.nn.silu(gate) * up
        return jnp.einsum('bsh,dh->bsd', gated, w_down)
    x = L0_attn_x
    x = x + _L0_attn_ref(_layernorm(x, axis=-1), L0_attn_Wqkv, L0_attn_bqkv, L0_attn_Wout, L0_attn_bout, L0_attn_slopes)
    x = x + _L0_ffn_ref(_layernorm(x, axis=-1), L0_ffn_gate_w, L0_ffn_w_gate, L0_ffn_w_up, L0_ffn_w_down)
    x = x + _L1_attn_ref(_layernorm(x, axis=-1), L1_attn_slope_rate, L1_attn_w_qkv, L1_attn_w_gate, L1_attn_w_out, L1_attn_norm_w)
    x = x + _L1_ffn_ref(_layernorm(x, axis=-1), L1_ffn_w_gate, L1_ffn_w_up, L1_ffn_w_down)
    return x

_drawn_inputs = setup_inputs


def setup_inputs(seed=0):
    import zlib

    import numpy as np

    out = dict(_drawn_inputs(seed))
    spreads = {'L0_attn_bqkv': (0.0, 0.1), 'L0_attn_bout': (0.0, 0.8), 'L1_attn_norm_w': (1.0, 0.6)}
    factors = {'L0_ffn_gate_w': 8.0,
     'L0_ffn_w_gate': 8.0,
     'L0_ffn_w_up': 8.0,
     'L0_ffn_w_down': 8.0,
     'L1_attn_slope_rate': 3.324,
     'L1_attn_w_gate': 8.0,
     'L1_ffn_w_gate': 8.0,
     'L1_ffn_w_up': 8.0,
     'L1_ffn_w_down': 8.0}
    for name, (base, spread) in spreads.items():
        noise = np.random.default_rng([zlib.crc32(name.encode()), seed]).standard_normal(out[name].shape)
        drawn = base * np.exp(spread * noise) if base else spread * noise
        out[name] = jnp.asarray(drawn.astype(out[name].dtype))
    for name, factor in factors.items():
        out[name] = (out[name] * factor).astype(out[name].dtype)
    return out
```

```python
from contextlib import ExitStack

import numpy as np

import concourse.bass as bass
from concourse import mybir

F32 = mybir.dt.float32
BF16 = mybir.dt.bfloat16
I32 = mybir.dt.int32
U32 = mybir.dt.uint32
ALU = mybir.AluOpType
ACT = mybir.ActivationFunctionType
AX = mybir.AxisListType.X

P = 128
NB, SEQ, D = 8, 256, 256
T = NB * SEQ
TB = SEQ // P
DC = D // P
H0, HD0 = 16, 16
G0 = 4
NG = H0 // G0
E, TOPK, FE = 64, 8, 96
CAP = 2 * T * TOPK // E
CT = CAP // P
H1, HD1 = 16, 128
C1 = H1 * HD1
FH = 1024
HJ = FH // P
EPS_LN, EPS_RMS = 1e-5, 1e-6
LOWEST = -3.0e38
STAGE_WORDS = 21800
DROPPED = 65536.0

CONSTS = {}
_at = 0
for _name, _n in (("ident", P), ("dist", SEQ), ("causal", SEQ), ("before", P), ("ones", P),
                  ("parity", 2), ("slot0", E), ("half", 4)):
    CONSTS[_name] = (_at, _at + _n)
    _at += _n
NCONST = _at


def shape_constants():
    p = np.arange(P)[:, None]
    i = np.arange(SEQ)[None, :]
    c = np.zeros((P, NCONST), np.float32)

    def put(name, a):
        c[:, CONSTS[name][0]:CONSTS[name][1]] = a

    put("ident", p == np.arange(P)[None, :])
    put("dist", np.maximum(i - p, 0))
    put("causal", i >= p)
    put("before", p < np.arange(P)[None, :])
    put("ones", 1.0)
    put("parity", np.concatenate([(p // HD0) % 2 == 0, (p // HD0) % 2 == 1], 1))
    put("slot0", np.arange(E)[None, :] * CAP + 1.0)
    put("half", -0.5)
    return c


class Steps:

    def __init__(self, eng, sem, per, turn):
        self.eng, self.sem, self.per, self.base, self.n = eng, sem, per, turn * per, 0

    def done(self, ins):
        ins.then_inc(self.sem, 1)
        self.n += 1

    def settled(self, alone=None):
        self.eng.wait_ge(self.sem, self.base + self.n)
        if alone is not None:
            self.eng.sem_inc(alone, 1)

    def end(self):
        assert self.n == self.per, (self.n, self.per)


def build(nc, x, consts, ids, w0, b0qk, b0v, w0out, b0out, slopes0, gatew, moe_in, moe_down,
          slopes1, w1qk, w1v, w1g, w1o, norm1, wf_gate, wf_up, wf_down, out,
          xhat_rows, slot_ids, y_rows):
    with ExitStack() as ctx:
        def sb(name, shape, dt=F32):
            return ctx.enter_context(nc.sbuf_tensor(name, shape, dt))

        def sem(name):
            return ctx.enter_context(nc.semaphore(name))

        bank = [ctx.enter_context(nc.psum_tensor(f"bank{i}", [P, 512], F32)) for i in range(8)]

        X = sb("X", [P, T // P, D])
        cst = sb("cst", [P, NCONST])
        tokens = sb("tokens", [P, T // P], I32)
        slope = sb("slope", [P, H0 + H1])
        nslope = sb("nslope", [P, H0 + H1])
        D1 = sb("D1", [P, H1, SEQ])
        W1qk = sb("W1qk", [P, DC, H1, 2, HD1])
        W1v = sb("W1v", [P, DC, C1])
        W1g = sb("W1g", [P, DC, H1, HD1])
        W1o = sb("W1o", [P, H1, D])
        nrm = sb("nrm", [P, H1])
        SLOT = sb("SLOT", [P, NB, TB * TOPK], I32)
        WGT = sb("WGT", [P, NB, TB * TOPK])
        ones_b = sb("ones_b", [P, P], BF16)
        before_b = sb("before_b", [P, P], BF16)
        bn = sb("bn", [P, TB, 6])
        bn2 = sb("bn2", [P, TB, 6])
        mv = sb("mv", [P, TB, 2])
        mv2 = sb("mv2", [P, TB, 2])
        var = sb("var", [P, TB])
        var2 = sb("var2", [P, TB])
        rstd = sb("rstd", [P, TB])
        rstd2 = sb("rstd2", [P, TB])

        def const(name):
            a, b = CONSTS[name]
            return cst[:, a:b]

        ident, dist, causal, half = const("ident"), const("dist"), const("causal"), const("half")
        parity, slot0, ones = const("parity"), const("slot0"), const("ones")

        STAGE = sb("STAGE", [P, STAGE_WORDS])

        def stage():
            at = [0]

            def take(shape, dt=F32):
                n = int(np.prod(shape))
                v = STAGE[:, at[0]:at[0] + n]
                at[0] += n
                assert at[0] <= STAGE_WORDS, at[0]
                if dt != F32:
                    v = v.bitcast(dt)
                if len(shape) > 1:
                    names = "abcd"[:len(shape)]
                    v = v.rearrange(f"p ({' '.join(names)}) -> p {' '.join(names)}",
                                    **{n: s for n, s in zip(names, shape)})
                return v
            return take

        take = stage()
        D0 = take([H0, SEQ])
        W0 = take([DC, 3 * D])
        W0o = take([DC, D])
        GW = take([DC, E])
        bqk = take([4])
        bqp = take([4])
        bv = take([D])
        bo = take([D])
        xhA = take([TB, D])
        xTA = take([DC, SEQ])
        kT = take([DC, SEQ])
        qz = take([H0, SEQ])
        vA = take([TB, D])
        PA = [take([3, 512]) for _ in range(2)]
        oA = take([TB, D])
        oTA = take([DC, SEQ])
        x1 = take([TB, D])
        xh2 = take([TB, D])
        x2T = take([DC, SEQ])
        logit = take([TB, E])
        left = take([TB, E])
        sel = take([TB, E])
        prob = take([TB, E])
        keep = take([TB, E])
        key = take([TB, E])
        top = take([TB, 8])
        ntop = take([TB])
        psumx = take([TB])
        rsum = take([TB])
        slotf = take([TB, TOPK])
        eq = take([TB, TOPK, E])
        wsum = take([TB * TOPK])
        scat = take([TB * TOPK], I32)
        tok = take([TB], I32)
        zero = take([P * CAP * E // P // P // 2])
        sel_b = sb("sel_b", [P, TB, E], BF16)
        seen_b = sb("seen_b", [P, TB, E], BF16)

        take = stage()
        Wgu = [take([DC, 2, FE]) for _ in range(2)]
        Wdn = [take([D]) for _ in range(2)]
        idx = [take([CT], I32) for _ in range(2)]
        xg = [take([CT, D]) for _ in range(2)]
        xTB = [take([DC, CAP]) for _ in range(2)]
        silu = [take([CAP]) for _ in range(2)]
        hB = [take([CAP]) for _ in range(2)]
        yo = [take([CT, D]) for _ in range(2)]

        take = stage()
        WF = take([DC, 2, FH])
        WFd = take([HJ, D])
        rows = take([TB * TOPK, D])
        sidx = take([TB * TOPK], I32)
        comb = take([TB, D])
        xh3 = take([TB, D])
        x3T = take([DC, SEQ])
        qkD = [take([2, SEQ]) for _ in range(2)]
        vD = take([TB, C1])
        wcur = take([TB * TOPK])
        PD = [take([3, P]) for _ in range(2)]
        gD = [take([SEQ]) for _ in range(2)]
        goD = [take([SEQ]) for _ in range(2)]
        sq = [take([SEQ]) for _ in range(2)]
        ssq = take([SEQ])
        x3 = take([TB, D])
        xh4 = xh3
        x4T = take([DC, SEQ])
        sgF = [take([SEQ]) for _ in range(2)]
        hF = rows.rearrange("p a b -> p (a b)")[:, 0:HJ * SEQ].rearrange("p (a b) -> p a b", a=HJ)
        outs = take([TB, D])

        NAMES = """
        x_loaded consts_loaded small_loaded w0_loaded table_zeroed zero_ready nslope_ready decay0_exp
        decay1_exp decay0_ready decay1_ready setup_dve bf_ready cleared
        a_xhat a_xT_ps a_xT a_q_ps a_k_ps a_v_ps a_q a_k a_v a_sc_ps a_prob a_o_ps a_o a_oT_ps a_oT
        a_out_ps a_x1 a_xh2 a_x2T_ps a_x2T a_log_ps a_ln_steps a_var a_rstd a_ln2_steps a_var2 a_rstd2
        a_sel_steps a_ntop a_exp a_selb a_rank_ps a_slot_steps a_scat a_tok a_ids a_stored a_x1sum
        b_x_ps b_xa b_xb b_gu_ps b_silu b_h b_y_ps b_ya b_yb
        l1_loaded w1o_scaled dve_carrier pool_carrier
        d_sidx d_wcur d_comb_steps d_ln3_steps d_var3 d_rstd3 d_xh3 d_x3T_ps d_x3T d_v_ps d_v
        d_qk_ps d_qk d_g_ps d_g d_s_ps d_p d_o_ps d_go d_sq d_ssq d_y_ps d_ssq_ps d_var d_rms d_x3
        d_ln4_steps d_var4 d_rstd4 d_xh4 d_x4T_ps d_x4T d_h_ps d_sg d_h d_dn_ps d_out d_stored
        """.split()
        S = {n: sem(n) for n in NAMES}
        b_wgu = [sem(f"b_wgu{i}") for i in range(2)]
        b_wdn = [sem(f"b_wdn{i}") for i in range(2)]
        b_idx = [sem(f"b_idx{i}") for i in range(2)]
        b_rows = [sem(f"b_rows{i}") for i in range(2)]
        b_stored = [sem(f"b_stored{i}") for i in range(2)]
        d_row = [sem(f"d_row{i}") for i in range(TB * TOPK)]

        def after(eng, name, value):
            if not isinstance(value, int) or value > 0:
                eng.wait_ge(S[name], value)

        NSETUP_LOADS = 5
        NL1_LOADS = 8
        B2 = 2
        LASTB = NB - 1

        block = ctx.enter_context(nc.Block())

        @block.sync
        def _(sp):
            sp.dma_start(cst[:], consts).then_inc(S["consts_loaded"], 16)
            sp.dma_start(X[:], x).then_inc(S["x_loaded"], 16)
            sp.dma_start(W0, w0).then_inc(S["w0_loaded"], 16)
            sp.dma_start(W0o, w0out).then_inc(S["w0_loaded"], 16)
            sp.dma_start(GW, gatew).then_inc(S["w0_loaded"], 16)
            sp.wait_ge(S["zero_ready"], 1)
            n = zero.shape[1]
            tab = slot_ids.rearrange("(a p n) o -> a p (n o)", a=E * CAP // (P * n), p=P)
            for a in range(tab.shape[0]):
                sp.dma_start(tab[a], zero.bitcast(I32)).then_inc(S["table_zeroed"], 16)
            sp.dma_start(W1qk[:], w1qk).then_inc(S["l1_loaded"], 16)
            sp.dma_start(W1v[:], w1v).then_inc(S["l1_loaded"], 16)
            sp.dma_start(W1g[:], w1g).then_inc(S["l1_loaded"], 16)
            sp.dma_start(W1o[:], w1o).then_inc(S["l1_loaded"], 16)
            sp.dma_start(nrm[:], norm1).then_inc(S["l1_loaded"], 16)

            def store_xhat(b):
                sp.wait_ge(S["a_xh2"], b + 1)
                sp.dma_start(xhat_rows[bass.ds(b * SEQ, SEQ), :].rearrange("(t p) d -> p t d", p=P),
                             xh2).then_inc(S["a_stored"], 16)

            with sp.Fori(0, NB) as b:
                store_xhat(b)

            sp.wait_ge(S["a_ids"], 16 * NB * TB * TOPK)
            sp.wait_ge(S["a_slot_steps"], NB * SLOT_STEPS)
            sp.wait_ge(S["a_stored"], 16 * NB)

            def load_ids(e, s):
                if not isinstance(e, int) or e >= B2:
                    sp.wait_ge(b_rows[s], (e - s) * 32)
                sp.dma_start(idx[s], slot_ids[bass.ds(e * CAP, CAP), :].rearrange(
                    "(p c) o -> p (c o)", c=CT)).then_inc(b_idx[s], 16)

            def load_gate_up(e, s):
                after(sp, "b_gu_ps", 2 * e - 2)
                sp.dma_start(Wgu[s], moe_in[bass.ds(e, 1)].rearrange("a p (c w f) -> (a p) c w f", c=DC, w=2)
                             ).then_inc(b_wgu[s], 16)

            def load_down(e, s):
                sp.dma_start(Wdn[s][0:FE, :], moe_down[bass.ds(e, 1)].rearrange("a f d -> (a f) d")
                             ).then_inc(b_wdn[s], 16)

            def store_expert(e, s):
                sp.wait_ge(S["b_ya"], e + 1)
                sp.wait_ge(S["b_yb"], e + 1)
                sp.dma_start(y_rows[bass.ds(e * CAP, CAP), :].rearrange("(p c) d -> p c d", c=CT),
                             yo[s]).then_inc(b_stored[s], 16)

            def expert_step(e, s, more_ids=True, more_weights=True):
                if more_ids:
                    load_ids(e + 2, s)
                if more_weights:
                    load_gate_up(e + 1, 1 - s)
                store_expert(e - 1, 1 - s)
                if more_weights:
                    load_down(e + 1, 1 - s)

            load_ids(0, 0)
            load_ids(1, 1)
            for s in range(2):
                load_gate_up(s, s)
                load_down(s, s)
            load_ids(2, 0)
            with sp.Fori(0, E // B2 - 2) as i:
                expert_step(i * 2 + 1, 1)
                expert_step(i * 2 + 2, 0)
            expert_step(E - 3, 1)
            expert_step(E - 2, 0, more_ids=False)
            expert_step(E - 1, 1, more_ids=False, more_weights=False)
            store_expert(E - 1, 1)

            sp.wait_ge(S["b_ya"], E)
            for s in range(2):
                sp.wait_ge(b_stored[s], 16 * E // 2)
            sp.dma_start(WF[:, :, 0, :], wf_gate).then_inc(S["l1_loaded"], 16)
            sp.dma_start(WF[:, :, 1, :], wf_up).then_inc(S["l1_loaded"], 16)
            sp.dma_start(WFd, wf_down).then_inc(S["l1_loaded"], 16)

            with sp.Fori(0, NB) as b:
                sp.wait_ge(S["d_out"], b + 1)
                sp.dma_start(out[bass.ds(b * SEQ, SEQ), :].rearrange("(t p) d -> p t d", p=P),
                             outs).then_inc(S["d_stored"], 16)
            sp.wait_ge(S["d_stored"], 16 * NB)

        def a_scatter(pool, b):
            pool.wait_ge(S["a_scat"], b + 1)
            pool.tensor_copy(tok, tokens[:, bass.ds(b * TB, TB)]).then_inc(S["a_tok"], 1)
            pool.wait_ge(S["a_tok"], b + 1)
            pool.sem_inc(S["pool_carrier"], 1)
            for t in range(TB):
                for k in range(TOPK):
                    c = t * TOPK + k
                    pool.indirect_dma_start(
                        slot_ids, bass.IndirectOffsetOnAxis(ap=scat[:, c:c + 1].bitcast(U32), axis=0),
                        tok[:, t:t + 1], None, bounds_check=E * CAP - 1, oob_is_err=False,
                    ).then_inc(S["a_ids"], 16)
            pool.wait_ge(S["a_ids"], (b + 1) * (16 * TB * TOPK))

        def rsqrt(pool, ready, done, v, r, n):
            pool.wait_ge(S[ready], n)
            pool.tensor_tensor(r, v, half[:, 0:TB], ALU.pow).then_inc(S[done], 1)

        @block.gpsimd
        def _(pool):
            pool.memset(zero, 0.0).then_inc(S["zero_ready"], 1)
            pool.memset(qz, 0.0).then_inc(S["cleared"], 1)
            pool.dma_start(tokens[:], ids).then_inc(S["small_loaded"], 16)
            pool.dma_start(slope[:, 0:H0], slopes0.partition_broadcast(P)).then_inc(S["small_loaded"], 16)
            pool.dma_start(slope[:, H0:], slopes1.partition_broadcast(P)).then_inc(S["small_loaded"], 16)
            pool.dma_start(bqk, b0qk).then_inc(S["small_loaded"], 16)
            pool.dma_start(bv, b0v.partition_broadcast(P)).then_inc(S["small_loaded"], 16)
            pool.dma_start(bo, b0out.partition_broadcast(P)).then_inc(S["small_loaded"], 16)
            pool.wait_ge(S["consts_loaded"], 16)
            pool.wait_ge(S["small_loaded"], 16 * 6)
            rsqrt(pool, "a_var", "a_rstd", var[:], rstd[:], 1)

            def turn(b, ahead, back, scatter):
                if back:
                    rsqrt(pool, "a_var2", "a_rstd2", var2[:], rstd2[:], b)
                if ahead:
                    rsqrt(pool, "a_var", "a_rstd", var[:], rstd[:], b + 2)
                if scatter:
                    a_scatter(pool, b - 2)

            turn(0, True, False, False)
            turn(1, True, True, False)
            pool.wait_ge(S["table_zeroed"], 16 * (E * CAP // (P * zero.shape[1])))
            with pool.Fori(2, LASTB) as b:
                turn(b, True, True, True)
            turn(LASTB, False, True, True)
            turn(NB, False, True, True)
            a_scatter(pool, LASTB)

            pool.wait_ge(S["a_stored"], 16 * NB)
            pool.wait_ge(S["a_slot_steps"], NB * SLOT_STEPS)

            def gather(e, s):
                pool.wait_ge(b_idx[s], (e - s) * 8 + 16)
                if not isinstance(e, int) or e >= B2:
                    pool.wait_ge(S["b_x_ps"], e - 1)
                pool.sem_inc(S["pool_carrier"], 1)
                for c in range(CT):
                    pool.indirect_dma_start(
                        xg[s][:, c, :], None, xhat_rows,
                        bass.IndirectOffsetOnAxis(ap=idx[s][:, c:c + 1].bitcast(U32), axis=0),
                        bounds_check=T - 1, oob_is_err=False).then_inc(b_rows[s], 16)

            gather(0, 0)
            gather(1, 1)
            with pool.Fori(1, E // B2) as i:
                for s in range(B2):
                    gather(i * B2 + s, s)

            for s in range(2):
                pool.wait_ge(b_stored[s], 16 * E // 2)
            pool.wait_ge(S["b_ya"], E)

            def slots_of(b):
                pool.tensor_copy(sidx, SLOT[:, b, :] if isinstance(b, int) else
                                 SLOT[:, bass.ds(b, 1), :].rearrange("p a n -> p (a n)")
                                 ).then_inc(S["d_sidx"], 1)
                pool.wait_ge(S["d_sidx"], b + 1)
                pool.sem_inc(S["pool_carrier"], 1)

            def gather_row(c):
                pool.indirect_dma_start(
                    rows[:, c, :], None, y_rows,
                    bass.IndirectOffsetOnAxis(ap=sidx[:, c:c + 1].bitcast(U32), axis=0),
                    bounds_check=E * CAP - 1, oob_is_err=False).then_inc(d_row[c], 16)

            slots_of(0)
            for c in range(TB * TOPK):
                gather_row(c)
            rsqrt(pool, "d_var3", "d_rstd3", var[:], rstd[:], 1)

            def dturn(b, ahead, back):
                if back:
                    rsqrt(pool, "d_var", "d_rms", var2[:], rstd2[:], b)
                    rsqrt(pool, "d_var4", "d_rstd4", var2[:], rstd2[:], b)
                if ahead:
                    pool.wait_ge(S["d_comb_steps"], (b + 1) * COMB_STEPS)
                    slots_of(b + 1)
                for h in range(H1):
                    if ahead and h < TOPK:
                        if h == 0 and back:
                            pool.wait_ge(S["d_dn_ps"], b)
                            pool.sem_inc(S["pool_carrier"], 1)
                        for t in range(TB):
                            gather_row(t * TOPK + h)
                    if ahead and h == 11:
                        rsqrt(pool, "d_var3", "d_rstd3", var[:], rstd[:], b + 2)
                    if h > 0:
                        pool.wait_ge(S["d_sq"], b * H1 + h + 1)
                        if h > 1:
                            pool.wait_ge(S["d_ssq"], b * (H1 - 1) + h - 1)
                        pool.tensor_tensor(ssq, ssq, sq[h % 2], ALU.add).then_inc(S["d_ssq"], 1)

            dturn(0, True, False)
            with pool.Fori(1, LASTB) as b:
                dturn(b, True, True)
            dturn(LASTB, False, True)
            rsqrt(pool, "d_var", "d_rms", var2[:], rstd2[:], NB)
            rsqrt(pool, "d_var4", "d_rstd4", var2[:], rstd2[:], NB)

        @block.tensor
        def _(pe):
            def transpose4(dst, src):
                for c in range(DC):
                    for t in range(TB):
                        ins = pe.transpose(dst[:, c * SEQ + t * P:c * SEQ + (t + 1) * P],
                                           src[:, t, c * P:(c + 1) * P], ident)
                return ins

            def a_front1(b):
                pe.wait_ge(S["a_xhat"], b + 1)
                after(pe, "a_v", b)
                transpose4(bank[0], xhA).then_inc(S["a_xT_ps"], 1)

            def a_back1(b):
                pe.wait_ge(S["a_o"], b + 1)
                after(pe, "a_x2T", b)
                transpose4(bank[1], oA).then_inc(S["a_oT_ps"], 1)

            def a_front2(b):
                pe.wait_ge(S["a_xT"], b + 1)
                if isinstance(b, int) and b == 0:
                    pe.wait_ge(S["w0_loaded"], 48)
                after(pe, "a_x1", b - 1)
                for q, (bk, done) in enumerate(((2, "a_q_ps"), (3, "a_k_ps"))):
                    if q:
                        after(pe, "a_slot_steps", (b - 1) * SLOT_STEPS)
                    for m in range(DC):
                        for c in range(DC):
                            ins = pe.matmul(bank[bk][:, m * SEQ:(m + 1) * SEQ],
                                            W0[:, c, q * D + m * P:q * D + (m + 1) * P], xTA[:, c, :],
                                            start=(c == 0), stop=(c == DC - 1))
                    ins.then_inc(S[done], 1)
                for t in range(TB):
                    for c in range(DC):
                        ins = pe.matmul(bank[0][:, t * D:(t + 1) * D], xTA[:, c, t * P:(t + 1) * P],
                                        W0[:, c, 2 * D:3 * D], start=(c == 0), stop=(c == DC - 1))
                ins.then_inc(S["a_v_ps"], 1)

            def a_out(b):
                pe.wait_ge(S["a_oT"], b + 1)
                after(pe, "a_q", b + 2 if not isinstance(b, int) or b < LASTB else NB)
                for t in range(TB):
                    for c in range(DC):
                        ins = pe.matmul(bank[2][:, t * D:(t + 1) * D], oTA[:, c, t * P:(t + 1) * P],
                                        W0o[:, c, :], start=(c == 0), stop=(c == DC - 1))
                ins.then_inc(S["a_out_ps"], 1)

            def a_scores(b, g):
                if g == 0:
                    pe.wait_ge(S["a_q"], b + 1)
                    pe.wait_ge(S["a_k"], b + 1)
                m = g * G0 * HD0 // P
                heads = slice(g * G0, (g + 1) * G0)
                for n in range(3):
                    after(pe, "a_prob", b * (3 * NG) + 3 * g + n - 2)
                    if n < 2:
                        ins = pe.matmul(bank[4 + n][:, :], kT[:, m, 0:P],
                                        qz[:, g * G0 + 2 * n:g * G0 + 2 * n + 2, :], start=True, stop=True)
                    else:
                        ins = pe.matmul(bank[4 + n][:, :], kT[:, m, P:SEQ], qz[:, heads, P:SEQ],
                                        start=True, stop=True)
                    ins.then_inc(S["a_sc_ps"], 1)

            def a_values(b, g):
                if g == 0:
                    pe.wait_ge(S["a_v"], b + 1)
                    after(pe, "a_o", b)
                pe.wait_ge(S["a_prob"], b * (3 * NG) + 3 * g + 3)
                Pg = PA[g % 2]
                for hh in range(G0):
                    h = g * G0 + hh
                    col = (hh % 2) * SEQ
                    vh = slice(h * HD0, (h + 1) * HD0)
                    pe.matmul(bank[7][:, h * HD0:(h + 1) * HD0], Pg[:, hh // 2, col:col + P], vA[:, 0, vh],
                              start=True, stop=True)
                    pe.matmul(bank[7][:, D + h * HD0:D + (h + 1) * HD0], Pg[:, hh // 2, col + P:col + SEQ],
                              vA[:, 0, vh], start=True, stop=False)
                    ins = pe.matmul(bank[7][:, D + h * HD0:D + (h + 1) * HD0], Pg[:, 2, hh * P:(hh + 1) * P],
                                    vA[:, 1, vh], start=False, stop=True)
                if g == NG - 1:
                    ins.then_inc(S["a_o_ps"], 1)

            def a_back2(b):
                pe.wait_ge(S["a_xh2"], b + 1)
                transpose4(bank[1], xh2).then_inc(S["a_x2T_ps"], 1)

            def a_logits(b):
                pe.wait_ge(S["a_x2T"], b + 1)
                after(pe, "a_slot_steps", b * SLOT_STEPS)
                after(pe, "a_k", b + 2 if not isinstance(b, int) or b < LASTB else NB)
                for t in range(TB):
                    for c in range(DC):
                        ins = pe.matmul(bank[3][:, t * E:(t + 1) * E], x2T[:, c, t * P:(t + 1) * P],
                                        GW[:, c, :], start=(c == 0), stop=(c == DC - 1))
                ins.then_inc(S["a_log_ps"], 1)

            def a_rank(b):
                pe.wait_ge(S["a_selb"], 2 * b + 2)
                for t in range(TB):
                    o = bank[3][:, 2 * P + t * E:2 * P + (t + 1) * E]
                    pe.matmul(o, before_b[:], sel_b[:, t, :], start=True, stop=False)
                    ins = pe.matmul(o, ones_b[:], seen_b[:, t, :], start=False, stop=True)
                ins.then_inc(S["a_rank_ps"], 1)

            def turn(b, front, back):
                if front:
                    a_front1(b)
                if back:
                    a_back1(b - 1)
                if front:
                    a_front2(b)
                if back:
                    a_out(b - 1)
                if front:
                    a_scores(b, 0)
                if back:
                    a_back2(b - 1)
                if front:
                    a_scores(b, 1)
                if back:
                    a_logits(b - 1)
                if front:
                    a_values(b, 0)
                    a_scores(b, 2)
                    a_values(b, 1)
                    a_scores(b, 3)
                    a_values(b, 2)
                if back:
                    a_rank(b - 1)
                if front:
                    a_values(b, 3)

            pe.wait_ge(S["consts_loaded"], 16)
            pe.wait_ge(S["bf_ready"], 2)
            pe.wait_ge(S["cleared"], 1)
            turn(0, True, False)
            with pe.Fori(1, NB) as b:
                turn(b, True, True)
            turn(NB, False, True)
            pe.wait_ge(S["a_slot_steps"], NB * SLOT_STEPS)

            def b_trans(e, s):
                pe.wait_ge(b_rows[s], (e - s) * 32 + 64)
                after(pe, "b_xa", e)
                after(pe, "b_xb", e)
                for c in range(DC):
                    for t in range(CT):
                        ins = pe.transpose(bank[c][:, t * P:(t + 1) * P], xg[s][:, t, c * P:(c + 1) * P], ident)
                ins.then_inc(S["b_x_ps"], 1)

            def b_hidden(e, s):
                pe.wait_ge(b_wgu[s], (e - s) * 8 + 16)
                pe.wait_ge(S["b_xa"], e + 1)
                pe.wait_ge(S["b_xb"], e + 1)
                after(pe, "b_h", e - 1)
                for w in range(2):
                    for c in range(DC):
                        ins = pe.matmul(bank[2 + 2 * s + w][0:FE, :], Wgu[s][:, c, w, :], xTB[s][:, c, :],
                                        start=(c == 0), stop=(c == DC - 1))
                    ins.then_inc(S["b_gu_ps"], 1)

            def b_out(e, s):
                pe.wait_ge(S["b_h"], e + 1)
                pe.wait_ge(b_wdn[s], (e - s) * 8 + 16)
                for n in range(2):
                    after(pe, "b_ya" if n == 0 else "b_yb", e)
                    for t in range(2):
                        q = 2 * n + t
                        ins = pe.matmul(bank[6 + n][:, t * D:(t + 1) * D], hB[s][0:FE, q * P:(q + 1) * P],
                                        Wdn[s][0:FE, :], start=True, stop=True)
                    ins.then_inc(S["b_y_ps"], 1)

            b_trans(0, 0)
            b_hidden(0, 0)
            b_trans(1, 1)
            with pe.Fori(0, E // B2 - 1) as i:
                for s in (1, 0):
                    e = i * 2 + (1 if s else 2)
                    b_hidden(e, s)
                    b_trans(e + 1, 1 - s)
                    b_out(e - 1, 1 - s)
            b_hidden(E - 1, 1)
            b_out(E - 2, 0)
            b_out(E - 1, 1)
            pe.wait_ge(S["b_ya"], E)
            pe.wait_ge(S["b_yb"], E)

            pe.wait_ge(S["w1o_scaled"], 1)
            pe.wait_ge(S["l1_loaded"], 16 * NL1_LOADS)

            def d_trans3(b):
                pe.wait_ge(S["d_xh3"], b + 1)
                after(pe, "d_x4T", b - 1)
                after(pe, "d_var", b)
                transpose4(bank[0], xh3).then_inc(S["d_x3T_ps"], 1)

            def d_values(b):
                pe.wait_ge(S["d_x3T"], b + 1)
                after(pe, "d_go", b * H1)
                after(pe, "d_sq", b * H1)
                after(pe, "d_out", b - 1)
                for n in range(8):
                    t, g = n % 2, n // 2
                    if n >= 6:
                        pe.wait_ge(S["d_v"], b * 8 + n - 5)
                    for c in range(DC):
                        ins = pe.matmul(bank[1 + n % 6][:, :], x3T[:, c, t * P:(t + 1) * P],
                                        W1v[:, c, g * 512:(g + 1) * 512], start=(c == 0), stop=(c == DC - 1))
                    ins.then_inc(S["d_v_ps"], 1)

            def d_project(b, h):
                after(pe, "d_qk", b * H1 + h - 1)
                if h == 0:
                    pe.wait_ge(S["d_v"], b * 8 + 8)
                for w in range(2):
                    for c in range(DC):
                        ins = pe.matmul(bank[1 + h % 2][:, w * SEQ:(w + 1) * SEQ], W1qk[:, c, h, w, :],
                                        x3T[:, c, :], start=(c == 0), stop=(c == DC - 1))
                ins.then_inc(S["d_qk_ps"], 1)
                after(pe, "d_sq", b * H1 + h - 1)
                after(pe, "d_go", b * H1 + h - 1)
                for c in range(DC):
                    ins = pe.matmul(bank[5 + h % 2][:, 0:SEQ], W1g[:, c, h, :], x3T[:, c, :],
                                    start=(c == 0), stop=(c == DC - 1))
                ins.then_inc(S["d_g_ps"], 1)

            def d_scores(b, h):
                pe.wait_ge(S["d_qk"], b * H1 + h + 1)
                after(pe, "d_p", b * H1 + h - 1)
                qk = qkD[h % 2]
                pe.matmul(bank[3 + h % 2][:, 0:SEQ], qk[:, 1, 0:P], qk[:, 0, :], start=True, stop=True)
                pe.matmul(bank[3 + h % 2][:, SEQ:SEQ + P], qk[:, 1, P:SEQ], qk[:, 0, P:SEQ],
                          start=True, stop=True).then_inc(S["d_s_ps"], 1)

            def d_attend(b, h):
                pe.wait_ge(S["d_p"], b * H1 + h + 1)
                pe.wait_ge(S["d_g"], b * H1 + h + 1)
                Ph = PD[h % 2]
                o = bank[5 + h % 2]
                vh = slice(h * HD1, (h + 1) * HD1)
                pe.matmul(o[:, SEQ:2 * SEQ], vD[:, 0, vh], Ph[:, 0:2, :], start=True, stop=False)
                pe.matmul(o[:, SEQ + P:2 * SEQ], vD[:, 1, vh], Ph[:, 2, :], start=False,
                          stop=True).then_inc(S["d_o_ps"], 1)

            def d_project_out(b, h):
                pe.wait_ge(S["d_go"], b * H1 + h + 1)
                if h == 0:
                    after(pe, "d_x3", b)
                for t in range(TB):
                    ins = pe.matmul(bank[7][:, t * D:(t + 1) * D], goD[h % 2][:, t * P:(t + 1) * P],
                                    W1o[:, h, :], start=(h == 0 and t == 0), stop=(h == H1 - 1),
                                    skip_group_check=True)
                ins.then_inc(S["d_y_ps"], 1)

            def d_square_sums(b):
                pe.wait_ge(S["d_ssq"], (b + 1) * (H1 - 1))
                for t in range(TB):
                    ins = pe.matmul(bank[0][:, t:t + 1], ssq[:, t * P:(t + 1) * P], ones[:, 0:1],
                                    start=True, stop=True)
                ins.then_inc(S["d_ssq_ps"], 1)

            def d_trans4(b):
                pe.wait_ge(S["d_xh4"], b + 1)
                after(pe, "d_x3T", b + 2 if not isinstance(b, int) or b < LASTB else NB)
                transpose4(bank[0], xh4).then_inc(S["d_x4T_ps"], 1)

            def d_ffn(b):
                pe.wait_ge(S["d_x4T"], b + 1)
                for j in range(HJ):
                    if j == 0:
                        after(pe, "d_v", b * 8 + 16 if not isinstance(b, int) or b < LASTB else NB * 8)
                    if j >= 4:
                        pe.wait_ge(S["d_h"], b * HJ + j - 3)
                    for w in range(2):
                        for c in range(DC):
                            ins = pe.matmul(bank[1 + j % 4][:, w * SEQ:(w + 1) * SEQ],
                                            WF[:, c, w, j * P:(j + 1) * P], x4T[:, c, :],
                                            start=(c == 0), stop=(c == DC - 1))
                    ins.then_inc(S["d_h_ps"], 1)
                for t in range(TB):
                    for j in range(HJ):
                        if t == 0:
                            pe.wait_ge(S["d_h"], b * HJ + j + 1)
                        ins = pe.matmul(bank[5][:, t * D:(t + 1) * D], hF[:, j, t * P:(t + 1) * P],
                                        WFd[:, j, :], start=(j == 0), stop=(j == HJ - 1))
                ins.then_inc(S["d_dn_ps"], 1)

            def dturn(b, front, back):
                if front:
                    d_trans3(b)
                    d_values(b)
                if back:
                    d_trans4(b - 1)
                    d_ffn(b - 1)
                if front:
                    if back:
                        after(pe, "d_out", b)
                    d_project(b, 0)
                    for h in range(H1):
                        d_scores(b, h)
                        if h + 1 < H1:
                            d_project(b, h + 1)
                        d_attend(b, h)
                        if h:
                            d_project_out(b, h - 1)
                    d_project_out(b, H1 - 1)
                    d_square_sums(b)

            dturn(0, True, False)
            with pe.Fori(1, NB) as b:
                dturn(b, True, True)
            dturn(NB, False, True)

        @block.scalar
        def _(act):
            act.wait_ge(S["consts_loaded"], 16)
            act.wait_ge(S["nslope_ready"], 1)
            for l, (dst, done) in enumerate(((D0, "decay0_exp"), (D1, "decay1_exp"))):
                for h in range(H0):
                    n = l * H0 + h
                    ins = nc.scalar.activation(dst[:, h, :], dist, ACT.Exp, scale=nslope[:, n:n + 1])
                ins.then_inc(S[done], 1)

            def copy(dst, src, ready, n, done):
                act.wait_ge(S[ready], n)
                nc.scalar.activation(dst, src, ACT.Copy).then_inc(S[done], 1)

            def split(a, n=DC):
                return a.rearrange("p (a b) -> p a b", a=n)

            def a_back(b):
                after(act, "a_out_ps", b)
                copy(oTA, split(bank[1][:, :]), "a_oT_ps", b + 1, "a_oT")

            def a_back2(b):
                after(act, "a_log_ps", b)
                copy(x2T, split(bank[1][:, :]), "a_x2T_ps", b + 1, "a_x2T")

            def a_exp(b):
                act.wait_ge(S["a_ntop"], b + 1)
                after(act, "a_slot_steps", b * SLOT_STEPS)
                for t in range(TB):
                    ins = nc.scalar.activation(prob[:, t, :], logit[:, t, :], ACT.Exp, bias=ntop[:, t:t + 1],
                                               accum_out=psumx[:, t:t + 1])
                ins.then_inc(S["a_exp"], 1)

            def a_end(b):
                after(act, "a_oT_ps", b)
                copy(oA, split(bank[7][:, :], TB), "a_o_ps", b + 1, "a_o")

            def turn(b, front, back):
                if front:
                    after(act, "a_v_ps", b)
                    copy(xTA, split(bank[0][:, :]), "a_xT_ps", b + 1, "a_xT")
                if back:
                    a_back(b - 1)
                if front:
                    act.wait_ge(S["a_q_ps"], b + 1)
                    after(act, "a_sc_ps", b * (3 * NG))
                    for h in range(H0):
                        m, g, odd = h * HD0 // P, (h * HD0 % P) // 32, h % 2
                        r = slice(32 * g, 32 * g + 32)
                        ins = nc.scalar.activation(
                            qz[r, h, :], bank[2][r, m * SEQ:(m + 1) * SEQ], ACT.Identity,
                            scale=parity[r, odd:odd + 1], bias=bqp[r, 2 * odd + m:2 * odd + m + 1])
                    ins.then_inc(S["a_q"], 1)
                if back:
                    a_back2(b - 1)
                    a_exp(b - 1)
                if front:
                    a_end(b)

            act.wait_ge(S["setup_dve"], 1)
            act.wait_ge(S["cleared"], 1)
            turn(0, True, False)
            with act.Fori(1, NB) as b:
                turn(b, True, True)
            turn(NB, False, True)
            act.wait_ge(S["a_slot_steps"], NB * SLOT_STEPS)
            act.wait_ge(S["a_stored"], 16 * NB)
            act.wait_ge(S["a_ids"], 16 * NB * TB * TOPK)

            def b_copy(e, s):
                after(act, "b_gu_ps", 2 * e - 2)
                copy(xTB[s][:, 0, :], bank[0][:, :], "b_x_ps", e + 1, "b_xa")

            def b_silu(e, s):
                after(act, "b_h", e - 1)
                act.wait_ge(S["b_gu_ps"], 2 * e + 1)
                nc.scalar.activation(silu[s][0:FE, :], bank[2 + 2 * s][0:FE, :], ACT.Silu).then_inc(S["b_silu"], 1)

            def b_result(e, s):
                if not isinstance(e, int) or e >= 2:
                    act.wait_ge(b_stored[s], (e - s) * 8)
                copy(yo[s][:, 0:2, :], split(bank[6][:, :]), "b_y_ps", 2 * e + 1, "b_ya")

            b_copy(0, 0)
            b_silu(0, 0)
            b_copy(1, 1)
            with act.Fori(0, E // B2 - 1) as i:
                for s in (1, 0):
                    e = i * 2 + (1 if s else 2)
                    b_silu(e, s)
                    b_copy(e + 1, 1 - s)
                    b_result(e - 1, 1 - s)
            b_silu(E - 1, 1)
            b_result(E - 2, 0)
            b_result(E - 1, 1)
            for s in range(2):
                act.wait_ge(b_stored[s], 16 * E // 2)
            act.wait_ge(S["b_yb"], E)

            def d_front(b):
                after(act, "d_y_ps", b * H1)
                copy(x3T, split(bank[0][:, :]), "d_x3T_ps", b + 1, "d_x3T")
                for n in range(8):
                    t, g = n % 2, n // 2
                    act.wait_ge(S["d_v_ps"], b * 8 + n + 1)
                    nc.scalar.activation(vD[:, t, g * 512:(g + 1) * 512], bank[1 + n % 6][:, :],
                                         ACT.Silu).then_inc(S["d_v"], 1)

            def d_back(b):
                after(act, "d_h_ps", b * HJ)
                copy(x4T, split(bank[0][:, :]), "d_x4T_ps", b + 1, "d_x4T")
                for j in range(HJ):
                    act.wait_ge(S["d_h_ps"], b * HJ + j + 1)
                    if j > 1:
                        act.wait_ge(S["d_h"], b * HJ + j - 1)
                    nc.scalar.activation(sgF[j % 2], bank[1 + j % 4][:, 0:SEQ], ACT.Silu).then_inc(S["d_sg"], 1)

            def d_silu(b, h):
                after(act, "d_s_ps", b * H1 + h - 1)
                act.wait_ge(S["d_qk_ps"], b * H1 + h + 1)
                nc.scalar.activation(qkD[h % 2][:, :, :], bank[1 + h % 2][:, :].rearrange("p (a b) -> p a b", a=2),
                                     ACT.Silu).then_inc(S["d_qk"], 1)
                act.wait_ge(S["d_g_ps"], b * H1 + h + 1)
                after(act, "d_go", b * H1 + h - 1)
                nc.scalar.activation(gD[h % 2], bank[5 + h % 2][:, 0:SEQ], ACT.Tanh, scale=0.5).then_inc(S["d_g"], 1)

            def d_square(b, h):
                if h == 0:
                    after(act, "d_ssq_ps", b)
                elif h > 1:
                    after(act, "d_ssq", b * (H1 - 1) + h - 2)
                elif h == 1:
                    after(act, "d_ssq", b * (H1 - 1))
                act.wait_ge(S["d_o_ps"], b * H1 + h + 1)
                nc.scalar.activation(ssq if h == 0 else sq[h % 2], bank[5 + h % 2][:, SEQ:2 * SEQ],
                                     ACT.Square).then_inc(S["d_sq"], 1)

            def dturn(b, front, back):
                if front:
                    d_front(b)
                if back:
                    d_back(b - 1)
                if front:
                    d_silu(b, 0)
                    for h in range(H1):
                        if h + 1 < H1:
                            d_silu(b, h + 1)
                        d_square(b, h)

            dturn(0, True, False)
            with act.Fori(1, NB) as b:
                dturn(b, True, True)
            dturn(NB, False, True)

        @block.vector
        def _(dve):
            dve.wait_ge(S["small_loaded"], 16 * 6)
            nc.vector.tensor_scalar(nslope[:], slope[:], -1.0, None, ALU.mult).then_inc(S["nslope_ready"], 1)
            dve.wait_ge(S["consts_loaded"], 16)
            nc.vector.tensor_copy(ones_b[:], ones).then_inc(S["bf_ready"], 1)
            nc.vector.tensor_copy(before_b[:], const("before")).then_inc(S["bf_ready"], 1)
            nc.vector.memset(seen_b[:], 0.0)
            for odd in range(2):
                ins = nc.vector.tensor_scalar(bqp[:, 2 * odd:2 * odd + 2], bqk[:, 0:2], parity[:, odd:odd + 1],
                                              None, ALU.mult)
            ins.then_inc(S["setup_dve"], 1)

            def decay(dst, ready, done):
                dve.wait_ge(S[ready], 1)
                for g in range(4):
                    hs = slice(4 * g, 4 * g + 4)
                    ins = nc.vector.tensor_tensor(dst[:, hs, :], dst[:, hs, :],
                                                  causal.unsqueeze(1).broadcast_to([P, 4, SEQ]), ALU.mult)
                ins.then_inc(S[done], 1)

            def normalize(src, dst, bn_, mv_, var_, rstd_, steps_sem, per, turn, var_done, rstd_done, free, done):
                st = Steps(dve, S[steps_sem], per, turn)
                for t in range(TB):
                    st.done(nc.vector.bn_stats(bn_[:, t, :], src(t)))
                st.settled(S["dve_carrier"])
                for t in range(TB):
                    st.done(nc.vector.bn_aggr(mv_[:, t, :], bn_[:, t, :]))
                st.settled()
                st.end()
                nc.vector.tensor_scalar(var_[:], mv_[:, :, 1], EPS_LN, None, ALU.add).then_inc(S[var_done], 1)
                for name, n in free:
                    after(dve, name, n)
                dve.wait_ge(S[rstd_done], turn + 1)
                for t in range(TB):
                    ins = nc.vector.tensor_scalar(dst[:, t, :], src(t), mv_[:, t, 0:1], rstd_[:, t:t + 1],
                                                  ALU.subtract, ALU.mult)
                ins.then_inc(S[done], 1)

            def xtile(b, t):
                return X[:, b * TB + t, :] if isinstance(b, int) else \
                    X[:, bass.ds(b * TB + t, 1), :].rearrange("p a d -> p (a d)")

            def a_norm(b):
                normalize(lambda t: xtile(b, t), xhA, bn, mv, var, rstd, "a_ln_steps", 4, b, "a_var", "a_rstd",
                          (("a_xT_ps", b),), "a_xhat")

            def a_keys(b):
                dve.wait_ge(S["a_k_ps"], b + 1)
                after(dve, "a_sc_ps", b * (3 * NG))
                for m in range(DC):
                    ins = nc.vector.tensor_scalar(kT[:, m, :], bank[3][:, m * SEQ:(m + 1) * SEQ],
                                                  bqk[:, 2 + m:3 + m], None, ALU.add)
                ins.then_inc(S["a_k"], 1)

            def a_vals(b):
                dve.wait_ge(S["a_v_ps"], b + 1)
                after(dve, "a_o_ps", b)
                nc.vector.tensor_tensor(vA, bank[0][:, :].rearrange("p (a b) -> p a b", a=TB),
                                        bv.unsqueeze(1).broadcast_to([P, TB, D]), ALU.add).then_inc(S["a_v"], 1)

            def a_mask(b, g):
                if g < 2:
                    after(dve, "a_o_ps", b)
                for n in range(3):
                    dve.wait_ge(S["a_sc_ps"], b * (3 * NG) + 3 * g + n + 1)
                    if n < 2:
                        h = g * G0 + 2 * n
                        o, s, d = PA[g % 2][:, n, :].rearrange("p (a b) -> p a b", a=2), \
                            bank[4 + n][:, :].rearrange("p (a b) -> p a b", a=2), D0[:, h:h + 2, :]
                    else:
                        o, s, d = PA[g % 2][:, n, :].rearrange("p (a b) -> p a b", a=G0), \
                            bank[4 + n][:, :].rearrange("p (a b) -> p a b", a=G0), D0[:, g * G0:g * G0 + G0, 0:P]
                    nc.vector.tensor_tensor(o, s, d, ALU.mult).then_inc(S["a_prob"], 1)

            def a_residual(b):
                dve.wait_ge(S["a_out_ps"], b + 1)
                nc.vector.tensor_tensor(x1, bank[2][:, :].rearrange("p (a b) -> p a b", a=TB),
                                        bo.unsqueeze(1).broadcast_to([P, TB, D]), ALU.add).then_inc(S["a_x1"], 1)
                dve.wait_ge(S["a_x1"], b + 1)
                for t in range(TB):
                    nc.vector.tensor_tensor(x1[:, t, :], x1[:, t, :], xtile(b, t), ALU.add).then_inc(S["a_x1sum"], 1)
                dve.wait_ge(S["a_x1sum"], 2 * b + 2)
                for t in range(TB):
                    nc.vector.tensor_scalar(xtile(b, t), x1[:, t, :], 1.0, None, ALU.mult)
                normalize(lambda t: x1[:, t, :], xh2, bn2, mv2, var2, rstd2, "a_ln2_steps", 4, b, "a_var2",
                          "a_rstd2", (("a_x2T_ps", b), ("a_stored", 16 * b)), "a_xh2")

            def a_select(b):
                st = Steps(dve, S["a_sel_steps"], SEL_STEPS, b)
                dve.wait_ge(S["a_log_ps"], b + 1)
                st.done(nc.vector.tensor_copy(logit, bank[3][:, 0:TB * E].rearrange("p (a b) -> p a b", a=TB)))
                st.settled(S["dve_carrier"])
                for t in range(TB):
                    st.done(nc.vector.max(top[:, t, :], logit[:, t, :]))
                st.settled()
                nc.vector.tensor_scalar(ntop, top[:, :, 0], -1.0, None, ALU.mult).then_inc(S["a_ntop"], 1)
                for t in range(TB):
                    st.done(nc.vector.match_replace(left[:, t, :], top[:, t, :], logit[:, t, :], LOWEST))
                st.settled()
                st.done(nc.vector.tensor_scalar(sel, left, LOWEST, None, ALU.is_le))
                st.settled()
                st.end()
                after(dve, "a_rank_ps", b)
                nc.vector.tensor_copy(sel_b[:], sel).then_inc(S["a_selb"], 1)
                nc.vector.tensor_tensor(seen_b[:, 1, :], seen_b[:, 0, :], sel[:, 0, :],
                                        ALU.add).then_inc(S["a_selb"], 1)

            def a_slots(b):
                st = Steps(dve, S["a_slot_steps"], SLOT_STEPS, b)
                dve.wait_ge(S["a_exp"], b + 1)
                st.done(nc.vector.reciprocal(rsum, psumx))
                dve.wait_ge(S["a_rank_ps"], b + 1)
                pos = bank[3][:, 2 * P:2 * P + TB * E].rearrange("p (a b) -> p a b", a=TB)
                st.done(nc.vector.tensor_tensor(seen_b[:, 0, :], seen_b[:, 1, :], sel[:, 1, :], ALU.add))
                st.done(nc.vector.tensor_scalar(keep, pos, float(CAP), None, ALU.is_lt))
                st.done(nc.vector.scalar_tensor_tensor(
                    out=key, in0=pos, scalar=float(CAP - 1),
                    in1=slot0.unsqueeze(1).broadcast_to([P, TB, E]), op0=ALU.min, op1=ALU.add))
                st.settled()
                st.done(nc.vector.tensor_tensor(key, key, sel, ALU.mult))
                st.done(nc.vector.tensor_tensor(keep, keep, sel, ALU.mult))
                st.settled()
                for t in range(TB):
                    st.done(nc.vector.scalar_tensor_tensor(out=prob[:, t, :], in0=prob[:, t, :],
                                                           scalar=rsum[:, t:t + 1], in1=keep[:, t, :],
                                                           op0=ALU.mult, op1=ALU.mult))
                    st.done(nc.vector.max(slotf[:, t, :], key[:, t, :]))
                st.settled()
                st.done(nc.vector.tensor_tensor(eq, key.unsqueeze(2).broadcast_to([P, TB, TOPK, E]),
                                                slotf.unsqueeze(3).broadcast_to([P, TB, TOPK, E]), ALU.is_equal))
                st.settled()
                st.done(nc.vector.tensor_tensor(eq, eq, prob.unsqueeze(2).broadcast_to([P, TB, TOPK, E]), ALU.mult))
                st.settled()
                st.done(nc.vector.tensor_reduce(wsum, eq.rearrange("p a b c -> p (a b) c"), AX, ALU.add))
                st.settled()
                flat = slotf.rearrange("p a b -> p (a b)")

                def of_batch(tensor):
                    return tensor[:, b, :] if isinstance(b, int) else \
                        tensor[:, bass.ds(b, 1), :].rearrange("p a n -> p (a n)")

                st.done(nc.vector.tensor_scalar(of_batch(WGT), wsum, 1.0, None, ALU.mult))
                st.done(nc.vector.tensor_scalar(of_batch(SLOT), flat, -1.0, None, ALU.add))
                st.done(nc.vector.tensor_scalar(wsum, wsum, 0.0, DROPPED, ALU.is_le, ALU.mult))
                st.settled()
                st.done(nc.vector.scalar_tensor_tensor(out=wsum, in0=flat, scalar=-1.0, in1=wsum,
                                                       op0=ALU.add, op1=ALU.add))
                st.settled()
                after(dve, "a_ids", b * (16 * TB * TOPK))
                nc.vector.tensor_copy(scat, wsum).then_inc(S["a_scat"], 1)
                st.end()

            def turn(b, ahead, front, back):
                if front:
                    a_keys(b)
                    a_vals(b)
                if back:
                    a_residual(b - 1)
                if ahead:
                    a_norm(b + 1)
                if front:
                    a_mask(b, 0)
                    a_mask(b, 1)
                if back:
                    a_select(b - 1)
                if front:
                    a_mask(b, 2)
                if back:
                    a_slots(b - 1)
                if front:
                    a_mask(b, 3)

            dve.wait_ge(S["x_loaded"], 16)
            a_norm(0)
            decay(D0, "decay0_exp", "decay0_ready")
            decay(D1, "decay1_exp", "decay1_ready")
            turn(0, True, True, False)
            with dve.Fori(1, LASTB) as b:
                turn(b, True, True, True)
            turn(LASTB, False, True, True)
            turn(NB, False, False, True)
            dve.wait_ge(S["a_ids"], 16 * NB * TB * TOPK)
            dve.wait_ge(S["a_stored"], 16 * NB)

            dve.wait_ge(S["l1_loaded"], 16 * 5)
            for h in range(H1):
                ins = nc.vector.tensor_scalar(W1o[:, h, :], W1o[:, h, :], nrm[:, h:h + 1], 0.5, ALU.mult, ALU.mult)
            ins.then_inc(S["w1o_scaled"], 1)

            def b_copy(e, s):
                after(dve, "b_gu_ps", 2 * e - 2)
                dve.wait_ge(S["b_x_ps"], e + 1)
                nc.vector.tensor_copy(xTB[s][:, 1, :], bank[1][:, :]).then_inc(S["b_xb"], 1)

            def b_mul(e, s):
                dve.wait_ge(S["b_silu"], e + 1)
                dve.wait_ge(S["b_gu_ps"], 2 * e + 2)
                after(dve, "b_y_ps", 2 * e - 2)
                nc.vector.tensor_tensor(hB[s][0:FE, :], silu[s][0:FE, :], bank[3 + 2 * s][0:FE, :],
                                        ALU.mult).then_inc(S["b_h"], 1)

            def b_result(e, s):
                if not isinstance(e, int) or e >= 2:
                    dve.wait_ge(b_stored[s], (e - s) * 8)
                dve.wait_ge(S["b_y_ps"], 2 * e + 2)
                nc.vector.tensor_copy(yo[s][:, 2:4, :], bank[7][:, :].rearrange("p (a b) -> p a b", a=2)
                                      ).then_inc(S["b_yb"], 1)

            b_copy(0, 0)
            b_mul(0, 0)
            b_copy(1, 1)
            with dve.Fori(0, E // B2 - 1) as i:
                for s in (1, 0):
                    e = i * 2 + (1 if s else 2)
                    b_mul(e, s)
                    b_copy(e + 1, 1 - s)
                    b_result(e - 1, 1 - s)
            b_mul(E - 1, 1)
            b_result(E - 2, 0)
            b_result(E - 1, 1)
            for s in range(2):
                dve.wait_ge(b_stored[s], 16 * E // 2)
            dve.wait_ge(S["b_ya"], E)

            def d_combine(b, k):
                for t in range(TB):
                    c = t * TOPK + k
                    dve.wait_ge(d_row[c], b * 16 + 16)
                if k:
                    dve.wait_ge(S["d_comb_steps"], b * COMB_STEPS + TB * k)
                for t in range(TB):
                    c = t * TOPK + k
                    nc.vector.scalar_tensor_tensor(
                        out=comb[:, t, :], in0=rows[:, c, :], scalar=wcur[:, c:c + 1],
                        in1=xtile(b, t) if k == 0 else comb[:, t, :],
                        op0=ALU.mult, op1=ALU.add).then_inc(S["d_comb_steps"], 1)

            def d_weights(b):
                after(dve, "d_comb_steps", b * COMB_STEPS)
                nc.vector.tensor_scalar(wcur[:], WGT[:, b, :] if isinstance(b, int) else
                                        WGT[:, bass.ds(b, 1), :].rearrange("p a n -> p (a n)"),
                                        1.0, None, ALU.mult).then_inc(S["d_wcur"], 1)
                dve.wait_ge(S["d_wcur"], b + 1)

            def d_norm3(b):
                dve.wait_ge(S["d_comb_steps"], (b + 1) * COMB_STEPS)
                for t in range(TB):
                    nc.vector.tensor_scalar(xtile(b, t), comb[:, t, :], 1.0, None, ALU.mult)
                normalize(lambda t: comb[:, t, :], xh3, bn, mv, var, rstd, "d_ln3_steps", 4, b, "d_var3",
                          "d_rstd3", (("d_x4T_ps", b - 1), ("d_x3T_ps", b)), "d_xh3")

            def d_mask(b, h):
                dve.wait_ge(S["d_s_ps"], b * H1 + h + 1)
                after(dve, "d_o_ps", b * H1 + h - 1)
                s = bank[3 + h % 2]
                nc.vector.tensor_tensor(PD[h % 2][:, 0:2, :].rearrange("p a b -> p (a b)"), s[:, 0:SEQ],
                                        D1[:, h, :], ALU.mult)
                nc.vector.tensor_tensor(PD[h % 2][:, 2, :], s[:, SEQ:SEQ + P], D1[:, h, 0:P],
                                        ALU.mult).then_inc(S["d_p"], 1)

            def d_gate(b, h):
                dve.wait_ge(S["d_sq"], b * H1 + h + 1)
                after(dve, "d_y_ps", b * H1 + h - 1)
                nc.vector.scalar_tensor_tensor(out=goD[h % 2], in0=gD[h % 2], scalar=1.0,
                                               in1=bank[5 + h % 2][:, SEQ:2 * SEQ], op0=ALU.add,
                                               op1=ALU.mult).then_inc(S["d_go"], 1)

            def d_residual(b):
                dve.wait_ge(S["d_ssq_ps"], b + 1)
                nc.vector.tensor_scalar(var2[:], bank[0][:, 0:TB], 1.0 / C1, EPS_RMS, ALU.mult,
                                        ALU.add).then_inc(S["d_var"], 1)
                dve.wait_ge(S["d_rms"], b + 1)
                for t in range(TB):
                    ins = nc.vector.scalar_tensor_tensor(out=x3[:, t, :], in0=bank[7][:, t * D:(t + 1) * D],
                                                         scalar=rstd2[:, t:t + 1], in1=xtile(b, t),
                                                         op0=ALU.mult, op1=ALU.add)
                ins.then_inc(S["d_x3"], 1)
                dve.wait_ge(S["d_x3"], b + 1)
                normalize(lambda t: x3[:, t, :], xh4, bn2, mv2, var2, rstd2, "d_ln4_steps", 4, b, "d_var4",
                          "d_rstd4", (("d_x3T_ps", b + 2 if not isinstance(b, int) or b < LASTB else NB),), "d_xh4")

            def d_ffn(b):
                for j in range(HJ):
                    dve.wait_ge(S["d_sg"], b * HJ + j + 1)
                    if j == 0:
                        after(dve, "d_dn_ps", b)
                    nc.vector.tensor_tensor(hF[:, j, :], sgF[j % 2], bank[1 + j % 4][:, SEQ:2 * SEQ],
                                            ALU.mult).then_inc(S["d_h"], 1)
                dve.wait_ge(S["d_dn_ps"], b + 1)
                after(dve, "d_stored", b * 16)
                nc.vector.tensor_tensor(outs, bank[5][:, :].rearrange("p (a b) -> p a b", a=TB), x3,
                                        ALU.add).then_inc(S["d_out"], 1)

            def dturn(b, ahead, front, back):
                if back:
                    d_residual(b - 1)
                    d_ffn(b - 1)
                if front:
                    for h in range(H1):
                        d_mask(b, h)
                        if ahead and h == 1:
                            d_weights(b + 1)
                        if ahead and 2 <= h < 2 + TOPK:
                            d_combine(b + 1, h - 2)
                        if ahead and h == 11:
                            d_norm3(b + 1)
                        d_gate(b, h)

            d_weights(0)
            for k in range(TOPK):
                d_combine(0, k)
            d_norm3(0)
            dturn(0, True, True, False)
            with dve.Fori(1, LASTB) as b:
                dturn(b, True, True, True)
            dturn(LASTB, False, True, True)
            dturn(NB, False, False, True)


SLOT_STEPS = 17
SEL_STEPS = 6
COMB_STEPS = TB * TOPK


def _chunks(a):
    return np.ascontiguousarray(a.reshape(-1, P, a.shape[1]).transpose(1, 0, 2))


def kernel(**inputs):
    import concourse.bacc as _bacc
    from concourse.bass_utils import run_bass_kernel_spmd as _run

    a = {k: np.asarray(v) for k, v in inputs.items()}
    w_qkv = a["L1_attn_w_qkv"].reshape(H1, 3, HD1, D)
    w_qk = w_qkv[:, :2].transpose(3, 0, 1, 2).reshape(D, -1)
    w_v = w_qkv[:, 2].reshape(C1, D).T
    bqkv = a["L0_attn_bqkv"]
    gu = np.stack([a["L0_ffn_w_gate"], a["L0_ffn_w_up"]], 1)
    gu = gu.reshape(E, 2, FE, DC, P).transpose(0, 4, 3, 1, 2).reshape(E, P, -1)
    ins = {
        "x": a["L0_attn_x"].reshape(T // P, P, D).transpose(1, 0, 2),
        "consts": shape_constants(),
        "ids": np.arange(T, dtype=np.int32).reshape(T // P, P).T,
        "w0": _chunks(a["L0_attn_Wqkv"]),
        "b0qk": bqkv[:2 * D].reshape(4, P).T,
        "b0v": bqkv[2 * D:],
        "w0out": _chunks(a["L0_attn_Wout"]),
        "b0out": a["L0_attn_bout"],
        "slopes0": a["L0_attn_slopes"],
        "gatew": _chunks(a["L0_ffn_gate_w"].T),
        "moe_in": gu,
        "moe_down": a["L0_ffn_w_down"].transpose(0, 2, 1),
        "slopes1": a["L1_attn_slope_rate"].reshape(H1),
        "w1qk": _chunks(w_qk).reshape(P, DC, H1, 2, HD1),
        "w1v": _chunks(w_v),
        "w1g": _chunks(a["L1_attn_w_gate"].T).reshape(P, DC, H1, HD1),
        "w1o": _chunks(a["L1_attn_w_out"].T),
        "norm1": a["L1_attn_norm_w"].reshape(H1, P).T,
        "wf_gate": _chunks(a["L1_ffn_w_gate"].T),
        "wf_up": _chunks(a["L1_ffn_w_up"].T),
        "wf_down": _chunks(a["L1_ffn_w_down"].T),
    }
    nc = _bacc.Bacc("TRN2", target_bir_lowering=False, num_devices=1)
    arrays, args = {}, []
    for name, v in ins.items():
        v = np.ascontiguousarray(v)
        arrays[f"in_{name}"] = v
        args.append(nc.dram_tensor(f"in_{name}", v.shape, mybir.dt.from_np(v.dtype), kind="ExternalInput").ap())
    args.append(nc.dram_tensor("out_0", (T, D), F32, kind="ExternalOutput").ap())
    args.append(nc.dram_tensor("xhat_rows", (T, D), F32, kind="Internal").ap())
    args.append(nc.dram_tensor("slot_ids", (E * CAP, 1), I32, kind="Internal").ap())
    args.append(nc.dram_tensor("y_rows", (E * CAP, D), F32, kind="Internal").ap())
    build(nc, *args)
    r = _run(nc, [arrays], core_ids=[0])
    return r.results[0]["out_0"].reshape(NB, SEQ, D)
```

```python
from contextlib import ExitStack

import numpy as np

import concourse.bass as bass
from concourse import mybir

F32 = mybir.dt.float32
F32R = mybir.dt.float32r
BF16 = mybir.dt.bfloat16
I32 = mybir.dt.int32
U32 = mybir.dt.uint32
ALU = mybir.AluOpType
ACT = mybir.ActivationFunctionType
AX = mybir.AxisListType.X

P = 128
NB, SEQ, D = 8, 256, 256
T = NB * SEQ
TB = SEQ // P
DC = D // P
H0, HD0 = 16, 16
G0 = 4
NG = H0 // G0
E, TOPK, FE = 64, 8, 96
CAP = 2 * T * TOPK // E
CT = CAP // P
H1, HD1 = 16, 128
C1 = H1 * HD1
FH = 1024
HJ = FH // P
EPS_LN, EPS_RMS = 1e-5, 1e-6
LOWEST = -3.0e38
VG = C1 // 512
RING = 4
STAGE_WORDS = 16900
LAYER1_WORDS = 11400
LAYER1_R_WORDS = 4 * DC * 512 + 4 * DC * SEQ
EXPERT_WORDS = 2 * (DC * 2 * FE + D) + (E + 2) * CT + 4 * CT * D + 2 * CAP
EXPERT_R_WORDS = 4 * (DC * 2 * FE + D) + 4 * DC * CAP + 4 * CAP
W1_WORDS = DC * C1 * 4 + H1 * D + 3 * HJ * D
W1_PIECES = E // 2
DROPPED = 65536.0

CONSTS = {}
_at = 0
for _name, _n in (("dist", SEQ), ("causal", SEQ), ("before", P), ("ones", P),
                  ("parity", 2), ("slot0", E)):
    CONSTS[_name] = (_at, _at + _n)
    _at += _n
NCONST = _at


def shape_constants():
    p = np.arange(P)[:, None]
    i = np.arange(SEQ)[None, :]
    c = np.zeros((P, NCONST), np.float32)

    def put(name, a):
        c[:, CONSTS[name][0]:CONSTS[name][1]] = a


    put("dist", np.maximum(i - p, 0))
    put("causal", i >= p)
    put("before", p < np.arange(P)[None, :])
    put("ones", 1.0)
    put("parity", np.concatenate([(p // HD0) % 2 == 0, (p // HD0) % 2 == 1], 1))
    put("slot0", np.arange(E)[None, :] * CAP + 1.0)

    return c


class Steps:

    def __init__(self, eng, sem, per, turn):
        self.eng, self.sem, self.per, self.base, self.n = eng, sem, per, turn * per, 0

    def done(self, ins):
        ins.then_inc(self.sem, 1)
        self.n += 1

    def settled(self, alone=None):
        self.eng.wait_ge(self.sem, self.base + self.n)
        if alone is not None:
            self.eng.sem_inc(alone, 1)

    def end(self):
        assert self.n == self.per, (self.n, self.per)


def build(nc, x, consts, ids, w0, b0qk, b0v, w0out, b0out, slopes0, gatew, moe_in, moe_down,
          slopes1, w1, norm1, identity, out,
          xhat_rows, slot_ids, y_rows):
    with ExitStack() as ctx:
        def sb(name, shape, dt=F32):
            return ctx.enter_context(nc.sbuf_tensor(name, shape, dt))

        def sem(name):
            return ctx.enter_context(nc.semaphore(name))

        bank = [ctx.enter_context(nc.psum_tensor(f"bank{i}", [P, 512], F32)) for i in range(8)]

        X = sb("X", [P, T // P, D])
        ident = sb("ident", [P, P])
        one = sb("one", [P, 1])
        tokens = sb("tokens", [P, T // P], I32)
        slope = sb("slope", [P, H0 + H1])
        nslope = sb("nslope", [P, H0 + H1])
        D1 = sb("D1", [P, H1, SEQ])
        W1 = sb("W1", [P, W1_WORDS])
        nrm = sb("nrm", [P, H1])
        SLOT = sb("SLOT", [P, NB, TB * TOPK], I32)
        WGT = sb("WGT", [P, NB, TB * TOPK])
        ones_b = sb("ones_b", [P, P], BF16)
        before_b = sb("before_b", [P, P], BF16)
        sel_b = sb("sel_b", [P, TB, E], BF16)
        seen_b = sb("seen_b", [P, TB, E], BF16)
        bn = sb("bn", [P, TB, 6])
        bn2 = sb("bn2", [P, TB, 6])
        mv = sb("mv", [P, TB, 2])
        mv2 = sb("mv2", [P, TB, 2])
        var = sb("var", [P, TB])
        var2 = sb("var2", [P, TB])
        rstd = sb("rstd", [P, TB])
        rstd2 = sb("rstd2", [P, TB])

        half = sb("half", [P, TB])


        def region(tensor):
            at = [0]

            def take(shape, dt=F32):
                n = int(np.prod(shape))
                v = tensor[:, at[0]:at[0] + n]
                at[0] += n
                assert at[0] <= tensor.shape[1], at[0]
                if dt != tensor.dtype:
                    v = v.bitcast(dt)
                if len(shape) > 1:
                    names = "abcd"[:len(shape)]
                    v = v.rearrange(f"p ({' '.join(names)}) -> p {' '.join(names)}",
                                    **{n: s for n, s in zip(names, shape)})
                return v
            return take

        def stage(*tensors):
            with ExitStack() as own:
                takes = [region(own.enter_context(nc.sbuf_tensor(name, [P, words], dt)))
                         for name, words, dt in tensors]
            return takes if len(takes) > 1 else takes[0]

        take = region(W1)
        W1v = take([VG, DC * 512])
        W1h = take([H1, DC * 3 * HD1])
        W1o = take([H1, D])
        WF = take([HJ, DC * 2 * P])
        WFd = take([HJ, D])

        take = region(W1)
        vz = take([TB, H0, P])
        qz = take([H0, SEQ])
        take = stage(("layer0", STAGE_WORDS, F32))
        cst = take([NCONST])

        def const(name):
            a, b = CONSTS[name]
            return cst[:, a:b]

        dist, causal, parity, slot0, ones = (const(n) for n in ("dist", "causal", "parity", "slot0", "ones"))
        D0 = take([H0, SEQ])
        W0 = take([DC, 3 * D])
        W0o = take([DC, D])
        GW = take([DC, E])
        bqk = take([4])
        bqp = take([4])
        bv = take([D])
        bo = take([D])
        xhA = take([TB, D])
        xTA = take([DC, SEQ])
        kT = take([DC, SEQ])
        PA = [take([3, 512]) for _ in range(2)]
        oTA = take([DC, SEQ])
        x1 = take([TB, D])
        xh2 = take([TB, D])
        x2T = take([DC, SEQ])
        logit = take([TB, E])
        left = take([TB, E])
        sel = take([TB, E])
        prob = take([TB, E])
        keep = take([TB, E])
        key = take([TB, E])
        top = take([TB, 8])
        ntop = take([TB])
        psumx = take([TB])
        rsum = take([TB])
        slotf = take([TB, TOPK])
        eq = take([TB, TOPK, E])
        wsum = take([TB * TOPK])
        scat = take([TB * TOPK], I32)
        tok = take([TB], I32)
        no_id = take([CAP * E // P // 2])

        take, take_r = stage(("experts", EXPERT_WORDS, F32), ("experts_r", EXPERT_R_WORDS, F32R))
        WE = DC * 2 * FE
        Wraw = [take([WE + D]) for _ in range(2)]
        Whi, Wlo = ([take_r([WE + D], F32R) for _ in range(2)] for _ in range(2))
        all_ids = take([E, CT], I32)
        idx = [take([CT], I32) for _ in range(2)]
        xg = [take([CT, D]) for _ in range(2)]
        xhi, xlo = ([take_r([DC, CAP], F32R) for _ in range(2)] for _ in range(2))
        hB = [take([CAP]) for _ in range(2)]
        hhi, hlo = ([take_r([CAP], F32R) for _ in range(2)] for _ in range(2))
        yo = [take([CT, D]) for _ in range(2)]

        take, take_r = stage(("layer1", LAYER1_WORDS, F32), ("layer1_r", LAYER1_R_WORDS, F32R))
        rows = take([TB * RING, D])
        sidx = take([TB * TOPK], I32)
        comb = take([TB, D])
        xh3 = take([TB, D])
        Whi1, Wlo1 = ([take_r([DC * 512], F32R) for _ in range(2)] for _ in range(2))
        x3hi, x3lo, x4hi, x4lo = (take_r([DC, SEQ], F32R) for _ in range(4))
        qkD = [take([2, SEQ]) for _ in range(2)]
        vD = take([TB, C1])
        wcur = take([TB * TOPK])
        PD = [take([3, P]) for _ in range(2)]
        sgF = [p.rearrange("p a b -> p (a b)")[:, 0:SEQ] for p in PD]
        gD = [take([SEQ]) for _ in range(2)]
        goD = [take([SEQ]) for _ in range(2)]
        sq = [take([SEQ]) for _ in range(2)]
        ssq = take([SEQ])
        x3 = take([TB, D])
        xh4 = xh3

        hF = rows.rearrange("p a b -> p (a b)")[:, 0:HJ * SEQ].rearrange("p (a b) -> p a b", a=HJ)


        NAMES = """
        x_first x_loaded ident_loaded consts_loaded small_loaded w0_loaded w0o_loaded norm_loaded table_filled no_id_ready xg_cleared nslope_ready decay0_exp
        decay1_exp decay0_ready decay1_ready setup_dve bf_ready cleared cleared_v half_ready
        a_xhat a_xT_ps a_xT a_q_ps a_k_ps a_v_ps a_q a_k a_v a_sc_ps a_prob a_pv_ps a_oT
        a_out_ps a_x1 a_xh2 a_x2T_ps a_x2T a_log_ps a_logit a_ln_steps a_var a_rstd a_ln2_steps a_var2 a_rstd2
        a_sel_steps a_ntop a_exp a_selb a_rank_ps a_pos_steps a_slot_steps a_scat a_tok a_ids a_stored a_x1sum
        b_first_ids b_all_ids b_idx b_x_ps b_xhi b_xlo b_whi b_wlo b_dhi b_dlo
        b_gu_ps b_silu b_h b_hhi b_hlo b_y_ps b_ya b_yb
        l1_loaded w1o_scaled dve_carrier pool_carrier
        d_sidx d_wcur d_comb_steps d_ln3_steps d_var3 d_rstd3 d_xh3 d_x3T_ps d_x3T d_x3lo d_x4lo d_whi d_wlo d_v_ps d_v
        d_qk_ps d_qk d_g_ps d_g d_s_ps d_p d_o_ps d_go d_sq d_ssq d_y_ps d_ssq_ps d_var d_rms d_x3
        d_ln4_steps d_var4 d_rstd4 d_xh4 d_x4T_ps d_x4T d_h_ps d_sg d_h d_dn_ps d_out d_stored
        """.split()
        S = {n: sem(n) for n in NAMES}
        b_wgu = [sem(f"b_wgu{i}") for i in range(2)]
        b_wdn = [sem(f"b_wdn{i}") for i in range(2)]

        b_rows = [sem(f"b_rows{i}") for i in range(2)]
        b_stored = [sem(f"b_stored{i}") for i in range(2)]
        d_row = [sem(f"d_row{i}") for i in range(TB * TOPK)]

        def row_at(t, k):
            return t * RING + k % RING

        V_USE, F_USE, H_USE, USES = 0, VG, VG + HJ, VG + HJ + H1

        def use_number(turn, i):
            if isinstance(turn, int) and turn == 0:
                return i if i < F_USE else i - HJ
            n = turn * USES + (i - HJ)
            return n - VG if isinstance(turn, int) and turn == NB else n

        def uses(front, back):
            return [i for i in range(USES) if (back if F_USE <= i < H_USE else front)]

        def two_ahead(turn, i, front, back):
            now = uses(front, back)
            last = isinstance(turn, int) and turn >= LASTB
            line = now + ([] if not front else uses(False, True)[:2] if last else uses(True, True)[:2])
            k = now.index(i) + 2
            if k >= len(line):
                return None
            return (turn if k < len(now) else turn + 1), line[k]

        def raw_weights(i):
            return W1v[:, i, :] if i < F_USE else W1h[:, i - H_USE, :] if i >= H_USE else WF[:, i - F_USE, :]

        def after(eng, name, value):
            if not isinstance(value, int) or value > 0:
                eng.wait_ge(S[name], value)

        NSMALL = 6

        B2 = 2
        FIRST_IDS = 4
        LASTB = NB - 1

        block = ctx.enter_context(nc.Block())

        @block.sync
        def _(sp):
            sp.dma_start(X[:, 0:TB, :], x[:, 0:TB, :]).then_inc(S["x_first"], 16)
            sp.dma_start(ident[:], identity).then_inc(S["ident_loaded"], 16)
            sp.dma_start(cst, consts).then_inc(S["consts_loaded"], 16)
            sp.dma_start(W0, w0).then_inc(S["w0_loaded"], 16)
            sp.dma_start(W0o, w0out).then_inc(S["w0o_loaded"], 16)
            sp.dma_start(GW, gatew).then_inc(S["w0o_loaded"], 16)
            sp.dma_start(nrm[:], norm1).then_inc(S["norm_loaded"], 16)
            sp.wait_ge(S["small_loaded"], 16 * NSMALL)
            sp.dma_start(X[:, TB:, :], x[:, TB:, :]).then_inc(S["x_loaded"], 16)
            sp.wait_ge(S["no_id_ready"], 1)
            n = no_id.shape[1]
            tab = slot_ids.rearrange("(a p n) o -> a p (n o)", a=E * CAP // (P * n), p=P)
            for a in range(tab.shape[0]):
                sp.dma_start(tab[a], no_id.bitcast(I32)).then_inc(S["table_filled"], 16)

            def store_xhat(b):
                sp.wait_ge(S["a_xh2"], b + 1)
                sp.dma_start(xhat_rows[bass.ds(b * SEQ, SEQ), :].rearrange("(t p) d -> p t d", p=P),
                             xh2).then_inc(S["a_stored"], 16)

            with sp.Fori(0, NB) as b:
                store_xhat(b)

            sp.wait_ge(S["a_scat"], NB)
            sp.wait_ge(S["decay1_ready"], 1)
            sp.wait_ge(S["a_stored"], 16 * NB)

            def load_ids(first, last, loaded):
                sp.dma_start(all_ids[:, first:last, :], slot_ids[first * CAP:last * CAP, :].rearrange(
                    "(e p c) o -> p e (c o)", p=P, c=CT)).then_inc(S[loaded], 16)

            def load_expert(e, s):
                after(sp, "b_wlo", e - 1)
                after(sp, "b_dlo", e - 1)
                sp.dma_start(Wraw[s][:, 0:WE], moe_in[bass.ds(e, 1)].rearrange("a p n -> (a p) n")
                             ).then_inc(b_wgu[s], 16)
                sp.dma_start(Wraw[s][0:FE, WE:], moe_down[bass.ds(e, 1)].rearrange("a f d -> (a f) d")
                             ).then_inc(b_wdn[s], 16)

            def store_expert(e, s):
                sp.wait_ge(S["b_ya"], e + 1)
                sp.wait_ge(S["b_yb"], e + 1)
                sp.dma_start(y_rows[bass.ds(e * CAP, CAP), :].rearrange("(p c) d -> p c d", c=CT),
                             yo[s]).then_inc(b_stored[s], 16)

            def expert_step(e, s, more_weights=True):
                if more_weights:
                    load_expert(e + 2, s)
                store_expert(e - 1, 1 - s)

            for s in range(2):
                load_expert(s, s)
            sp.wait_ge(S["a_ids"], 16 * NB * TB * TOPK)
            load_ids(0, FIRST_IDS, "b_first_ids")
            load_ids(FIRST_IDS, E, "b_all_ids")
            load_expert(2, 0)

            def load_layer1(i):
                n = W1_WORDS // W1_PIECES
                sp.dma_start(W1[:, bass.ds(i * n, n)], w1[:, bass.ds(i * n, n)]).then_inc(S["l1_loaded"], 16)

            with sp.Fori(0, E // B2 - 2) as i:
                expert_step(i * 2 + 1, 1)
                load_layer1(i)
                expert_step(i * 2 + 2, 0)
            expert_step(E - 3, 1)
            load_layer1(E // B2 - 2)
            expert_step(E - 2, 0, more_weights=False)
            load_layer1(E // B2 - 1)
            expert_step(E - 1, 1, more_weights=False)
            store_expert(E - 1, 1)

            for s in range(2):
                sp.wait_ge(b_stored[s], 16 * E // 2)

            with sp.Fori(0, NB) as b:
                sp.wait_ge(S["d_out"], b + 1)
                sp.dma_start(out[bass.ds(b * SEQ, SEQ), :].rearrange("(t p) d -> p t d", p=P),
                             x3).then_inc(S["d_stored"], 16)
            sp.wait_ge(S["d_stored"], 16 * NB)

        def a_scatter(pool, b):
            after(pool, "a_ids", b * (16 * TB * TOPK))
            pool.wait_ge(S["a_scat"], b + 1)
            pool.tensor_copy(tok, tokens[:, bass.ds(b * TB, TB)]).then_inc(S["a_tok"], 1)
            pool.wait_ge(S["a_tok"], b + 1)
            pool.sem_inc(S["pool_carrier"], 1)
            for c in range(TB * TOPK):
                pool.indirect_dma_start(
                    slot_ids, bass.IndirectOffsetOnAxis(ap=scat[:, c:c + 1].bitcast(U32), axis=0),
                    tok[:, c // TOPK:c // TOPK + 1], None, bounds_check=E * CAP - 1, oob_is_err=False,
                ).then_inc(S["a_ids"], 16)

        def rsqrt(pool, ready, done, v, r, n):
            pool.wait_ge(S[ready], n)
            pool.tensor_tensor(r, v, half[:, 0:TB], ALU.pow).then_inc(S[done], 1)

        @block.gpsimd
        def _(pool):
            pool.memset(one[:], 1.0)
            pool.memset(half[:], -0.5).then_inc(S["half_ready"], 1)
            pool.memset(no_id, 1.0).then_inc(S["no_id_ready"], 1)
            pool.wait_ge(S["half_ready"], 1)
            rsqrt(pool, "a_var", "a_rstd", var[:], rstd[:], 1)
            pool.memset(qz, 0.0).then_inc(S["cleared"], 1)

            def turn(b, ahead, back, scatter):
                if back:
                    rsqrt(pool, "a_var2", "a_rstd2", var2[:], rstd2[:], b)
                if scatter:
                    a_scatter(pool, b - 2)
                if ahead:
                    rsqrt(pool, "a_var", "a_rstd", var[:], rstd[:], b + 3)

            rsqrt(pool, "a_var", "a_rstd", var[:], rstd[:], 2)
            turn(0, True, False, False)
            turn(1, True, True, False)
            pool.wait_ge(S["small_loaded"], 16 * NSMALL)
            pool.wait_ge(S["table_filled"], 16 * (E * CAP // (P * no_id.shape[1])))
            turn(2, True, True, True)
            with pool.Fori(3, LASTB - 1) as b:
                turn(b, True, True, True)
            turn(LASTB - 1, False, True, True)
            turn(LASTB, False, True, True)
            rsqrt(pool, "a_var2", "a_rstd2", var2[:], rstd2[:], NB)
            a_scatter(pool, LASTB - 1)
            a_scatter(pool, LASTB)

            pool.wait_ge(S["a_stored"], 16 * NB)
            pool.wait_ge(S["a_slot_steps"], NB * SLOT_STEPS)

            def gather(e, s):
                if not isinstance(e, int) or e >= B2:
                    pool.wait_ge(S["b_x_ps"], e - 1)
                    pool.wait_ge(b_rows[s], (e - s) * 32)
                    pool.sem_inc(S["pool_carrier"], 1)
                pool.tensor_copy(idx[s], all_ids[:, bass.ds(e, 1), :].rearrange("p a b -> p (a b)")
                                 ).then_inc(S["b_idx"], 1)
                pool.wait_ge(S["b_idx"], e + 1)
                pool.sem_inc(S["pool_carrier"], 1)
                for c in range(CT):
                    pool.indirect_dma_start(
                        xg[s][:, c, :], None, xhat_rows,
                        bass.IndirectOffsetOnAxis(ap=idx[s][:, c:c + 1].bitcast(U32), axis=0),
                        bounds_check=T - 1, oob_is_err=False).then_inc(b_rows[s], 16)

            pool.wait_ge(S["b_first_ids"], 16)
            pool.wait_ge(S["xg_cleared"], 1)
            for e in range(FIRST_IDS):
                gather(e, e % 2)
            pool.wait_ge(S["b_all_ids"], 16)
            with pool.Fori(FIRST_IDS // B2, E // B2) as i:
                for s in range(B2):
                    gather(i * B2 + s, s)

            for s in range(2):
                pool.wait_ge(b_stored[s], 16 * E // 2)
            pool.wait_ge(S["b_ya"], E)

            def slots_of(b):
                pool.tensor_copy(sidx, SLOT[:, b, :] if isinstance(b, int) else
                                 SLOT[:, bass.ds(b, 1), :].rearrange("p a n -> p (a n)")
                                 ).then_inc(S["d_sidx"], 1)
                pool.wait_ge(S["d_sidx"], b + 1)
                pool.sem_inc(S["pool_carrier"], 1)

            def gather_rows(b, k):
                if k >= RING:
                    pool.wait_ge(S["d_comb_steps"], b * COMB_STEPS + TB * (k - RING + 1))
                    pool.sem_inc(S["pool_carrier"], 1)
                for t in range(TB):
                    gather_row(t * TOPK + k, row_at(t, k))

            def gather_row(c, at):
                pool.indirect_dma_start(
                    rows[:, at, :], None, y_rows,
                    bass.IndirectOffsetOnAxis(ap=sidx[:, c:c + 1].bitcast(U32), axis=0),
                    bounds_check=E * CAP - 1, oob_is_err=False).then_inc(d_row[c], 16)

            slots_of(0)
            for k in range(TOPK):
                gather_rows(0, k)
            rsqrt(pool, "d_var3", "d_rstd3", var[:], rstd[:], 1)

            def dturn(b, ahead, back):
                if back:
                    rsqrt(pool, "d_var", "d_rms", var2[:], rstd2[:], b)
                    rsqrt(pool, "d_var4", "d_rstd4", var2[:], rstd2[:], b)
                if ahead:
                    pool.wait_ge(S["d_comb_steps"], (b + 1) * COMB_STEPS)
                    slots_of(b + 1)
                for h in range(H1):
                    if ahead and h < TOPK:
                        if h == 0 and back:
                            pool.wait_ge(S["d_dn_ps"], b)
                            pool.sem_inc(S["pool_carrier"], 1)
                        gather_rows(b + 1, h)
                    if ahead and h == 11:
                        rsqrt(pool, "d_var3", "d_rstd3", var[:], rstd[:], b + 2)
                    if h > 0:
                        pool.wait_ge(S["d_sq"], b * H1 + h + 1)
                        if h > 1:
                            pool.wait_ge(S["d_ssq"], b * (H1 - 1) + h - 1)
                        pool.tensor_tensor(ssq, ssq, sq[h % 2], ALU.add).then_inc(S["d_ssq"], 1)

            dturn(0, True, False)
            with pool.Fori(1, LASTB) as b:
                dturn(b, True, True)
            dturn(LASTB, False, True)
            rsqrt(pool, "d_var", "d_rms", var2[:], rstd2[:], NB)
            rsqrt(pool, "d_var4", "d_rstd4", var2[:], rstd2[:], NB)

        @block.tensor
        def _(pe):
            def transpose4(dst, src):
                for c in range(DC):
                    for t in range(TB):
                        ins = pe.transpose(dst[:, c * SEQ + t * P:c * SEQ + (t + 1) * P],
                                           src[:, t, c * P:(c + 1) * P], ident[:])
                return ins

            def a_trans(b):
                pe.wait_ge(S["a_xhat"], b + 1)
                after(pe, "a_pos_steps", (b - 2) * POS_STEPS)
                transpose4(bank[0], xhA).then_inc(S["a_xT_ps"], 1)

            def a_query(b):
                pe.wait_ge(S["a_xT"], b + 1)
                if isinstance(b, int) and b == 0:
                    pe.wait_ge(S["w0_loaded"], 16)
                after(pe, "a_x1", b - 1)
                a_feature_major(0, 2).then_inc(S["a_q_ps"], 1)

            def a_key(b):
                after(pe, "a_logit", b - 1)
                a_feature_major(1, 3).then_inc(S["a_k_ps"], 1)

            def a_feature_major(which, bk):
                for m in range(DC):
                    for c in range(DC):
                        ins = pe.matmul(bank[bk][:, m * SEQ:(m + 1) * SEQ],
                                        W0[:, c, which * D + m * P:which * D + (m + 1) * P], xTA[:, c, :],
                                        start=(c == 0), stop=(c == DC - 1))
                return ins

            def a_value(b):
                after(pe, "a_v", 2 * b)
                for t in range(TB):
                    for c in range(DC):
                        ins = pe.matmul(bank[1][:, t * D:(t + 1) * D], xTA[:, c, t * P:(t + 1) * P],
                                        W0[:, c, 2 * D:3 * D], start=(c == 0), stop=(c == DC - 1))
                ins.then_inc(S["a_v_ps"], 1)

            def a_out(b):
                pe.wait_ge(S["a_oT"], b + 1)
                after(pe, "a_q", NG * (b + 2 if not isinstance(b, int) or b < LASTB else NB))
                if isinstance(b, int) and b == 0:
                    pe.wait_ge(S["w0o_loaded"], 32)
                for t in range(TB):
                    for c in range(DC):
                        ins = pe.matmul(bank[2][:, t * D:(t + 1) * D], oTA[:, c, t * P:(t + 1) * P],
                                        W0o[:, c, :], start=(c == 0), stop=(c == DC - 1))
                ins.then_inc(S["a_out_ps"], 1)

            def a_scores(b, g):
                pe.wait_ge(S["a_q"], b * NG + g + 1)
                if g == 0:
                    pe.wait_ge(S["a_k"], b + 1)
                m = g * G0 * HD0 // P
                heads = slice(g * G0, (g + 1) * G0)
                for n in range(3):
                    after(pe, "a_prob", b * (3 * NG) + 3 * g + n - 2)
                    if n < 2:
                        ins = pe.matmul(bank[4 + n][:, :], kT[:, m, 0:P],
                                        qz[:, g * G0 + 2 * n:g * G0 + 2 * n + 2, :], start=True, stop=True)
                    else:
                        ins = pe.matmul(bank[4 + n][:, :], kT[:, m, P:SEQ], qz[:, heads, P:SEQ],
                                        start=True, stop=True)
                    ins.then_inc(S["a_sc_ps"], 1)

            def a_attend(b, g):
                if g == 0:
                    after(pe, "a_oT", b)
                if g % 2 == 0:
                    pe.wait_ge(S["a_v"], 2 * b + g // 2 + 1)
                pe.wait_ge(S["a_prob"], b * (3 * NG) + 3 * g + 3)
                Pg = PA[g % 2]
                m = g // 2
                for hh in range(G0):
                    h = g * G0 + hh
                    col = (hh % 2) * SEQ
                    last = g % 2 == 1 and hh == G0 - 1
                    pe.matmul(bank[7][:, m * SEQ:(m + 1) * SEQ], vz[:, 0, h, :], Pg[:, hh // 2, col:col + SEQ],
                              start=(g % 2 == 0 and hh == 0), stop=last, skip_group_check=True)
                    ins = pe.matmul(bank[7][:, m * SEQ + P:(m + 1) * SEQ], vz[:, 1, h, :],
                                    Pg[:, 2, hh * P:(hh + 1) * P], start=False, stop=last,
                                    skip_group_check=True)
                ins.then_inc(S["a_pv_ps"], 1)

            def a_back2(b):
                pe.wait_ge(S["a_xh2"], b + 1)
                after(pe, "a_xT", b + 3 if not isinstance(b, int) or b < LASTB - 1 else NB)
                transpose4(bank[0], xh2).then_inc(S["a_x2T_ps"], 1)

            def a_logits(b):
                pe.wait_ge(S["a_x2T"], b + 1)
                after(pe, "a_k", b + 2 if not isinstance(b, int) or b < LASTB else NB)
                for t in range(TB):
                    for c in range(DC):
                        ins = pe.matmul(bank[3][:, t * E:(t + 1) * E], x2T[:, c, t * P:(t + 1) * P],
                                        GW[:, c, :], start=(c == 0), stop=(c == DC - 1))
                ins.then_inc(S["a_log_ps"], 1)

            def a_rank(b):
                pe.wait_ge(S["a_selb"], 2 * b + 2)
                for t in range(TB):
                    o = bank[0][:, t * E:(t + 1) * E]
                    pe.matmul(o, before_b[:], sel_b[:, t, :], start=True, stop=False)
                    ins = pe.matmul(o, ones_b[:], seen_b[:, t, :], start=False, stop=True)
                ins.then_inc(S["a_rank_ps"], 1)

            def turn(b, front, ahead, back):
                if front:
                    a_scores(b, 0)
                if back:
                    a_out(b - 1)
                if front:
                    a_scores(b, 1)
                    a_attend(b, 0)
                if ahead:
                    a_trans(b + 1)
                if front:
                    a_scores(b, 2)
                if back:
                    a_back2(b - 1)
                if front:
                    a_attend(b, 1)
                    a_scores(b, 3)
                if ahead:
                    a_query(b + 1)
                if back:
                    a_logits(b - 1)
                if front:
                    a_attend(b, 2)
                if ahead:
                    a_key(b + 1)
                    a_value(b + 1)
                if back:
                    a_rank(b - 1)
                if front:
                    a_attend(b, 3)

            pe.wait_ge(S["ident_loaded"], 16)
            a_trans(0)
            a_query(0)
            a_key(0)
            a_value(0)
            pe.wait_ge(S["bf_ready"], 2)
            pe.wait_ge(S["cleared"], 1)
            pe.wait_ge(S["cleared_v"], 1)
            turn(0, True, True, False)
            turn(1, True, True, True)
            with pe.Fori(2, LASTB) as b:
                turn(b, True, True, True)
            turn(LASTB, True, False, True)
            turn(NB, False, False, True)
            pe.wait_ge(S["a_pos_steps"], NB * POS_STEPS)

            def b_trans(e, s):
                pe.wait_ge(b_rows[s], (e - s) * 32 + 64)
                after(pe, "b_xlo", 2 * e)
                for c in range(DC):
                    for t in range(CT):
                        ins = pe.transpose(bank[c][:, t * P:(t + 1) * P], xg[s][:, t, c * P:(c + 1) * P], ident[:])
                ins.then_inc(S["b_x_ps"], 1)

            def b_hidden(e, s):
                pe.wait_ge(S["b_wlo"], e + 1)
                pe.wait_ge(S["b_xlo"], 2 * e + 2)
                after(pe, "b_h", e - 1)
                for w in range(2):
                    n = 0
                    for c in range(DC):
                        at = (c * 2 + w) * FE
                        for W, x_ in ((Whi, xhi), (Whi, xlo), (Wlo, xhi)):
                            ins = pe.matmul(bank[2 + 2 * s + w][0:FE, :], W[s][:, at:at + FE], x_[s][:, c, :],
                                            start=(n == 0), stop=(n == 3 * DC - 1))
                            n += 1
                    ins.then_inc(S["b_gu_ps"], 1)

            def b_out(e, s):
                pe.wait_ge(S["b_hlo"], e + 1)
                pe.wait_ge(S["b_dlo"], e + 1)
                for n in range(2):
                    after(pe, "b_ya" if n == 0 else "b_yb", e)
                    for t in range(2):
                        q = 2 * n + t
                        for k, (h, W) in enumerate(((hhi, Whi), (hhi, Wlo), (hlo, Whi))):
                            ins = pe.matmul(bank[6 + n][:, t * D:(t + 1) * D], h[s][0:FE, q * P:(q + 1) * P],
                                            W[s][0:FE, WE:], start=(k == 0), stop=(k == 2))
                    ins.then_inc(S["b_y_ps"], 1)

            def b_pair(i):
                for s in (1, 0):
                    e = i * 2 + (1 if s else 2)
                    b_trans(e + 1, 1 - s)
                    b_hidden(e, s)
                    b_out(e - 1, 1 - s)

            b_trans(0, 0)
            b_trans(1, 1)
            b_hidden(0, 0)

            b_pair(0)
            with pe.Fori(1, E // B2 - 1) as i:
                b_pair(i)
            b_hidden(E - 1, 1)
            b_out(E - 2, 0)
            b_out(E - 1, 1)
            pe.wait_ge(S["b_ya"], E)
            pe.wait_ge(S["b_yb"], E)

            pe.wait_ge(S["w1o_scaled"], 1)
            pe.wait_ge(S["l1_loaded"], 16 * W1_PIECES)

            def d_trans3(b):
                pe.wait_ge(S["d_xh3"], b + 1)
                after(pe, "d_x4lo", b - 1)
                after(pe, "d_out", b - 1)
                transpose4(bank[0], xh3).then_inc(S["d_x3T_ps"], 1)

            def d_values(b, tiles):
                for n in tiles:
                    t, g = n % 2, n // 2
                    if n == 0:
                        pe.wait_ge(S["d_x3lo"], b + 1)
                        after(pe, "d_qk", b * H1 - 1)
                    elif n == 1:
                        after(pe, "d_qk", b * H1)
                    elif n == 2:
                        after(pe, "d_p", b * H1)
                    elif n == 4:
                        after(pe, "d_go", b * H1)
                        after(pe, "d_sq", b * H1)
                    elif n >= 6:
                        pe.wait_ge(S["d_v"], b * 8 + n - 5)
                    s = g % 2
                    pe.wait_ge(S["d_whi"], use_number(b, V_USE + g) + 1)
                    for k, (x_, W, c) in enumerate((x_, W, c) for x_, W in (
                            (x3hi, Whi1), (x3lo, Whi1), (x3hi, Wlo1)) for c in range(DC)):
                        if k == 2 * DC:
                            pe.wait_ge(S["d_wlo"], use_number(b, V_USE + g) + 1)
                        ins = pe.matmul(bank[1 + n % 6][:, :], x_[:, c, t * P:(t + 1) * P],
                                        W[s][:, c * 512:(c + 1) * 512], start=(k == 0), stop=(k == 3 * DC - 1))
                    ins.then_inc(S["d_v_ps"], 1)

            def three_passes(outs, use, s, step, hi, lo):
                pe.wait_ge(S["d_whi"], use + 1)
                for n, (out, at) in enumerate(outs):
                    for c in range(DC):
                        for x_ in (hi, lo):
                            pe.matmul(out, Whi1[s][:, c * step + at:c * step + at + P], x_[:, c, :],
                                      start=(n == 0 and c == 0 and x_ is hi), stop=False, skip_group_check=True)
                pe.wait_ge(S["d_wlo"], use + 1)
                for out, at in outs:
                    for c in range(DC):
                        ins = pe.matmul(out, Wlo1[s][:, c * step + at:c * step + at + P], hi[:, c, :],
                                        start=False, stop=(c == DC - 1), skip_group_check=True)
                return ins

            def d_project(b, h):
                after(pe, "d_qk", b * H1 + h - 1)
                if h == 0:
                    pe.wait_ge(S["d_v"], b * 8 + 8)
                use = use_number(b, H_USE + h)
                three_passes([(bank[1 + h % 2][:, w * SEQ:(w + 1) * SEQ], w * P) for w in range(2)],
                             use, h % 2, 3 * P, x3hi, x3lo).then_inc(S["d_qk_ps"], 1)
                after(pe, "d_sq", b * H1 + h - 1)
                after(pe, "d_go", b * H1 + h - 1)
                three_passes([(bank[5 + h % 2][:, 0:SEQ], 2 * P)], use, h % 2, 3 * P, x3hi, x3lo
                             ).then_inc(S["d_g_ps"], 1)

            def d_scores(b, h):
                pe.wait_ge(S["d_qk"], b * H1 + h + 1)
                after(pe, "d_p", b * H1 + h - 1)
                qk = qkD[h % 2]
                pe.matmul(bank[3 + h % 2][:, 0:SEQ], qk[:, 1, 0:P], qk[:, 0, :], start=True, stop=True)
                pe.matmul(bank[3 + h % 2][:, SEQ:SEQ + P], qk[:, 1, P:SEQ], qk[:, 0, P:SEQ],
                          start=True, stop=True).then_inc(S["d_s_ps"], 1)

            def d_attend(b, h):
                pe.wait_ge(S["d_p"], b * H1 + h + 1)
                pe.wait_ge(S["d_g"], b * H1 + h + 1)
                Ph = PD[h % 2]
                o = bank[5 + h % 2]
                vh = slice(h * HD1, (h + 1) * HD1)
                pe.matmul(o[:, SEQ:2 * SEQ], vD[:, 0, vh], Ph[:, 0:2, :], start=True, stop=False)
                pe.matmul(o[:, SEQ + P:2 * SEQ], vD[:, 1, vh], Ph[:, 2, :], start=False,
                          stop=True).then_inc(S["d_o_ps"], 1)

            def d_project_out(b, h):
                pe.wait_ge(S["d_go"], b * H1 + h + 1)
                if h == 0:
                    after(pe, "d_x3", b)
                for t in range(TB):
                    ins = pe.matmul(bank[7][:, t * D:(t + 1) * D], goD[h % 2][:, t * P:(t + 1) * P],
                                    W1o[:, h, :], start=(h == 0 and t == 0), stop=(h == H1 - 1),
                                    skip_group_check=True)
                ins.then_inc(S["d_y_ps"], 1)

            def d_square_sums(b):
                pe.wait_ge(S["d_ssq"], (b + 1) * (H1 - 1))
                after(pe, "d_x3lo", b + 2 if not isinstance(b, int) or b < LASTB else NB)
                for t in range(TB):
                    ins = pe.matmul(bank[0][:, t:t + 1], ssq[:, t * P:(t + 1) * P], one[:],
                                    start=True, stop=True)
                ins.then_inc(S["d_ssq_ps"], 1)

            def d_trans4(b):
                pe.wait_ge(S["d_xh4"], b + 1)
                pe.wait_ge(S["d_var"], b + 1)
                transpose4(bank[0], xh4).then_inc(S["d_x4T_ps"], 1)

            def d_ffn(b):
                pe.wait_ge(S["d_x4lo"], b + 1)
                for j in range(HJ):
                    if j == 0:
                        after(pe, "d_v", b * 8 + 16 if not isinstance(b, int) or b < LASTB else NB * 8)
                    if j >= 4:
                        pe.wait_ge(S["d_h"], b * HJ + j - 3)
                    three_passes([(bank[1 + j % 4][:, w * SEQ:(w + 1) * SEQ], w * P) for w in range(2)],
                                 use_number(b + 1, F_USE + j), j % 2, 2 * P, x4hi, x4lo
                                 ).then_inc(S["d_h_ps"], 1)

            def d_down(b):
                for t in range(TB):
                    for j in range(HJ):
                        if t == 0:
                            pe.wait_ge(S["d_h"], b * HJ + j + 1)
                        ins = pe.matmul(bank[0][:, t * D:(t + 1) * D], hF[:, j, t * P:(t + 1) * P],
                                        WFd[:, j, :], start=(j == 0), stop=(j == HJ - 1))
                ins.then_inc(S["d_dn_ps"], 1)

            def dturn(b, front, back):
                if back:
                    d_project_out(b - 1, H1 - 1)
                    d_square_sums(b - 1)
                if front:
                    d_values(b, range(2, 6))
                if back:
                    d_trans4(b - 1)
                if front:
                    d_values(b, range(6, 8))
                if back:
                    d_ffn(b - 1)
                if front:
                    if back:
                        pe.wait_ge(S["d_h"], (b - 1) * HJ + 5)
                    d_project(b, 0)
                if back:
                    d_down(b - 1)
                if front:
                    for h in range(H1):
                        d_scores(b, h)
                        if h + 1 < H1:
                            d_project(b, h + 1)
                        if h + 1 == H1 - 1 and not (isinstance(b, int) and b == LASTB):
                            d_trans3(b + 1)
                        v_ahead = h == H1 - 1 and not (isinstance(b, int) and b == LASTB)
                        if v_ahead:
                            d_values(b + 1, range(1))
                        d_attend(b, h)
                        if h:
                            d_project_out(b, h - 1)
                        if v_ahead:
                            d_values(b + 1, range(1, 2))

            d_trans3(0)
            d_values(0, range(2))
            dturn(0, True, False)
            dturn(1, True, True)
            with pe.Fori(2, LASTB) as b:
                dturn(b, True, True)
            dturn(LASTB, True, True)
            dturn(NB, False, True)

        @block.scalar
        def _(act):
            act.dma_start(slope[:, 0:H0], slopes0.partition_broadcast(P)).then_inc(S["small_loaded"], 16)
            act.dma_start(slope[:, H0:], slopes1.partition_broadcast(P)).then_inc(S["small_loaded"], 16)
            act.dma_start(bqk, b0qk).then_inc(S["small_loaded"], 16)
            act.dma_start(bv, b0v.partition_broadcast(P)).then_inc(S["small_loaded"], 16)
            act.dma_start(bo, b0out.partition_broadcast(P)).then_inc(S["small_loaded"], 16)
            act.dma_start(tokens[:], ids).then_inc(S["small_loaded"], 16)
            act.wait_ge(S["consts_loaded"], 16)
            act.wait_ge(S["nslope_ready"], 1)

            def decay(l, dst, done, heads):
                for h in heads:
                    n = l * H0 + h
                    ins = nc.scalar.activation(dst[:, h, :], dist, ACT.Exp, scale=nslope[:, n:n + 1])
                    if h % 4 == 3:
                        ins.then_inc(S[done], 1)

            decay(0, D0, "decay0_exp", range(H0 // 2))

            def copy(dst, src, ready, n, done):
                act.wait_ge(S[ready], n)
                nc.scalar.activation(dst, src, ACT.Copy).then_inc(S[done], 1)

            def split(a, n=DC):
                return a.rearrange("p (a b) -> p a b", a=n)

            def a_xT(b):
                after(act, "a_v_ps", b)
                copy(xTA, split(bank[0][:, :]), "a_xT_ps", b + 1, "a_xT")

            def a_qz(b):
                act.wait_ge(S["a_q_ps"], b + 1)
                for h in range(H0):
                    if h % G0 == 0:
                        after(act, "a_sc_ps", (b - 1) * (3 * NG) + 3 * (h // G0) + 3)
                    m, g, odd = h * HD0 // P, (h * HD0 % P) // 32, h % 2
                    r = slice(32 * g, 32 * g + 32)
                    ins = nc.scalar.activation(
                        qz[r, h, :], bank[2][r, m * SEQ:(m + 1) * SEQ], ACT.Identity,
                        scale=parity[r, odd:odd + 1], bias=bqp[r, 2 * odd + m:2 * odd + m + 1])
                    if h % G0 == G0 - 1:
                        ins.then_inc(S["a_q"], 1)

            def a_keys(b):
                act.wait_ge(S["a_k_ps"], b + 1)
                after(act, "a_sc_ps", b * (3 * NG))
                for m in range(DC):
                    ins = nc.scalar.activation(kT[:, m, :], bank[3][:, m * SEQ:(m + 1) * SEQ], ACT.Identity,
                                               bias=bqk[:, 2 + m:3 + m])
                ins.then_inc(S["a_k"], 1)

            def a_oT(b):
                after(act, "a_out_ps", b)
                copy(oTA, split(bank[7][:, :]), "a_pv_ps", (b + 1) * NG, "a_oT")

            def a_back2(b):
                after(act, "a_log_ps", b)
                copy(x2T, split(bank[0][:, :]), "a_x2T_ps", b + 1, "a_x2T")

            def a_exp(b):
                act.wait_ge(S["a_ntop"], b + 1)
                after(act, "a_slot_steps", b * SLOT_STEPS)
                for t in range(TB):
                    ins = nc.scalar.activation(prob[:, t, :], logit[:, t, :], ACT.Exp, bias=ntop[:, t:t + 1],
                                               accum_out=psumx[:, t:t + 1])
                ins.then_inc(S["a_exp"], 1)

            def turn(b, front, ahead, back):
                if ahead:
                    a_xT(b + 1)
                if back:
                    a_back2(b - 1)
                if ahead:
                    a_qz(b + 1)
                if back:
                    a_exp(b - 1)
                if ahead:
                    a_keys(b + 1)
                if front:
                    a_oT(b)

            a_xT(0)
            decay(0, D0, "decay0_exp", range(H0 // 2, H0))
            act.wait_ge(S["setup_dve"], 1)
            act.wait_ge(S["cleared"], 1)
            a_qz(0)
            a_keys(0)
            turn(0, True, True, False)
            turn(1, True, True, True)
            with act.Fori(2, LASTB) as b:
                turn(b, True, True, True)
            turn(LASTB, True, False, True)
            turn(NB, False, False, True)
            decay(1, D1, "decay1_exp", range(H1))
            act.wait_ge(S["a_slot_steps"], NB * SLOT_STEPS)
            act.wait_ge(S["a_stored"], 16 * NB)
            act.wait_ge(S["a_ids"], 16 * NB * TB * TOPK)

            def b_copy(e, s):
                after(act, "b_gu_ps", 2 * e - 2)
                act.wait_ge(S["b_x_ps"], e + 1)
                for c in range(DC):
                    nc.scalar.activation(xhi[s][:, c, :], bank[c][:, :], ACT.Copy).then_inc(S["b_xhi"], 1)

            def b_gate_up(e, s):
                act.wait_ge(b_wgu[s], (e - s) * 8 + 16)
                after(act, "b_gu_ps", 2 * e - 2)
                nc.scalar.activation(Whi[s][:, 0:WE], Wraw[s][:, 0:WE], ACT.Copy).then_inc(S["b_whi"], 1)

            def b_down(e, s):
                act.wait_ge(b_wdn[s], (e - s) * 8 + 16)
                after(act, "b_y_ps", 2 * e - 2)
                nc.scalar.activation(Whi[s][0:FE, WE:], Wraw[s][0:FE, WE:], ACT.Copy).then_inc(S["b_dhi"], 1)

            def b_silu(e, s):
                after(act, "b_hlo", e - 1)
                act.wait_ge(S["b_gu_ps"], 2 * e + 1)
                nc.scalar.activation(hB[s][0:FE, :], bank[2 + 2 * s][0:FE, :], ACT.Silu).then_inc(S["b_silu"], 1)

            def b_hidden(e, s):
                after(act, "b_y_ps", 2 * e - 2)
                copy(hhi[s][0:FE, :], hB[s][0:FE, :], "b_h", e + 1, "b_hhi")

            def b_result(e, s):
                if not isinstance(e, int) or e >= 2:
                    act.wait_ge(b_stored[s], (e - s) * 8)
                copy(yo[s][:, 0:2, :], split(bank[6][:, :]), "b_y_ps", 2 * e + 1, "b_ya")

            def b_pair(i):
                for s in (1, 0):
                    e = i * 2 + (1 if s else 2)
                    b_copy(e + 1, 1 - s)
                    b_gate_up(e + 1, 1 - s)
                    b_silu(e, s)
                    b_hidden(e, s)
                    b_result(e - 1, 1 - s)
                    b_down(e + 1, 1 - s)

            for e in range(2):
                b_gate_up(e, e)
                b_down(e, e)
            for e in range(2):
                b_copy(e, e)
            b_silu(0, 0)
            b_hidden(0, 0)

            b_pair(0)
            with act.Fori(1, E // B2 - 1) as i:
                b_pair(i)
            b_silu(E - 1, 1)
            b_hidden(E - 1, 1)
            b_result(E - 2, 0)
            b_result(E - 1, 1)
            for s in range(2):
                act.wait_ge(b_stored[s], 16 * E // 2)
            act.wait_ge(S["b_yb"], E)

            def split_weights(turn, i):
                W = raw_weights(i)
                nc.scalar.activation(Whi1[i % 2][:, 0:W.shape[1]], W, ACT.Copy).then_inc(S["d_whi"], 1)

            def refill(turn, i, front, back):
                if two_ahead(turn, i, front, back):
                    split_weights(*two_ahead(turn, i, front, back))

            def d_high3(b):
                after(act, "d_g_ps", b * H1)
                copy(x3hi, split(bank[0][:, :]), "d_x3T_ps", b + 1, "d_x3T")

            def d_front(b, back, tiles):
                for n in tiles:
                    t, g = n % 2, n // 2
                    if back and n == 6:
                        d_high4(b - 1)
                    act.wait_ge(S["d_v_ps"], b * 8 + n + 1)
                    nc.scalar.activation(vD[:, t, g * 512:(g + 1) * 512], bank[1 + n % 6][:, :],
                                         ACT.Silu).then_inc(S["d_v"], 1)
                    if t == TB - 1:
                        refill(b, V_USE + g, True, back)

            def d_high4(b):
                after(act, "d_h_ps", b * HJ)
                copy(x4hi, split(bank[0][:, :]), "d_x4T_ps", b + 1, "d_x4T")

            def d_back(b, front):
                if not front:
                    d_high4(b)
                for j in range(HJ):
                    act.wait_ge(S["d_h_ps"], b * HJ + j + 1)
                    refill(b + 1, F_USE + j, front, True)
                    if j > 1:
                        act.wait_ge(S["d_h"], b * HJ + j - 1)
                    nc.scalar.activation(sgF[j % 2], bank[1 + j % 4][:, 0:SEQ], ACT.Silu).then_inc(S["d_sg"], 1)

            def d_silu(b, h, back):
                after(act, "d_s_ps", b * H1 + h - 1)
                act.wait_ge(S["d_qk_ps"], b * H1 + h + 1)
                nc.scalar.activation(qkD[h % 2][:, :, :], bank[1 + h % 2][:, :].rearrange("p (a b) -> p a b", a=2),
                                     ACT.Silu).then_inc(S["d_qk"], 1)
                act.wait_ge(S["d_g_ps"], b * H1 + h + 1)
                after(act, "d_go", b * H1 + h - 1)
                nc.scalar.activation(gD[h % 2], bank[5 + h % 2][:, 0:SEQ], ACT.Tanh, scale=0.5).then_inc(S["d_g"], 1)
                refill(b, H_USE + h, True, back)

            def d_square(b, h):
                if h == 0:
                    after(act, "d_ssq_ps", b)
                elif h > 1:
                    after(act, "d_ssq", b * (H1 - 1) + h - 2)
                elif h == 1:
                    after(act, "d_ssq", b * (H1 - 1))
                act.wait_ge(S["d_o_ps"], b * H1 + h + 1)
                nc.scalar.activation(ssq if h == 0 else sq[h % 2], bank[5 + h % 2][:, SEQ:2 * SEQ],
                                     ACT.Square).then_inc(S["d_sq"], 1)

            def dturn(b, front, back):
                if front:
                    d_front(b, back, range(1, 8))
                if back:
                    d_back(b - 1, front)
                if front:
                    d_silu(b, 0, back)
                    for h in range(H1):
                        if h + 1 < H1:
                            d_silu(b, h + 1, back)
                        if h + 1 == H1 - 1 and not (isinstance(b, int) and b == LASTB):
                            d_high3(b + 1)
                        if h == H1 - 1 and not (isinstance(b, int) and b == LASTB):
                            d_front(b + 1, True, range(1))
                        d_square(b, h)

            act.wait_ge(S["l1_loaded"], 16 * W1_PIECES)
            for i in range(2):
                split_weights(0, V_USE + i)
            d_high3(0)
            d_front(0, False, range(1))
            dturn(0, True, False)
            dturn(1, True, True)
            with act.Fori(2, LASTB) as b:
                dturn(b, True, True)
            dturn(LASTB, True, True)
            dturn(NB, False, True)

        @block.vector
        def _(dve):
            nc.vector.memset(vz, 0.0).then_inc(S["cleared_v"], 1)
            nc.vector.memset(seen_b[:], 0.0)

            def decay(dst, ready, done):
                for g in range(4):
                    hs = slice(4 * g, 4 * g + 4)
                    dve.wait_ge(S[ready], g + 1)
                    ins = nc.vector.tensor_tensor(dst[:, hs, :], dst[:, hs, :],
                                                  causal.unsqueeze(1).broadcast_to([P, 4, SEQ]), ALU.mult)
                ins.then_inc(S[done], 1)

            def variances(src, bn_, mv_, var_, steps_sem, per, turn, var_done):
                st = Steps(dve, S[steps_sem], per, turn)
                for t in range(TB):
                    st.done(nc.vector.bn_stats(bn_[:, t, :], src(t)))
                st.settled(S["dve_carrier"])
                for t in range(TB):
                    st.done(nc.vector.bn_aggr(mv_[:, t, :], bn_[:, t, :]))
                st.settled()
                st.end()
                nc.vector.tensor_scalar(var_[:], mv_[:, :, 1], EPS_LN, None, ALU.add).then_inc(S[var_done], 1)

            def scale_rows(src, dst, mv_, rstd_, turn, rstd_done, free, done):
                for name, n in free:
                    after(dve, name, n)
                dve.wait_ge(S[rstd_done], turn + 1)
                for t in range(TB):
                    ins = nc.vector.tensor_scalar(dst[:, t, :], src(t), mv_[:, t, 0:1], rstd_[:, t:t + 1],
                                                  ALU.subtract, ALU.mult)
                ins.then_inc(S[done], 1)

            def normalize(src, dst, bn_, mv_, var_, rstd_, steps_sem, per, turn, var_done, rstd_done, free, done):
                variances(src, bn_, mv_, var_, steps_sem, per, turn, var_done)
                scale_rows(src, dst, mv_, rstd_, turn, rstd_done, free, done)

            def xtile(b, t):
                return X[:, b * TB + t, :] if isinstance(b, int) else \
                    X[:, bass.ds(b * TB + t, 1), :].rearrange("p a d -> p (a d)")

            def a_stats(b):
                variances(lambda t: xtile(b, t), bn, mv, var, "a_ln_steps", 4, b, "a_var")

            def a_norm(b):
                scale_rows(lambda t: xtile(b, t), xhA, mv, rstd, b, "a_rstd", (("a_xT_ps", b),), "a_xhat")

            def a_vals(b, m):
                dve.wait_ge(S["a_v_ps"], b + 1)
                after(dve, "a_pv_ps", (b - 1) * NG + 2 * m + 2)
                n = H0 // 2
                for t in range(TB):
                    dst = vz[:, t, m * n:(m + 1) * n, :].rearrange("p a b -> p (a b)")
                    dst = bass.AP(dst.tensor, dst.offset, [dst.ap[0], [P + HD0, n], [1, HD0]])
                    ins = nc.vector.tensor_tensor(
                        dst, bank[1][:, t * D + m * P:t * D + (m + 1) * P].rearrange("p (a b) -> p a b", a=n),
                        bv[:, m * P:(m + 1) * P].rearrange("p (a b) -> p a b", a=n), ALU.add)
                ins.then_inc(S["a_v"], 1)

            def a_mask(b, g):
                after(dve, "a_pv_ps", b * NG + g - 1)
                for n in range(3):
                    dve.wait_ge(S["a_sc_ps"], b * (3 * NG) + 3 * g + n + 1)
                    if n < 2:
                        h = g * G0 + 2 * n
                        o, s, d = PA[g % 2][:, n, :].rearrange("p (a b) -> p a b", a=2), \
                            bank[4 + n][:, :].rearrange("p (a b) -> p a b", a=2), D0[:, h:h + 2, :]
                    else:
                        o, s, d = PA[g % 2][:, n, :].rearrange("p (a b) -> p a b", a=G0), \
                            bank[4 + n][:, :].rearrange("p (a b) -> p a b", a=G0), D0[:, g * G0:g * G0 + G0, 0:P]
                    nc.vector.tensor_tensor(o, s, d, ALU.mult).then_inc(S["a_prob"], 1)

            def a_residual(b):
                dve.wait_ge(S["a_out_ps"], b + 1)
                nc.vector.tensor_tensor(x1, bank[2][:, :].rearrange("p (a b) -> p a b", a=TB),
                                        bo.unsqueeze(1).broadcast_to([P, TB, D]), ALU.add).then_inc(S["a_x1"], 1)
                dve.wait_ge(S["a_x1"], b + 1)
                for t in range(TB):
                    nc.vector.tensor_tensor(x1[:, t, :], x1[:, t, :], xtile(b, t), ALU.add).then_inc(S["a_x1sum"], 1)
                dve.wait_ge(S["a_x1sum"], 2 * b + 2)
                variances(lambda t: x1[:, t, :], bn2, mv2, var2, "a_ln2_steps", 4, b, "a_var2")
                for t in range(TB):
                    nc.vector.tensor_scalar(xtile(b, t), x1[:, t, :], 1.0, None, ALU.mult)
                scale_rows(lambda t: x1[:, t, :], xh2, mv2, rstd2, b, "a_rstd2",
                           (("a_x2T_ps", b), ("a_stored", 16 * b)), "a_xh2")

            def a_select(b):
                st = Steps(dve, S["a_sel_steps"], SEL_STEPS, b)
                dve.wait_ge(S["a_log_ps"], b + 1)
                nc.vector.tensor_copy(logit, bank[3][:, 0:TB * E].rearrange("p (a b) -> p a b", a=TB)
                                      ).then_inc(S["a_logit"], 1)
                dve.wait_ge(S["a_logit"], b + 1)
                dve.sem_inc(S["dve_carrier"], 1)
                for t in range(TB):
                    st.done(nc.vector.max(top[:, t, :], logit[:, t, :]))
                st.settled()
                nc.vector.tensor_scalar(ntop, top[:, :, 0], -1.0, None, ALU.mult).then_inc(S["a_ntop"], 1)
                for t in range(TB):
                    st.done(nc.vector.match_replace(left[:, t, :], top[:, t, :], logit[:, t, :], LOWEST))
                st.settled()
                st.done(nc.vector.tensor_scalar(sel, left, LOWEST, None, ALU.is_le))
                st.settled()
                st.end()
                after(dve, "a_rank_ps", b)
                nc.vector.tensor_copy(sel_b[:], sel).then_inc(S["a_selb"], 1)
                nc.vector.tensor_tensor(seen_b[:, 1, :], seen_b[:, 0, :], sel[:, 0, :],
                                        ALU.add).then_inc(S["a_selb"], 1)

            def a_places(b):
                st = Steps(dve, S["a_pos_steps"], POS_STEPS, b)
                dve.wait_ge(S["a_rank_ps"], b + 1)
                pos = bank[0][:, 0:TB * E].rearrange("p (a b) -> p a b", a=TB)
                st.done(nc.vector.tensor_tensor(seen_b[:, 0, :], seen_b[:, 1, :], sel[:, 1, :], ALU.add))
                st.done(nc.vector.tensor_scalar(keep, pos, float(CAP), None, ALU.is_lt))
                st.done(nc.vector.scalar_tensor_tensor(
                    out=key, in0=pos, scalar=float(CAP - 1),
                    in1=slot0.unsqueeze(1).broadcast_to([P, TB, E]), op0=ALU.min, op1=ALU.add))
                st.settled()
                st.done(nc.vector.tensor_tensor(key, key, sel, ALU.mult))
                st.done(nc.vector.tensor_tensor(keep, keep, sel, ALU.mult))
                st.end()

            def a_slots1(b):
                st = Steps(dve, S["a_slot_steps"], SLOT_STEPS, b)
                dve.wait_ge(S["a_exp"], b + 1)
                st.done(nc.vector.reciprocal(rsum, psumx))
                dve.wait_ge(S["a_pos_steps"], (b + 1) * POS_STEPS)
                st.settled(S["dve_carrier"])
                for t in range(TB):
                    st.done(nc.vector.max(slotf[:, t, :], key[:, t, :]))
                    st.done(nc.vector.scalar_tensor_tensor(out=prob[:, t, :], in0=prob[:, t, :],
                                                           scalar=rsum[:, t:t + 1], in1=keep[:, t, :],
                                                           op0=ALU.mult, op1=ALU.mult))
                st.settled()
                st.done(nc.vector.tensor_tensor(eq, key.unsqueeze(2).broadcast_to([P, TB, TOPK, E]),
                                                slotf.unsqueeze(3).broadcast_to([P, TB, TOPK, E]), ALU.is_equal))
                assert st.n == SLOT1_STEPS

            def a_slots2(b):
                st = Steps(dve, S["a_slot_steps"], SLOT_STEPS, b)
                st.n = SLOT1_STEPS
                st.settled()
                st.done(nc.vector.tensor_tensor(eq, eq, prob.unsqueeze(2).broadcast_to([P, TB, TOPK, E]), ALU.mult))
                st.settled()
                st.done(nc.vector.tensor_reduce(wsum, eq.rearrange("p a b c -> p (a b) c"), AX, ALU.add))
                st.settled()
                flat = slotf.rearrange("p a b -> p (a b)")

                def of_batch(tensor):
                    return tensor[:, b, :] if isinstance(b, int) else \
                        tensor[:, bass.ds(b, 1), :].rearrange("p a n -> p (a n)")

                st.done(nc.vector.tensor_scalar(of_batch(WGT), wsum, 1.0, None, ALU.mult))
                st.done(nc.vector.tensor_scalar(of_batch(SLOT), flat, -1.0, None, ALU.add))
                st.done(nc.vector.tensor_scalar(wsum, wsum, 0.0, DROPPED, ALU.is_le, ALU.mult))
                st.settled()
                st.done(nc.vector.scalar_tensor_tensor(out=wsum, in0=flat, scalar=-1.0, in1=wsum,
                                                       op0=ALU.add, op1=ALU.add))
                st.end()

            def a_slots3(b):
                dve.wait_ge(S["a_slot_steps"], (b + 1) * SLOT_STEPS)
                after(dve, "a_ids", b * (16 * TB * TOPK))
                nc.vector.tensor_copy(scat, wsum).then_inc(S["a_scat"], 1)

            def turn(b, stats, front, ahead, back, back2):
                if front:
                    a_vals(b, 1)
                    a_mask(b, 0)
                if back2:
                    a_slots2(b - 2)
                if ahead:
                    a_norm(b + 1)
                if front:
                    a_mask(b, 1)
                if back2:
                    a_slots3(b - 2)
                if back:
                    a_residual(b - 1)
                if front:
                    a_mask(b, 2)
                    a_mask(b, 3)
                if back:
                    a_select(b - 1)
                if ahead:
                    a_vals(b + 1, 0)
                if stats:
                    a_stats(b + 2)
                if back:
                    a_places(b - 1)
                    a_slots1(b - 1)
                    if not ahead:
                        a_slots2(b - 1)
                        if not front:
                            a_slots3(b - 1)

            dve.wait_ge(S["x_first"], 16)
            a_stats(0)
            a_norm(0)
            dve.wait_ge(S["small_loaded"], 16 * NSMALL)
            nc.vector.tensor_scalar(nslope[:], slope[:], -1.0, None, ALU.mult).then_inc(S["nslope_ready"], 1)
            dve.wait_ge(S["consts_loaded"], 16)
            for odd in range(2):
                ins = nc.vector.tensor_scalar(bqp[:, 2 * odd:2 * odd + 2], bqk[:, 0:2], parity[:, odd:odd + 1],
                                              None, ALU.mult)
            ins.then_inc(S["setup_dve"], 1)
            nc.vector.tensor_copy(ones_b[:], ones).then_inc(S["bf_ready"], 1)
            nc.vector.tensor_copy(before_b[:], const("before")).then_inc(S["bf_ready"], 1)
            decay(D0, "decay0_exp", "decay0_ready")
            dve.wait_ge(S["cleared_v"], 1)
            a_vals(0, 0)
            dve.wait_ge(S["x_loaded"], 16)
            a_stats(1)
            dve.wait_ge(S["decay0_ready"], 1)
            turn(0, True, True, True, False, False)
            turn(1, True, True, True, True, False)
            turn(2, True, True, True, True, True)
            with dve.Fori(3, LASTB - 1) as b:
                turn(b, True, True, True, True, True)
            turn(LASTB - 1, False, True, True, True, True)
            turn(LASTB, False, True, False, True, True)
            a_slots3(LASTB - 1)
            turn(NB, False, False, False, True, False)
            decay(D1, "decay1_exp", "decay1_ready")
            dve.wait_ge(S["a_ids"], 16 * NB * TB * TOPK)
            dve.wait_ge(S["a_stored"], 16 * NB)

            def b_copy(e, s):
                after(dve, "b_gu_ps", 2 * e - 2)
                for c in range(DC):
                    dve.wait_ge(S["b_xhi"], 2 * e + c + 1)
                    nc.vector.tensor_tensor(xlo[s][:, c, :], bank[c][:, :], xhi[s][:, c, :].bitcast(F32),
                                            ALU.subtract).then_inc(S["b_xlo"], 1)

            def b_gate_up(e, s):
                dve.wait_ge(S["b_whi"], e + 1)
                after(dve, "b_gu_ps", 2 * e - 2)
                nc.vector.tensor_tensor(Wlo[s][:, 0:WE], Wraw[s][:, 0:WE], Whi[s][:, 0:WE].bitcast(F32),
                                        ALU.subtract).then_inc(S["b_wlo"], 1)

            def b_down(e, s):
                dve.wait_ge(S["b_dhi"], e + 1)
                after(dve, "b_y_ps", 2 * e - 2)
                nc.vector.tensor_tensor(Wlo[s][0:FE, WE:], Wraw[s][0:FE, WE:], Whi[s][0:FE, WE:].bitcast(F32),
                                        ALU.subtract).then_inc(S["b_dlo"], 1)

            def b_mul(e, s):
                dve.wait_ge(S["b_silu"], e + 1)
                dve.wait_ge(S["b_gu_ps"], 2 * e + 2)
                nc.vector.tensor_tensor(hB[s][0:FE, :], hB[s][0:FE, :], bank[3 + 2 * s][0:FE, :],
                                        ALU.mult).then_inc(S["b_h"], 1)

            def b_rest(e, s):
                dve.wait_ge(S["b_hhi"], e + 1)
                after(dve, "b_y_ps", 2 * e - 2)
                nc.vector.tensor_tensor(hlo[s][0:FE, :], hB[s][0:FE, :], hhi[s][0:FE, :].bitcast(F32),
                                        ALU.subtract).then_inc(S["b_hlo"], 1)

            def b_result(e, s):
                if not isinstance(e, int) or e >= 2:
                    dve.wait_ge(b_stored[s], (e - s) * 8)
                dve.wait_ge(S["b_y_ps"], 2 * e + 2)
                nc.vector.tensor_copy(yo[s][:, 2:4, :], bank[7][:, :].rearrange("p (a b) -> p a b", a=2)
                                      ).then_inc(S["b_yb"], 1)

            def b_pair(i):
                for s in (1, 0):
                    e = i * 2 + (1 if s else 2)
                    b_copy(e + 1, 1 - s)
                    b_gate_up(e + 1, 1 - s)
                    b_mul(e, s)
                    b_rest(e, s)
                    b_result(e - 1, 1 - s)
                    b_down(e + 1, 1 - s)

            for s in range(2):
                ins = nc.vector.memset(xg[s], 0.0)
            ins.then_inc(S["xg_cleared"], 1)
            for e in range(2):
                b_gate_up(e, e)
                b_down(e, e)
            for e in range(2):
                b_copy(e, e)
            b_mul(0, 0)
            b_rest(0, 0)

            b_pair(0)
            with dve.Fori(1, E // B2 - 1) as i:
                b_pair(i)
            b_mul(E - 1, 1)
            b_rest(E - 1, 1)
            b_result(E - 2, 0)
            b_result(E - 1, 1)
            for s in range(2):
                dve.wait_ge(b_stored[s], 16 * E // 2)
            dve.wait_ge(S["b_ya"], E)

            def low_part(dst, src, hi):
                return nc.vector.tensor_tensor(dst, src, hi.bitcast(F32), ALU.subtract)

            def split_weights(turn, i):
                W = raw_weights(i)
                dve.wait_ge(S["d_whi"], use_number(turn, i) + 1)
                low_part(Wlo1[i % 2][:, 0:W.shape[1]], W, Whi1[i % 2][:, 0:W.shape[1]]).then_inc(S["d_wlo"], 1)

            def refill(turn, i, front, back):
                if two_ahead(turn, i, front, back):
                    split_weights(*two_ahead(turn, i, front, back))

            def d_low3(b):
                after(dve, "d_g_ps", b * H1)
                dve.wait_ge(S["d_x3T"], b + 1)
                low_part(x3lo, bank[0][:, :].rearrange("p (a b) -> p a b", a=DC), x3hi).then_inc(S["d_x3lo"], 1)

            def d_low4(b):
                after(dve, "d_h_ps", b * HJ)
                dve.wait_ge(S["d_x4T"], b + 1)
                low_part(x4lo, bank[0][:, :].rearrange("p (a b) -> p a b", a=DC), x4hi).then_inc(S["d_x4lo"], 1)

            dve.wait_ge(S["l1_loaded"], 16 * W1_PIECES)
            for i in range(2):
                split_weights(0, V_USE + i)
            dve.wait_ge(S["norm_loaded"], 16)
            for h in range(H1):
                ins = nc.vector.tensor_scalar(W1o[:, h, :], W1o[:, h, :], nrm[:, h:h + 1], 0.5, ALU.mult, ALU.mult)
            ins.then_inc(S["w1o_scaled"], 1)

            def d_combine(b, k):
                for t in range(TB):
                    c = t * TOPK + k
                    dve.wait_ge(d_row[c], b * 16 + 16)
                if k:
                    dve.wait_ge(S["d_comb_steps"], b * COMB_STEPS + TB * k)
                for t in range(TB):
                    c = t * TOPK + k
                    nc.vector.scalar_tensor_tensor(
                        out=comb[:, t, :], in0=rows[:, row_at(t, k), :], scalar=wcur[:, c:c + 1],
                        in1=xtile(b, t) if k == 0 else comb[:, t, :],
                        op0=ALU.mult, op1=ALU.add).then_inc(S["d_comb_steps"], 1)

            def d_weights(b):
                after(dve, "d_comb_steps", b * COMB_STEPS)
                nc.vector.tensor_scalar(wcur[:], WGT[:, b, :] if isinstance(b, int) else
                                        WGT[:, bass.ds(b, 1), :].rearrange("p a n -> p (a n)"),
                                        1.0, None, ALU.mult).then_inc(S["d_wcur"], 1)
                dve.wait_ge(S["d_wcur"], b + 1)

            def d_norm3(b):
                dve.wait_ge(S["d_comb_steps"], (b + 1) * COMB_STEPS)
                for t in range(TB):
                    nc.vector.tensor_scalar(xtile(b, t), comb[:, t, :], 1.0, None, ALU.mult)
                normalize(lambda t: comb[:, t, :], xh3, bn, mv, var, rstd, "d_ln3_steps", 4, b, "d_var3",
                          "d_rstd3", (("d_x4T_ps", b - 1), ("d_x3T_ps", b)), "d_xh3")

            def d_mask(b, h):
                dve.wait_ge(S["d_s_ps"], b * H1 + h + 1)
                after(dve, "d_o_ps", b * H1 + h - 1)
                s = bank[3 + h % 2]
                nc.vector.tensor_tensor(PD[h % 2][:, 0:2, :].rearrange("p a b -> p (a b)"), s[:, 0:SEQ],
                                        D1[:, h, :], ALU.mult)
                nc.vector.tensor_tensor(PD[h % 2][:, 2, :], s[:, SEQ:SEQ + P], D1[:, h, 0:P],
                                        ALU.mult).then_inc(S["d_p"], 1)

            def d_gate(b, h):
                dve.wait_ge(S["d_sq"], b * H1 + h + 1)
                after(dve, "d_y_ps", b * H1 + h - 1)
                nc.vector.scalar_tensor_tensor(out=goD[h % 2], in0=gD[h % 2], scalar=1.0,
                                               in1=bank[5 + h % 2][:, SEQ:2 * SEQ], op0=ALU.add,
                                               op1=ALU.mult).then_inc(S["d_go"], 1)

            def d_mean_square(b):
                dve.wait_ge(S["d_ssq_ps"], b + 1)
                nc.vector.tensor_scalar(var2[:], bank[0][:, 0:TB], 1.0 / C1, EPS_RMS, ALU.mult,
                                        ALU.add).then_inc(S["d_var"], 1)

            def d_residual(b):
                dve.wait_ge(S["d_rms"], b + 1)
                after(dve, "d_stored", b * 16)
                for t in range(TB):
                    ins = nc.vector.scalar_tensor_tensor(out=x3[:, t, :], in0=bank[7][:, t * D:(t + 1) * D],
                                                         scalar=rstd2[:, t:t + 1], in1=xtile(b, t),
                                                         op0=ALU.mult, op1=ALU.add)
                ins.then_inc(S["d_x3"], 1)
                dve.wait_ge(S["d_x3"], b + 1)
                normalize(lambda t: x3[:, t, :], xh4, bn2, mv2, var2, rstd2, "d_ln4_steps", 4, b, "d_var4",
                          "d_rstd4", (("d_x3T_ps", b + 2 if not isinstance(b, int) or b < LASTB else NB),), "d_xh4")

            def d_ffn(b, front):
                for j in range(HJ):
                    refill(b + 1, F_USE + j, front, True)
                    dve.wait_ge(S["d_sg"], b * HJ + j + 1)
                    if j == 0:
                        after(dve, "d_dn_ps", b)
                    nc.vector.tensor_tensor(hF[:, j, :], sgF[j % 2], bank[1 + j % 4][:, SEQ:2 * SEQ],
                                            ALU.mult).then_inc(S["d_h"], 1)
                dve.wait_ge(S["d_dn_ps"], b + 1)
                nc.vector.tensor_tensor(x3, bank[0][:, :].rearrange("p (a b) -> p a b", a=TB), x3,
                                        ALU.add).then_inc(S["d_out"], 1)

            def dturn(b, ahead, front, back):
                if back:
                    d_mean_square(b - 1)
                if front:
                    refill(b, V_USE, True, back)
                if back:
                    d_residual(b - 1)
                if front:
                    for g in range(1, VG - 1):
                        refill(b, V_USE + g, True, back)
                if back:
                    d_low4(b - 1)
                if front:
                    refill(b, V_USE + VG - 1, True, back)
                if back:
                    d_ffn(b - 1, front)
                if front:
                    for h in range(H1):
                        d_mask(b, h)
                        refill(b, H_USE + h, True, back)
                        if ahead and h == 1:
                            d_weights(b + 1)
                        if ahead and 2 <= h < 2 + TOPK:
                            d_combine(b + 1, h - 2)
                        if ahead and h == 11:
                            d_norm3(b + 1)
                        if ahead and h == H1 - 2:
                            d_low3(b + 1)
                        d_gate(b, h)

            d_weights(0)
            for k in range(TOPK):
                d_combine(0, k)
            d_norm3(0)
            d_low3(0)
            dturn(0, True, True, False)
            dturn(1, True, True, True)
            with dve.Fori(2, LASTB) as b:
                dturn(b, True, True, True)
            dturn(LASTB, False, True, True)
            dturn(NB, False, False, True)


SLOT1_STEPS, SLOT_STEPS = 6, 12
POS_STEPS = 5
SEL_STEPS = 5
COMB_STEPS = TB * TOPK


def _chunks(a):
    return np.ascontiguousarray(a.reshape(-1, P, a.shape[1]).transpose(1, 0, 2))


def kernel(**inputs):
    import concourse.bacc as _bacc
    from concourse.bass_utils import run_bass_kernel_spmd as _run

    a = {k: np.asarray(v) for k, v in inputs.items()}
    w_qkv = a["L1_attn_w_qkv"].reshape(H1, 3, HD1, D)
    w_v = w_qkv[:, 2].reshape(VG, 512, DC, P).transpose(3, 0, 2, 1)
    w_head = np.concatenate([w_qkv[:, :2], a["L1_attn_w_gate"].reshape(H1, 1, HD1, D)], 1)
    w_head = w_head.reshape(H1, 3, HD1, DC, P).transpose(4, 0, 3, 1, 2)
    w_ffn = np.stack([a["L1_ffn_w_gate"], a["L1_ffn_w_up"]])
    w_ffn = w_ffn.reshape(2, HJ, P, DC, P).transpose(4, 1, 3, 0, 2)
    bqkv = a["L0_attn_bqkv"]
    gu = np.stack([a["L0_ffn_w_gate"], a["L0_ffn_w_up"]], 1)
    gu = gu.reshape(E, 2, FE, DC, P).transpose(0, 4, 3, 1, 2).reshape(E, P, -1)
    ins = {
        "x": a["L0_attn_x"].reshape(T // P, P, D).transpose(1, 0, 2),
        "consts": shape_constants(),
        "ids": np.arange(T, dtype=np.int32).reshape(T // P, P).T,
        "w0": _chunks(a["L0_attn_Wqkv"]),
        "b0qk": bqkv[:2 * D].reshape(4, P).T,
        "b0v": bqkv[2 * D:],
        "w0out": _chunks(a["L0_attn_Wout"]),
        "b0out": a["L0_attn_bout"],
        "slopes0": a["L0_attn_slopes"],
        "gatew": _chunks(a["L0_ffn_gate_w"].T),
        "moe_in": gu,
        "moe_down": a["L0_ffn_w_down"].transpose(0, 2, 1),
        "slopes1": a["L1_attn_slope_rate"].reshape(H1),
        "w1": np.concatenate([v.reshape(P, -1) for v in (
            w_v, w_head, _chunks(a["L1_attn_w_out"].T), w_ffn, _chunks(a["L1_ffn_w_down"].T))], 1),
        "norm1": a["L1_attn_norm_w"].reshape(H1, P).T,
        "identity": np.eye(P, dtype=np.float32),
    }
    nc = _bacc.Bacc("TRN2", target_bir_lowering=False, num_devices=1)
    arrays, args = {}, []
    for name, v in ins.items():
        v = np.ascontiguousarray(v)
        arrays[f"in_{name}"] = v
        args.append(nc.dram_tensor(f"in_{name}", v.shape, mybir.dt.from_np(v.dtype), kind="ExternalInput").ap())
    args.append(nc.dram_tensor("out_0", (T, D), F32, kind="ExternalOutput").ap())
    args.append(nc.dram_tensor("xhat_rows", (T, D), F32, kind="Internal").ap())
    args.append(nc.dram_tensor("slot_ids", (E * CAP, 1), I32, kind="Internal").ap())
    args.append(nc.dram_tensor("y_rows", (E * CAP, D), F32, kind="Internal").ap())
    build(nc, *args)
    r = _run(nc, [arrays], core_ids=[0])
    return r.results[0]["out_0"].reshape(NB, SEQ, D)
```

```python
from contextlib import ExitStack

import numpy as np

import concourse.bass as bass
from concourse import mybir

F32 = mybir.dt.float32
F32R = mybir.dt.float32r
BF16 = mybir.dt.bfloat16
I32 = mybir.dt.int32
U32 = mybir.dt.uint32
ALU = mybir.AluOpType
ACT = mybir.ActivationFunctionType
AX = mybir.AxisListType.X

P = 128
NB, SEQ, D = 8, 256, 256
T = NB * SEQ
TB = SEQ // P
DC = D // P
H0, HD0 = 16, 16
G0 = 4
NG = H0 // G0
E, TOPK, FE = 64, 8, 96
CAP = 2 * T * TOPK // E
CT = CAP // P
H1, HD1 = 16, 128
C1 = H1 * HD1
FH = 1024
HJ = FH // P
EPS_LN, EPS_RMS = 1e-5, 1e-6
LOWEST = -3.0e38
VG = C1 // 512
HW, FW = DC * 3 * HD1, DC * 2 * P
OUT_SPLIT = H1 - 2
RING = 4
LAYER0_R_WORDS = 2 * H0 * SEQ + 5 * DC * SEQ + 2 * DC * 3 * D
LAYER1_WORDS = 10350
LAYER1_R_WORDS = 4 * DC * 512 + 4 * DC * SEQ + 4 * SEQ
EXPERT_WORDS = 2 * (DC * 2 * FE + D) + (E + 2) * CT + 4 * CT * D + 2 * CAP
EXPERT_R_WORDS = 4 * (DC * 2 * FE + D) + 4 * DC * CAP + 4 * CAP
W1_WORDS = DC * C1 * 4 + H1 * D + 3 * HJ * D
W1_PIECES = E // 2
DROPPED = 65536.0

CONSTS = {}
_at = 0
for _name, _n in (("dist", SEQ), ("causal", SEQ), ("before", P), ("ones", P),
                  ("parity", 2), ("slot0", E)):
    CONSTS[_name] = (_at, _at + _n)
    _at += _n
NCONST = _at


def shape_constants():
    p = np.arange(P)[:, None]
    i = np.arange(SEQ)[None, :]
    c = np.zeros((P, NCONST), np.float32)

    def put(name, a):
        c[:, CONSTS[name][0]:CONSTS[name][1]] = a

    put("dist", np.maximum(i - p, 0))
    put("causal", i >= p)
    put("before", p < np.arange(P)[None, :])
    put("ones", 1.0)
    put("parity", np.concatenate([(p // HD0) % 2 == 0, (p // HD0) % 2 == 1], 1))
    put("slot0", np.arange(E)[None, :] * CAP + 1.0)
    return c


class Steps:

    def __init__(self, eng, sem, per, turn):
        self.eng, self.sem, self.per, self.base, self.n = eng, sem, per, turn * per, 0

    def done(self, ins):
        ins.then_inc(self.sem, 1)
        self.n += 1

    def settled(self, alone=None):
        self.eng.wait_ge(self.sem, self.base + self.n)
        if alone is not None:
            self.eng.sem_inc(alone, 1)

    def end(self):
        assert self.n == self.per, (self.n, self.per)


def build(nc, x, consts, ids, w0, b0qk, b0v, w0out, b0out, slopes0, gatew, moe_in, moe_down,
          slopes1, w1, norm1, identity, out,
          xhat_rows, slot_ids, y_rows):
    with ExitStack() as ctx:
        def sb(name, shape, dt=F32):
            return ctx.enter_context(nc.sbuf_tensor(name, shape, dt))

        def sem(name):
            return ctx.enter_context(nc.semaphore(name))

        bank = [ctx.enter_context(nc.psum_tensor(f"bank{i}", [P, 512], F32)) for i in range(8)]

        X = sb("X", [P, T // P, D])
        ident = sb("ident", [P, P])
        one = sb("one", [P, 1])
        tokens = sb("tokens", [P, T // P], I32)
        slope = sb("slope", [P, H0 + H1])
        nslope = sb("nslope", [P, H0 + H1])
        D1 = sb("D1", [P, H1, SEQ])
        W1 = sb("W1", [P, W1_WORDS])
        nrm = sb("nrm", [P, H1])
        SLOT = sb("SLOT", [P, NB, TB * TOPK], I32)
        WGT = sb("WGT", [P, NB, TB * TOPK])
        ones_b = sb("ones_b", [P, P], BF16)
        before_b = sb("before_b", [P, P], BF16)
        sel_b = sb("sel_b", [P, TB, E], BF16)
        seen_b = sb("seen_b", [P, TB, E], BF16)
        bn = sb("bn", [P, TB, 6])
        bn2 = sb("bn2", [P, TB, 6])
        mv = sb("mv", [P, TB, 2])
        mv2 = sb("mv2", [P, TB, 2])
        var = sb("var", [P, TB])
        var2 = sb("var2", [P, TB])
        rstd = sb("rstd", [P, TB])
        rstd2 = sb("rstd2", [P, TB])

        half = sb("half", [P, TB])


        def region(tensor):
            at = [0]

            def take(shape, dt=F32):
                n = int(np.prod(shape))
                v = tensor[:, at[0]:at[0] + n]
                at[0] += n
                assert at[0] <= tensor.shape[1], at[0]
                if dt != tensor.dtype:
                    v = v.bitcast(dt)
                if len(shape) > 1:
                    names = "abcd"[:len(shape)]
                    v = v.rearrange(f"p ({' '.join(names)}) -> p {' '.join(names)}",
                                    **{n: s for n, s in zip(names, shape)})
                return v
            return take

        def stage(*tensors):
            with ExitStack() as own:
                takes = [region(own.enter_context(nc.sbuf_tensor(name, [P, words], dt)))
                         for name, words, dt in tensors]
            return takes if len(takes) > 1 else takes[0]

        take = region(W1)
        W1v = take([VG, DC * 512])
        W1h = take([H1, HW + D])
        WF = take([HJ, FW + D])

        def out_weights(h):
            return W1h[:, h + 2, HW:] if h < OUT_SPLIT else WF[:, h - OUT_SPLIT, FW:]

        take = region(W1)
        vz = take([TB, H0, P])
        take_r = stage(("layer0_r", LAYER0_R_WORDS, F32R))
        qzhi, qzlo = (take_r([H0, SEQ], F32R) for _ in range(2))
        qhi, khi, klo, xAhi, xAlo = (take_r([DC, SEQ], F32R) for _ in range(5))
        W0hi, W0lo = (take_r([DC, 3 * D], F32R) for _ in range(2))
        cst = take([NCONST])

        def const(name):
            a, b = CONSTS[name]
            return cst[:, a:b]

        dist, causal, parity, slot0, ones = (const(n) for n in ("dist", "causal", "parity", "slot0", "ones"))
        D0 = take([H0, SEQ])
        W0 = take([DC, 3 * D])
        W0o = take([DC, D])
        GW = take([DC, E])
        bqk = take([4])
        bv = take([D])
        bo = take([D])
        xhA = take([TB, D])
        qf = take([DC, SEQ])
        qrest = take([DC, SEQ])
        PA = [take([3, 512]) for _ in range(2)]
        oTA = take([DC, SEQ])
        x1 = take([TB, D])
        xh2 = take([TB, D])
        x2T = take([DC, SEQ])
        logit = take([TB, E])
        left = take([TB, E])
        sel = take([TB, E])
        prob = take([TB, E])
        keep = take([TB, E])
        key = take([TB, E])
        top = take([TB, 8])
        ntop = take([TB])
        psumx = take([TB])
        rsum = take([TB])
        slotf = take([TB, TOPK])
        eq = take([TB, TOPK, E])
        wsum = take([TB * TOPK])
        scat = [take([TB * TOPK], I32) for _ in range(2)]
        tok = [take([TB], I32) for _ in range(2)]
        no_id = take([CAP * E // P // 2])

        take, take_r = stage(("experts", EXPERT_WORDS, F32), ("experts_r", EXPERT_R_WORDS, F32R))
        WE = DC * 2 * FE
        Wraw = [take([WE + D]) for _ in range(2)]
        Whi, Wlo = ([take_r([WE + D], F32R) for _ in range(2)] for _ in range(2))
        all_ids = take([E, CT], I32)
        idx = [take([CT], I32) for _ in range(2)]
        xg = [take([CT, D]) for _ in range(2)]
        xhi, xlo = ([take_r([DC, CAP], F32R) for _ in range(2)] for _ in range(2))
        hB = [take([CAP]) for _ in range(2)]
        hhi, hlo = ([take_r([CAP], F32R) for _ in range(2)] for _ in range(2))
        yo = [take([CT, D]) for _ in range(2)]

        take, take_r = stage(("layer1", LAYER1_WORDS, F32), ("layer1_r", LAYER1_R_WORDS, F32R))
        rows = take([TB * RING, D])
        sidx = take([TB * TOPK], I32)
        xh3 = take([TB, D])
        Whi1, Wlo1 = ([take_r([DC * 512], F32R) for _ in range(2)] for _ in range(2))
        x3hi, x3lo, x4hi, x4lo = (take_r([DC, SEQ], F32R) for _ in range(4))
        qkD = [take([2, SEQ]) for _ in range(2)]
        vD = take([TB, C1])
        wcur = take([TB * TOPK])
        PD = [take([3, P]) for _ in range(2)]
        sgF = [p.rearrange("p a b -> p (a b)")[:, 0:SEQ] for p in PD]
        gD = [take([SEQ]) for _ in range(2)]
        ghi, glo = ([take_r([SEQ], F32R) for _ in range(2)] for _ in range(2))
        sq = [take([SEQ]) for _ in range(2)]
        ssq = take([SEQ])
        x3 = take([TB, D])
        xh4 = xh3

        NAMES = """
        x_first x_loaded ident_loaded consts_loaded small_loaded w0_loaded w0o_loaded norm_loaded table_filled
        no_id_ready xg_cleared nslope_ready decay0_exp decay1_exp decay0_ready decay1_ready bf_ready cleared cleared_v half_ready
        a_w0hi a_w0lo a_xlo a_qf a_qhi a_qrest a_klo
        a_xhat a_xT_ps a_xT a_q_ps a_k_ps a_v_ps a_q a_k a_v a_sc_ps a_prob a_pv_ps a_oT
        a_out_ps a_x1 a_xh2 a_x2T_ps a_x2T a_log_ps a_logit a_ln_steps a_var a_rstd a_ln2_steps a_var2 a_rstd2
        a_sel_steps a_ntop a_exp a_selb a_rank_ps a_pos_steps a_slot_steps a_scat a_tok a_ids a_stored a_x1sum
        b_first_ids b_all_ids b_idx b_x_ps b_xhi b_xlo b_whi b_wlo b_dhi b_dlo
        b_gu_ps b_silu b_h b_hhi b_hlo b_y_ps b_ya b_yb
        l1_loaded w1o_scaled dve_carrier pool_carrier
        d_sidx d_wcur d_comb_steps d_ln3_steps d_var3 d_rstd3 d_xh3 d_x3T_ps d_x3T d_x3lo d_x4lo d_whi d_wlo d_v_ps d_v
        d_qk_ps d_qk d_g_ps d_g d_s_ps d_p d_o_ps d_go d_sq d_ssq d_y_ps d_ssq_ps d_var d_rms d_x3
        d_ln4_steps d_var4 d_rstd4 d_xh4 d_x4T_ps d_x4T d_h_ps d_sg d_h d_hhi d_hlo d_down d_ghi d_glo d_out d_stored
        """.split()
        S = {n: sem(n) for n in NAMES}
        b_wgu = [sem(f"b_wgu{i}") for i in range(2)]
        b_wdn = [sem(f"b_wdn{i}") for i in range(2)]

        b_rows = [sem(f"b_rows{i}") for i in range(2)]
        b_stored = [sem(f"b_stored{i}") for i in range(2)]
        d_row = [sem(f"d_row{i}") for i in range(TB * TOPK)]

        def row_at(t, k):
            return t * RING + k % RING

        V_USE, F_USE, H_USE, USES = 0, VG, VG + HJ, VG + HJ + H1

        def use_number(turn, i):
            if isinstance(turn, int) and turn == 0:
                return i if i < F_USE else i - HJ
            n = turn * USES + (i - HJ)
            return n - VG if isinstance(turn, int) and turn == NB else n

        def uses(front, back):
            return [i for i in range(USES) if (back if F_USE <= i < H_USE else
                                               front or (back and H_USE <= i < H_USE + 2))]

        def two_ahead(turn, i, front, back):
            now = uses(front, back)
            last = isinstance(turn, int) and turn >= LASTB
            line = now + ([] if not front else uses(False, True)[:2] if last else uses(True, True)[:2])
            k = now.index(i) + 2
            if k >= len(line):
                return None
            return (turn if k < len(now) else turn + 1), line[k]

        def raw_weights(i):
            if i < F_USE:
                return W1v[:, i, :]
            if i < H_USE:
                return WF[:, i - F_USE, :] if i >= F_USE + 2 else WF[:, i - F_USE, 0:FW]
            return W1h[:, i - H_USE, :]

        def after(eng, name, value):
            if not isinstance(value, int) or value > 0:
                eng.wait_ge(S[name], value)

        NSMALL = 6

        B2 = 2
        FIRST_IDS = 4
        LASTB = NB - 1

        block = ctx.enter_context(nc.Block())

        @block.sync
        def _(sp):
            sp.dma_start(X[:, 0:TB, :], x[:, 0:TB, :]).then_inc(S["x_first"], 16)
            sp.dma_start(ident[:], identity).then_inc(S["ident_loaded"], 16)
            sp.dma_start(cst, consts).then_inc(S["consts_loaded"], 16)
            sp.dma_start(W0, w0).then_inc(S["w0_loaded"], 16)
            sp.dma_start(W0o, w0out).then_inc(S["w0o_loaded"], 16)
            sp.dma_start(GW, gatew).then_inc(S["w0o_loaded"], 16)
            sp.dma_start(nrm[:], norm1).then_inc(S["norm_loaded"], 16)
            sp.wait_ge(S["small_loaded"], 16 * NSMALL)
            sp.dma_start(X[:, TB:, :], x[:, TB:, :]).then_inc(S["x_loaded"], 16)
            sp.wait_ge(S["no_id_ready"], 1)
            n = no_id.shape[1]
            tab = slot_ids.rearrange("(a p n) o -> a p (n o)", a=E * CAP // (P * n), p=P)
            for a in range(tab.shape[0]):
                sp.dma_start(tab[a], no_id.bitcast(I32)).then_inc(S["table_filled"], 16)

            def store_xhat(b):
                sp.wait_ge(S["a_xh2"], b + 1)
                sp.dma_start(xhat_rows[bass.ds(b * SEQ, SEQ), :].rearrange("(t p) d -> p t d", p=P),
                             xh2).then_inc(S["a_stored"], 16)

            with sp.Fori(0, NB) as b:
                store_xhat(b)

            sp.wait_ge(S["a_scat"], NB)
            sp.wait_ge(S["decay1_ready"], 4)
            sp.wait_ge(S["a_stored"], 16 * NB)

            def load_ids(first, last, loaded):
                sp.dma_start(all_ids[:, first:last, :], slot_ids[first * CAP:last * CAP, :].rearrange(
                    "(e p c) o -> p e (c o)", p=P, c=CT)).then_inc(S[loaded], 16)

            def load_expert(e, s):
                after(sp, "b_wlo", e - 1)
                after(sp, "b_dlo", e - 1)
                sp.dma_start(Wraw[s][:, 0:WE], moe_in[bass.ds(e, 1)].rearrange("a p n -> (a p) n")
                             ).then_inc(b_wgu[s], 16)
                sp.dma_start(Wraw[s][0:FE, WE:], moe_down[bass.ds(e, 1)].rearrange("a f d -> (a f) d")
                             ).then_inc(b_wdn[s], 16)

            def store_expert(e, s):
                sp.wait_ge(S["b_ya"], e + 1)
                sp.wait_ge(S["b_yb"], e + 1)
                sp.dma_start(y_rows[bass.ds(e * CAP, CAP), :].rearrange("(p c) d -> p c d", c=CT),
                             yo[s]).then_inc(b_stored[s], 16)

            def expert_step(e, s, more_weights=True):
                if more_weights:
                    load_expert(e + 2, s)
                store_expert(e - 1, 1 - s)

            for s in range(2):
                load_expert(s, s)
            sp.wait_ge(S["a_ids"], 16 * NB * TB * TOPK)
            load_ids(0, FIRST_IDS, "b_first_ids")
            load_ids(FIRST_IDS, E, "b_all_ids")
            load_expert(2, 0)

            def load_layer1(i):
                n = W1_WORDS // W1_PIECES
                sp.dma_start(W1[:, bass.ds(i * n, n)], w1[:, bass.ds(i * n, n)]).then_inc(S["l1_loaded"], 16)

            with sp.Fori(0, E // B2 - 2) as i:
                expert_step(i * 2 + 1, 1)
                load_layer1(i)
                expert_step(i * 2 + 2, 0)
            expert_step(E - 3, 1)
            load_layer1(E // B2 - 2)
            expert_step(E - 2, 0, more_weights=False)
            load_layer1(E // B2 - 1)
            expert_step(E - 1, 1, more_weights=False)
            store_expert(E - 1, 1)

            for s in range(2):
                sp.wait_ge(b_stored[s], 16 * E // 2)

            with sp.Fori(0, NB) as b:
                sp.wait_ge(S["d_out"], b + 1)
                sp.dma_start(out[bass.ds(b * SEQ, SEQ), :].rearrange("(t p) d -> p t d", p=P),
                             x3).then_inc(S["d_stored"], 16)
            sp.wait_ge(S["d_stored"], 16 * NB)

        def own(b):
            return 1 if isinstance(b, int) and b == LASTB else 0

        def a_scatter(pool, b, pairs=range(TB * TOPK)):
            if pairs[0] == 0:
                if not own(b):
                    after(pool, "a_ids", b * (16 * TB * TOPK))
                pool.wait_ge(S["a_scat"], b + 1)
                pool.tensor_copy(tok[own(b)], tokens[:, bass.ds(b * TB, TB)]).then_inc(S["a_tok"], 1)
                pool.wait_ge(S["a_tok"], b + 1)
                pool.sem_inc(S["pool_carrier"], 1)
            for c in pairs:
                pool.indirect_dma_start(
                    slot_ids, bass.IndirectOffsetOnAxis(ap=scat[own(b)][:, c:c + 1].bitcast(U32), axis=0),
                    tok[own(b)][:, c // TOPK:c // TOPK + 1], None, bounds_check=E * CAP - 1, oob_is_err=False,
                ).then_inc(S["a_ids"], 16)

        def rsqrt(pool, ready, done, v, r, n):
            pool.wait_ge(S[ready], n)
            pool.tensor_tensor(r, v, half[:, 0:TB], ALU.pow).then_inc(S[done], 1)

        @block.gpsimd
        def _(pool):
            pool.memset(one[:], 1.0)
            pool.memset(half[:], -0.5).then_inc(S["half_ready"], 1)
            pool.memset(no_id, 1.0).then_inc(S["no_id_ready"], 1)
            pool.wait_ge(S["half_ready"], 1)
            rsqrt(pool, "a_var", "a_rstd", var[:], rstd[:], 1)
            pool.memset(qzhi.bitcast(F32), 0.0).then_inc(S["cleared"], 1)
            pool.memset(qzlo.bitcast(F32), 0.0).then_inc(S["cleared"], 1)

            def turn(b, ahead, back, scatter):
                if back:
                    rsqrt(pool, "a_var2", "a_rstd2", var2[:], rstd2[:], b)
                if scatter:
                    a_scatter(pool, b - 2)
                if ahead:
                    rsqrt(pool, "a_var", "a_rstd", var[:], rstd[:], b + 3)

            rsqrt(pool, "a_var", "a_rstd", var[:], rstd[:], 2)
            turn(0, True, False, False)
            turn(1, True, True, False)
            pool.wait_ge(S["small_loaded"], 16 * NSMALL)
            pool.wait_ge(S["table_filled"], 16 * (E * CAP // (P * no_id.shape[1])))
            turn(2, True, True, True)
            with pool.Fori(3, LASTB - 1) as b:
                turn(b, True, True, True)
            turn(LASTB - 1, False, True, True)
            turn(LASTB, False, True, True)
            a_scatter(pool, LASTB - 1, range(2))
            rsqrt(pool, "a_var2", "a_rstd2", var2[:], rstd2[:], NB)
            a_scatter(pool, LASTB - 1, range(2, TB * TOPK))
            a_scatter(pool, LASTB)

            pool.wait_ge(S["a_stored"], 16 * NB)
            pool.wait_ge(S["a_slot_steps"], NB * SLOT_STEPS)

            def gather(e, s):
                if not isinstance(e, int) or e >= B2:
                    pool.wait_ge(S["b_x_ps"], e - 1)
                    pool.wait_ge(b_rows[s], (e - s) * 32)
                    pool.sem_inc(S["pool_carrier"], 1)
                pool.tensor_copy(idx[s], all_ids[:, bass.ds(e, 1), :].rearrange("p a b -> p (a b)")
                                 ).then_inc(S["b_idx"], 1)
                pool.wait_ge(S["b_idx"], e + 1)
                pool.sem_inc(S["pool_carrier"], 1)
                for c in range(CT):
                    pool.indirect_dma_start(
                        xg[s][:, c, :], None, xhat_rows,
                        bass.IndirectOffsetOnAxis(ap=idx[s][:, c:c + 1].bitcast(U32), axis=0),
                        bounds_check=T - 1, oob_is_err=False).then_inc(b_rows[s], 16)

            pool.wait_ge(S["b_first_ids"], 16)
            pool.wait_ge(S["xg_cleared"], 1)
            for e in range(FIRST_IDS):
                gather(e, e % 2)
            pool.wait_ge(S["b_all_ids"], 16)
            with pool.Fori(FIRST_IDS // B2, E // B2) as i:
                for s in range(B2):
                    gather(i * B2 + s, s)

            for s in range(2):
                pool.wait_ge(b_stored[s], 16 * E // 2)
            pool.wait_ge(S["b_ya"], E)

            def slots_of(b):
                pool.tensor_copy(sidx, SLOT[:, b, :] if isinstance(b, int) else
                                 SLOT[:, bass.ds(b, 1), :].rearrange("p a n -> p (a n)")
                                 ).then_inc(S["d_sidx"], 1)
                pool.wait_ge(S["d_sidx"], b + 1)
                pool.sem_inc(S["pool_carrier"], 1)

            def gather_rows(b, k):
                if k >= RING:
                    pool.wait_ge(S["d_comb_steps"], b * COMB_STEPS + TB * (k - RING + 1))
                    pool.sem_inc(S["pool_carrier"], 1)
                for t in range(TB):
                    gather_row(t * TOPK + k, row_at(t, k))

            def gather_row(c, at):
                pool.indirect_dma_start(
                    rows[:, at, :], None, y_rows,
                    bass.IndirectOffsetOnAxis(ap=sidx[:, c:c + 1].bitcast(U32), axis=0),
                    bounds_check=E * CAP - 1, oob_is_err=False).then_inc(d_row[c], 16)

            slots_of(0)
            for k in range(TOPK):
                gather_rows(0, k)
            rsqrt(pool, "d_var3", "d_rstd3", var[:], rstd[:], 1)

            def dturn(b, ahead, back):
                if back:
                    rsqrt(pool, "d_var", "d_rms", var2[:], rstd2[:], b)
                    rsqrt(pool, "d_var4", "d_rstd4", var2[:], rstd2[:], b)
                if ahead:
                    pool.wait_ge(S["d_comb_steps"], (b + 1) * COMB_STEPS)
                    slots_of(b + 1)
                for h in range(H1):
                    if ahead and h < TOPK:

                        gather_rows(b + 1, h)
                    if ahead and h == 11:
                        rsqrt(pool, "d_var3", "d_rstd3", var[:], rstd[:], b + 2)
                    if h > 0:
                        pool.wait_ge(S["d_sq"], b * H1 + h + 1)
                        if h > 1:
                            pool.wait_ge(S["d_ssq"], b * (H1 - 1) + h - 1)
                        pool.tensor_tensor(ssq, ssq, sq[h % 2], ALU.add).then_inc(S["d_ssq"], 1)

            dturn(0, True, False)
            with pool.Fori(1, LASTB) as b:
                dturn(b, True, True)
            dturn(LASTB, False, True)
            rsqrt(pool, "d_var", "d_rms", var2[:], rstd2[:], NB)
            rsqrt(pool, "d_var4", "d_rstd4", var2[:], rstd2[:], NB)

        @block.tensor
        def _(pe):
            def transpose4(dst, src):
                for c in range(DC):
                    for t in range(TB):
                        ins = pe.transpose(dst[:, c * SEQ + t * P:c * SEQ + (t + 1) * P],
                                           src[:, t, c * P:(c + 1) * P], ident[:])
                return ins

            def a_trans(b):
                pe.wait_ge(S["a_xhat"], b + 1)
                after(pe, "a_pos_steps", (b - 2) * POS_STEPS)
                transpose4(bank[0], xhA).then_inc(S["a_xT_ps"], 1)

            def a_query(b):
                pe.wait_ge(S["a_xlo"], b + 1)
                after(pe, "a_x1", b - 1)
                a_feature_major(0, 2).then_inc(S["a_q_ps"], 1)

            def a_key(b):
                after(pe, "a_logit", b - 1)
                a_feature_major(1, 3).then_inc(S["a_k_ps"], 1)

            def a_feature_major(which, bk):
                pe.wait_ge(S["a_w0lo"], which + 1)
                for m in range(DC):
                    cols = slice(which * D + m * P, which * D + (m + 1) * P)
                    for k, (c, W, x_) in enumerate((c, W, x_) for c in range(DC) for W, x_ in (
                            (W0hi, xAhi), (W0hi, xAlo), (W0lo, xAhi))):
                        ins = pe.matmul(bank[bk][:, m * SEQ:(m + 1) * SEQ], W[:, c, cols], x_[:, c, :],
                                        start=(k == 0), stop=(k == 3 * DC - 1))
                return ins

            def a_value(b):
                after(pe, "a_v", 2 * b)
                pe.wait_ge(S["a_w0lo"], 3)
                for t in range(TB):
                    for k, (c, x_, W) in enumerate((c, x_, W) for c in range(DC) for x_, W in (
                            (xAhi, W0hi), (xAhi, W0lo), (xAlo, W0hi))):
                        ins = pe.matmul(bank[1][:, t * D:(t + 1) * D], x_[:, c, t * P:(t + 1) * P],
                                        W[:, c, 2 * D:3 * D], start=(k == 0), stop=(k == 3 * DC - 1))
                ins.then_inc(S["a_v_ps"], 1)

            def a_out(b):
                pe.wait_ge(S["a_oT"], b + 1)
                after(pe, "a_qf", b + 2 if not isinstance(b, int) or b < LASTB else NB)
                if isinstance(b, int) and b == 0:
                    pe.wait_ge(S["w0o_loaded"], 32)
                for t in range(TB):
                    for c in range(DC):
                        ins = pe.matmul(bank[2][:, t * D:(t + 1) * D], oTA[:, c, t * P:(t + 1) * P],
                                        W0o[:, c, :], start=(c == 0), stop=(c == DC - 1))
                ins.then_inc(S["a_out_ps"], 1)

            def a_scores(b, g):
                pe.wait_ge(S["a_q"], b * NG + g + 1)
                if g == 0:
                    pe.wait_ge(S["a_klo"], b + 1)
                m = g * G0 * HD0 // P
                heads = slice(g * G0, (g + 1) * G0)
                for n in range(3):
                    after(pe, "a_prob", b * (3 * NG) + 3 * g + n - 2)
                    for i, (k_, q) in enumerate(((khi, qzhi), (khi, qzlo), (klo, qzhi))):
                        if n < 2:
                            ins = pe.matmul(bank[4 + n][:, :], k_[:, m, 0:P],
                                            q[:, g * G0 + 2 * n:g * G0 + 2 * n + 2, :],
                                            start=(i == 0), stop=(i == 2))
                        else:
                            ins = pe.matmul(bank[4 + n][:, :], k_[:, m, P:SEQ], q[:, heads, P:SEQ],
                                            start=(i == 0), stop=(i == 2))
                    ins.then_inc(S["a_sc_ps"], 1)

            def a_attend(b, g):
                if g == 0:
                    after(pe, "a_oT", b)
                if g % 2 == 0:
                    pe.wait_ge(S["a_v"], 2 * b + g // 2 + 1)
                pe.wait_ge(S["a_prob"], b * (3 * NG) + 3 * g + 3)
                Pg = PA[g % 2]
                m = g // 2
                for hh in range(G0):
                    h = g * G0 + hh
                    col = (hh % 2) * SEQ
                    last = g % 2 == 1 and hh == G0 - 1
                    pe.matmul(bank[7][:, m * SEQ:(m + 1) * SEQ], vz[:, 0, h, :], Pg[:, hh // 2, col:col + SEQ],
                              start=(g % 2 == 0 and hh == 0), stop=last, skip_group_check=True)
                    ins = pe.matmul(bank[7][:, m * SEQ + P:(m + 1) * SEQ], vz[:, 1, h, :],
                                    Pg[:, 2, hh * P:(hh + 1) * P], start=False, stop=last,
                                    skip_group_check=True)
                ins.then_inc(S["a_pv_ps"], 1)

            def a_back2(b):
                pe.wait_ge(S["a_xh2"], b + 1)
                after(pe, "a_xlo", b + 3 if not isinstance(b, int) or b < LASTB - 1 else NB)
                transpose4(bank[0], xh2).then_inc(S["a_x2T_ps"], 1)

            def a_logits(b):
                pe.wait_ge(S["a_x2T"], b + 1)
                after(pe, "a_klo", b + 2 if not isinstance(b, int) or b < LASTB else NB)
                for t in range(TB):
                    for c in range(DC):
                        ins = pe.matmul(bank[3][:, t * E:(t + 1) * E], x2T[:, c, t * P:(t + 1) * P],
                                        GW[:, c, :], start=(c == 0), stop=(c == DC - 1))
                ins.then_inc(S["a_log_ps"], 1)

            def a_rank(b):
                pe.wait_ge(S["a_selb"], 2 * b + 2)
                for t in range(TB):
                    o = bank[0][:, t * E:(t + 1) * E]
                    pe.matmul(o, before_b[:], sel_b[:, t, :], start=True, stop=False)
                    ins = pe.matmul(o, ones_b[:], seen_b[:, t, :], start=False, stop=True)
                ins.then_inc(S["a_rank_ps"], 1)

            def turn(b, front, ahead, back):
                if front:
                    a_scores(b, 0)
                if back:
                    a_out(b - 1)
                if front:
                    a_scores(b, 1)
                    a_attend(b, 0)
                if ahead:
                    a_trans(b + 1)
                if front:
                    a_scores(b, 2)
                if back:
                    a_back2(b - 1)
                if front:
                    a_attend(b, 1)
                    a_scores(b, 3)
                if ahead:
                    a_query(b + 1)
                if back:
                    a_logits(b - 1)
                if front:
                    a_attend(b, 2)
                if ahead:
                    a_key(b + 1)
                    a_value(b + 1)
                if back:
                    a_rank(b - 1)
                if front:
                    a_attend(b, 3)

            pe.wait_ge(S["ident_loaded"], 16)
            a_trans(0)
            a_query(0)
            a_key(0)
            a_value(0)
            pe.wait_ge(S["bf_ready"], 2)
            pe.wait_ge(S["cleared"], 2)
            pe.wait_ge(S["cleared_v"], 1)
            turn(0, True, True, False)
            turn(1, True, True, True)
            with pe.Fori(2, LASTB) as b:
                turn(b, True, True, True)
            turn(LASTB, True, False, True)
            turn(NB, False, False, True)
            pe.wait_ge(S["a_pos_steps"], NB * POS_STEPS)

            def b_trans(e, s):
                pe.wait_ge(b_rows[s], (e - s) * 32 + 64)
                after(pe, "b_xlo", 2 * e)
                for c in range(DC):
                    for t in range(CT):
                        ins = pe.transpose(bank[c][:, t * P:(t + 1) * P], xg[s][:, t, c * P:(c + 1) * P], ident[:])
                ins.then_inc(S["b_x_ps"], 1)

            def b_hidden(e, s):
                pe.wait_ge(S["b_wlo"], e + 1)
                pe.wait_ge(S["b_xlo"], 2 * e + 2)
                after(pe, "b_h", e - 1)
                for w in range(2):
                    n = 0
                    for c in range(DC):
                        at = (c * 2 + w) * FE
                        for W, x_ in ((Whi, xhi), (Whi, xlo), (Wlo, xhi)):
                            ins = pe.matmul(bank[2 + 2 * s + w][0:FE, :], W[s][:, at:at + FE], x_[s][:, c, :],
                                            start=(n == 0), stop=(n == 3 * DC - 1))
                            n += 1
                    ins.then_inc(S["b_gu_ps"], 1)

            def b_out(e, s):
                pe.wait_ge(S["b_hlo"], e + 1)
                pe.wait_ge(S["b_dlo"], e + 1)
                for n in range(2):
                    after(pe, "b_ya" if n == 0 else "b_yb", e)
                    for t in range(2):
                        q = 2 * n + t
                        for k, (h, W) in enumerate(((hhi, Whi), (hhi, Wlo), (hlo, Whi))):
                            ins = pe.matmul(bank[6 + n][:, t * D:(t + 1) * D], h[s][0:FE, q * P:(q + 1) * P],
                                            W[s][0:FE, WE:], start=(k == 0), stop=(k == 2))
                    ins.then_inc(S["b_y_ps"], 1)

            def b_pair(i):
                for s in (1, 0):
                    e = i * 2 + (1 if s else 2)
                    b_trans(e + 1, 1 - s)
                    b_hidden(e, s)
                    b_out(e - 1, 1 - s)

            b_trans(0, 0)
            b_trans(1, 1)
            b_hidden(0, 0)

            b_pair(0)
            with pe.Fori(1, E // B2 - 1) as i:
                b_pair(i)
            b_hidden(E - 1, 1)
            b_out(E - 2, 0)
            b_out(E - 1, 1)
            pe.wait_ge(S["b_ya"], E)
            pe.wait_ge(S["b_yb"], E)

            pe.wait_ge(S["w1o_scaled"], 1)
            pe.wait_ge(S["l1_loaded"], 16 * W1_PIECES)

            def d_trans3(b):
                pe.wait_ge(S["d_xh3"], b + 1)
                after(pe, "d_x4lo", b - 1)
                after(pe, "d_out", b - 1)
                transpose4(bank[0], xh3).then_inc(S["d_x3T_ps"], 1)

            def d_values(b, tiles):
                for n in tiles:
                    t, g = n % 2, n // 2
                    if n == 0:
                        pe.wait_ge(S["d_x3lo"], b + 1)
                        after(pe, "d_qk", b * H1 - 1)
                    elif n == 1:
                        after(pe, "d_qk", b * H1)
                    elif n == 2:
                        after(pe, "d_p", b * H1)
                    elif n == 4:
                        after(pe, "d_go", b * H1)
                        after(pe, "d_sq", b * H1)
                    elif n >= 6:
                        pe.wait_ge(S["d_v"], b * 8 + n - 5)
                    s = g % 2
                    pe.wait_ge(S["d_whi"], use_number(b, V_USE + g) + 1)
                    for k, (x_, W, c) in enumerate((x_, W, c) for x_, W in (
                            (x3hi, Whi1), (x3lo, Whi1), (x3hi, Wlo1)) for c in range(DC)):
                        if k == 2 * DC:
                            pe.wait_ge(S["d_wlo"], use_number(b, V_USE + g) + 1)
                        ins = pe.matmul(bank[1 + n % 6][:, :], x_[:, c, t * P:(t + 1) * P],
                                        W[s][:, c * 512:(c + 1) * 512], start=(k == 0), stop=(k == 3 * DC - 1))
                    ins.then_inc(S["d_v_ps"], 1)

            def three_passes(outs, use, s, step, hi, lo):
                pe.wait_ge(S["d_whi"], use + 1)
                for n, (out, at) in enumerate(outs):
                    for c in range(DC):
                        for x_ in (hi, lo):
                            pe.matmul(out, Whi1[s][:, c * step + at:c * step + at + P], x_[:, c, :],
                                      start=(n == 0 and c == 0 and x_ is hi), stop=False, skip_group_check=True)
                pe.wait_ge(S["d_wlo"], use + 1)
                for out, at in outs:
                    for c in range(DC):
                        ins = pe.matmul(out, Wlo1[s][:, c * step + at:c * step + at + P], hi[:, c, :],
                                        start=False, stop=(c == DC - 1), skip_group_check=True)
                return ins

            def d_project(b, h):
                after(pe, "d_qk", b * H1 + h - 1)
                if h == 0:
                    pe.wait_ge(S["d_v"], b * 8 + 8)
                use = use_number(b, H_USE + h)
                three_passes([(bank[1 + h % 2][:, w * SEQ:(w + 1) * SEQ], w * P) for w in range(2)],
                             use, h % 2, 3 * P, x3hi, x3lo).then_inc(S["d_qk_ps"], 1)
                after(pe, "d_sq", b * H1 + h - 1)
                after(pe, "d_go", b * H1 + h - 1)
                three_passes([(bank[5 + h % 2][:, 0:SEQ], 2 * P)], use, h % 2, 3 * P, x3hi, x3lo
                             ).then_inc(S["d_g_ps"], 1)

            def d_scores(b, h):
                pe.wait_ge(S["d_qk"], b * H1 + h + 1)
                after(pe, "d_p", b * H1 + h - 1)
                qk = qkD[h % 2]
                pe.matmul(bank[3 + h % 2][:, 0:SEQ], qk[:, 1, 0:P], qk[:, 0, :], start=True, stop=True)
                pe.matmul(bank[3 + h % 2][:, SEQ:SEQ + P], qk[:, 1, P:SEQ], qk[:, 0, P:SEQ],
                          start=True, stop=True).then_inc(S["d_s_ps"], 1)

            def d_attend(b, h):
                pe.wait_ge(S["d_p"], b * H1 + h + 1)
                pe.wait_ge(S["d_g"], b * H1 + h + 1)
                Ph = PD[h % 2]
                o = bank[5 + h % 2]
                vh = slice(h * HD1, (h + 1) * HD1)
                pe.matmul(o[:, SEQ:2 * SEQ], vD[:, 0, vh], Ph[:, 0:2, :], start=True, stop=False)
                pe.matmul(o[:, SEQ + P:2 * SEQ], vD[:, 1, vh], Ph[:, 2, :], start=False,
                          stop=True).then_inc(S["d_o_ps"], 1)

            def d_project_out(b, h):
                if h < OUT_SPLIT:
                    pe.wait_ge(S["d_glo"], b * OUT_SPLIT + h + 1)
                    terms = [(ghi, Whi1), (ghi, Wlo1), (glo, Whi1)]
                else:
                    pe.wait_ge(S["d_go"], b * H1 + h + 1)
                    terms = [(gD, None)]
                if h == 0:
                    after(pe, "d_x3", b)
                for t in range(TB):
                    for k, (g, W) in enumerate(terms):
                        ins = pe.matmul(bank[7][:, t * D:(t + 1) * D], g[h % 2][:, t * P:(t + 1) * P],
                                        W[h % 2][:, HW:] if W else out_weights(h),
                                        start=(h == 0 and t == 0 and k == 0), stop=(h == H1 - 1),
                                        skip_group_check=True)
                ins.then_inc(S["d_y_ps"], 1)

            def d_square_sums(b):
                pe.wait_ge(S["d_ssq"], (b + 1) * (H1 - 1))
                after(pe, "d_x3lo", b + 2 if not isinstance(b, int) or b < LASTB else NB)
                for t in range(TB):
                    ins = pe.matmul(bank[0][:, t:t + 1], ssq[:, t * P:(t + 1) * P], one[:],
                                    start=True, stop=True)
                ins.then_inc(S["d_ssq_ps"], 1)

            def d_trans4(b):
                pe.wait_ge(S["d_xh4"], b + 1)
                pe.wait_ge(S["d_var"], b + 1)
                transpose4(bank[0], xh4).then_inc(S["d_x4T_ps"], 1)

            def d_ffn(b):
                pe.wait_ge(S["d_x4lo"], b + 1)
                for j in range(HJ):
                    if j == 0:
                        after(pe, "d_v", b * 8 + 16 if not isinstance(b, int) or b < LASTB else NB * 8)
                    if j >= 4:
                        pe.wait_ge(S["d_h"], b * HJ + j - 3)
                    three_passes([(bank[1 + j % 4][:, w * SEQ:(w + 1) * SEQ], w * P) for w in range(2)],
                                 use_number(b + 1, F_USE + j), j % 2, 2 * P, x4hi, x4lo
                                 ).then_inc(S["d_h_ps"], 1)
                    if j >= 2:
                        d_down(b, j - 2)

            def d_down(b, j):
                pe.wait_ge(S["d_hlo"], b * HJ + j + 1)
                pe.wait_ge(S["d_wlo"], use_number(b + 1, F_USE + j + 2) + 1)
                at = FW if j < HJ - 2 else HW
                for t in range(TB):
                    for k, (g, W) in enumerate(((ghi, Whi1), (ghi, Wlo1), (glo, Whi1))):
                        ins = pe.matmul(bank[0][:, t * D:(t + 1) * D], g[j % 2][:, t * P:(t + 1) * P],
                                        W[j % 2][:, at:at + D], start=(j == 0 and t == 0 and k == 0),
                                        stop=(j == HJ - 1), skip_group_check=True)
                ins.then_inc(S["d_down"], 1)

            def dturn(b, front, back):
                if back:
                    d_project_out(b - 1, H1 - 1)
                    d_square_sums(b - 1)
                if front:
                    d_values(b, range(2, 6))
                if back:
                    d_trans4(b - 1)
                if front:
                    d_values(b, range(6, 8))
                if back:
                    d_ffn(b - 1)
                if front:
                    if back:
                        pe.wait_ge(S["d_h"], (b - 1) * HJ + 5)
                    d_project(b, 0)
                if back:
                    d_down(b - 1, HJ - 2)
                    if not front:
                        d_down(b - 1, HJ - 1)
                if front:
                    for h in range(H1):
                        d_scores(b, h)
                        if h + 1 < H1:
                            d_project(b, h + 1)
                        if back and h == 0:
                            d_down(b - 1, HJ - 1)
                        if h + 1 == H1 - 1 and not (isinstance(b, int) and b == LASTB):
                            d_trans3(b + 1)
                        v_ahead = h == H1 - 1 and not (isinstance(b, int) and b == LASTB)
                        if v_ahead:
                            d_values(b + 1, range(1))
                        d_attend(b, h)
                        if h:
                            d_project_out(b, h - 1)
                        if v_ahead:
                            d_values(b + 1, range(1, 2))

            d_trans3(0)
            d_values(0, range(2))
            dturn(0, True, False)
            dturn(1, True, True)
            with pe.Fori(2, LASTB) as b:
                dturn(b, True, True)
            dturn(LASTB, True, True)
            dturn(NB, False, True)

        @block.scalar
        def _(act):
            act.dma_start(slope[:, 0:H0], slopes0.partition_broadcast(P)).then_inc(S["small_loaded"], 16)
            act.dma_start(slope[:, H0:], slopes1.partition_broadcast(P)).then_inc(S["small_loaded"], 16)
            act.dma_start(bqk, b0qk).then_inc(S["small_loaded"], 16)
            act.dma_start(bv, b0v.partition_broadcast(P)).then_inc(S["small_loaded"], 16)
            act.dma_start(bo, b0out.partition_broadcast(P)).then_inc(S["small_loaded"], 16)
            act.dma_start(tokens[:], ids).then_inc(S["small_loaded"], 16)

            def decay(l, dst, done, heads):
                for h in heads:
                    n = l * H0 + h
                    ins = nc.scalar.activation(dst[:, h, :], dist, ACT.Exp, scale=nslope[:, n:n + 1])
                    if h % 4 == 3:
                        ins.then_inc(S[done], 1)

            act.wait_ge(S["w0_loaded"], 16)
            for i in range(3):
                cols = slice(i * D, (i + 1) * D)
                nc.scalar.activation(W0hi[:, :, cols], W0[:, :, cols], ACT.Copy).then_inc(S["a_w0hi"], 1)

            def copy(dst, src, ready, n, done):
                act.wait_ge(S[ready], n)
                nc.scalar.activation(dst, src, ACT.Copy).then_inc(S[done], 1)

            def split(a, n=DC):
                return a.rearrange("p (a b) -> p a b", a=n)

            def a_xT(b):
                after(act, "a_v_ps", b)
                copy(xAhi, split(bank[0][:, :]), "a_xT_ps", b + 1, "a_xT")

            def a_query(b):
                act.wait_ge(S["a_q_ps"], b + 1)
                after(act, "a_q", NG * b)
                for m in range(DC):
                    ins = nc.scalar.activation(qf[:, m, :], bank[2][:, m * SEQ:(m + 1) * SEQ], ACT.Identity,
                                               bias=bqk[:, m:m + 1])
                ins.then_inc(S["a_qf"], 1)
                after(act, "a_qrest", b)
                copy(qhi, qf, "a_qf", b + 1, "a_qhi")

            def a_qz(b, groups):
                for g4 in groups:
                    after(act, "a_sc_ps", (b - 1) * (3 * NG) + 3 * g4 + 3)
                    act.wait_ge(S["a_qhi"], b + 1)
                    for dst, src in ((qzhi, qf), (qzlo, qrest)):
                        if dst is qzlo:
                            act.wait_ge(S["a_qrest"], b + 1)
                        for h in range(g4 * G0, (g4 + 1) * G0):
                            m, g, odd = h * HD0 // P, (h * HD0 % P) // 32, h % 2
                            r = slice(32 * g, 32 * g + 32)
                            ins = nc.scalar.activation(dst[r, h, :], src[r, m, :], ACT.Identity,
                                                       scale=parity[r, odd:odd + 1])
                    ins.then_inc(S["a_q"], 1)

            def a_keys(b):
                act.wait_ge(S["a_k_ps"], b + 1)
                after(act, "a_sc_ps", b * (3 * NG))
                for m in range(DC):
                    ins = nc.scalar.activation(khi[:, m, :], bank[3][:, m * SEQ:(m + 1) * SEQ], ACT.Identity,
                                               bias=bqk[:, 2 + m:3 + m])
                ins.then_inc(S["a_k"], 1)

            def a_oT(b):
                after(act, "a_out_ps", b)
                copy(oTA, split(bank[7][:, :]), "a_pv_ps", (b + 1) * NG, "a_oT")

            def a_back2(b):
                after(act, "a_log_ps", b)
                copy(x2T, split(bank[0][:, :]), "a_x2T_ps", b + 1, "a_x2T")

            def a_exp(b):
                act.wait_ge(S["a_ntop"], b + 1)
                after(act, "a_slot_steps", b * SLOT_STEPS)
                for t in range(TB):
                    ins = nc.scalar.activation(prob[:, t, :], logit[:, t, :], ACT.Exp, bias=ntop[:, t:t + 1],
                                               accum_out=psumx[:, t:t + 1])
                ins.then_inc(S["a_exp"], 1)

            def turn(b, front, ahead, back):
                if front:
                    a_qz(b, range(2, 4))
                if ahead:
                    a_xT(b + 1)
                if back:
                    a_back2(b - 1)
                if ahead:
                    a_query(b + 1)
                    a_qz(b + 1, range(1))
                    a_keys(b + 1)
                if back:
                    a_exp(b - 1)
                if front:
                    a_oT(b)
                if ahead:
                    a_qz(b + 1, range(1, 2))

            a_xT(0)
            act.wait_ge(S["consts_loaded"], 16)
            act.wait_ge(S["nslope_ready"], 1)
            decay(0, D0, "decay0_exp", range(H0 // 4))
            a_query(0)
            a_keys(0)
            act.wait_ge(S["cleared"], 2)
            a_qz(0, range(2))
            decay(0, D0, "decay0_exp", range(H0 // 4, H0))
            turn(0, True, True, False)
            turn(1, True, True, True)
            with act.Fori(2, LASTB) as b:
                turn(b, True, True, True)
            turn(LASTB, True, False, True)
            turn(NB, False, False, True)
            decay(1, D1, "decay1_exp", range(H1))
            act.wait_ge(S["a_slot_steps"], NB * SLOT_STEPS)
            act.wait_ge(S["a_stored"], 16 * NB)
            act.wait_ge(S["a_ids"], 16 * NB * TB * TOPK)

            def b_copy(e, s):
                after(act, "b_gu_ps", 2 * e - 2)
                act.wait_ge(S["b_x_ps"], e + 1)
                for c in range(DC):
                    nc.scalar.activation(xhi[s][:, c, :], bank[c][:, :], ACT.Copy).then_inc(S["b_xhi"], 1)

            def b_gate_up(e, s):
                act.wait_ge(b_wgu[s], (e - s) * 8 + 16)
                after(act, "b_gu_ps", 2 * e - 2)
                nc.scalar.activation(Whi[s][:, 0:WE], Wraw[s][:, 0:WE], ACT.Copy).then_inc(S["b_whi"], 1)

            def b_down(e, s):
                act.wait_ge(b_wdn[s], (e - s) * 8 + 16)
                after(act, "b_y_ps", 2 * e - 2)
                nc.scalar.activation(Whi[s][0:FE, WE:], Wraw[s][0:FE, WE:], ACT.Copy).then_inc(S["b_dhi"], 1)

            def b_silu(e, s):
                after(act, "b_hlo", e - 1)
                act.wait_ge(S["b_gu_ps"], 2 * e + 1)
                nc.scalar.activation(hB[s][0:FE, :], bank[2 + 2 * s][0:FE, :], ACT.Silu).then_inc(S["b_silu"], 1)

            def b_hidden(e, s):
                after(act, "b_y_ps", 2 * e - 2)
                copy(hhi[s][0:FE, :], hB[s][0:FE, :], "b_h", e + 1, "b_hhi")

            def b_result(e, s):
                if not isinstance(e, int) or e >= 2:
                    act.wait_ge(b_stored[s], (e - s) * 8)
                copy(yo[s][:, 0:2, :], split(bank[6][:, :]), "b_y_ps", 2 * e + 1, "b_ya")

            def b_pair(i):
                for s in (1, 0):
                    e = i * 2 + (1 if s else 2)
                    b_copy(e + 1, 1 - s)
                    b_gate_up(e + 1, 1 - s)
                    b_silu(e, s)
                    b_hidden(e, s)
                    b_result(e - 1, 1 - s)
                    b_down(e + 1, 1 - s)

            for e in range(2):
                b_gate_up(e, e)
                b_down(e, e)
            for e in range(2):
                b_copy(e, e)
            b_silu(0, 0)
            b_hidden(0, 0)

            b_pair(0)
            with act.Fori(1, E // B2 - 1) as i:
                b_pair(i)
            b_silu(E - 1, 1)
            b_hidden(E - 1, 1)
            b_result(E - 2, 0)
            b_result(E - 1, 1)
            for s in range(2):
                act.wait_ge(b_stored[s], 16 * E // 2)
            act.wait_ge(S["b_yb"], E)

            def split_weights(turn, i):
                W = raw_weights(i)
                nc.scalar.activation(Whi1[i % 2][:, 0:W.shape[1]], W, ACT.Copy).then_inc(S["d_whi"], 1)

            def refill(turn, i, front, back):
                if two_ahead(turn, i, front, back):
                    split_weights(*two_ahead(turn, i, front, back))

            def d_high3(b):
                after(act, "d_g_ps", b * H1)
                copy(x3hi, split(bank[0][:, :]), "d_x3T_ps", b + 1, "d_x3T")

            def d_front(b, back, tiles):
                for n in tiles:
                    t, g = n % 2, n // 2
                    if back and n == 6:
                        d_high4(b - 1)
                    act.wait_ge(S["d_v_ps"], b * 8 + n + 1)
                    nc.scalar.activation(vD[:, t, g * 512:(g + 1) * 512], bank[1 + n % 6][:, :],
                                         ACT.Silu).then_inc(S["d_v"], 1)
                    if t == TB - 1:
                        refill(b, V_USE + g, True, back)

            def d_high4(b):
                after(act, "d_h_ps", b * HJ)
                copy(x4hi, split(bank[0][:, :]), "d_x4T_ps", b + 1, "d_x4T")

            def d_back(b, front):
                if not front:
                    d_high4(b)
                for j in range(HJ):
                    act.wait_ge(S["d_h_ps"], b * HJ + j + 1)
                    if j > 1:
                        act.wait_ge(S["d_hlo"], b * HJ + j - 1)
                    nc.scalar.activation(sgF[j % 2], bank[1 + j % 4][:, 0:SEQ], ACT.Silu).then_inc(S["d_sg"], 1)
                    if j > 1:
                        act.wait_ge(S["d_down"], b * HJ + j - 1)
                    refill(b + 1, F_USE + j, front, True)
                    if j == 0:
                        act.wait_ge(S["d_y_ps"], (b + 1) * H1)
                    copy(ghi[j % 2], sgF[j % 2], "d_h", b * HJ + j + 1, "d_hhi")

            def d_refill(b, h, back):
                act.wait_ge(S["d_g_ps"], b * H1 + h + 1)
                if h >= 2:
                    act.wait_ge(S["d_y_ps"], b * H1 + h - 1)
                elif back:
                    act.wait_ge(S["d_down"], b * HJ - 1 + h)
                refill(b, H_USE + h, True, back)

            def d_high_gated(b, h):
                if h == 0:
                    after(act, "d_down", b * HJ)
                copy(ghi[h % 2], gD[h % 2], "d_go", b * H1 + h + 1, "d_ghi")

            def d_silu(b, h):
                after(act, "d_s_ps", b * H1 + h - 1)
                act.wait_ge(S["d_qk_ps"], b * H1 + h + 1)
                nc.scalar.activation(qkD[h % 2][:, :, :], bank[1 + h % 2][:, :].rearrange("p (a b) -> p a b", a=2),
                                     ACT.Silu).then_inc(S["d_qk"], 1)
                act.wait_ge(S["d_g_ps"], b * H1 + h + 1)
                if h < 2:
                    after(act, "d_y_ps", (b - 1) * H1 + OUT_SPLIT + h + 1)
                else:
                    act.wait_ge(S["d_glo"], b * OUT_SPLIT + h - 1)
                nc.scalar.activation(gD[h % 2], bank[5 + h % 2][:, 0:SEQ], ACT.Tanh, scale=0.5).then_inc(S["d_g"], 1)

            def d_square(b, h):
                if h == 0:
                    after(act, "d_ssq_ps", b)
                elif h > 1:
                    after(act, "d_ssq", b * (H1 - 1) + h - 2)
                elif h == 1:
                    after(act, "d_ssq", b * (H1 - 1))
                act.wait_ge(S["d_o_ps"], b * H1 + h + 1)
                nc.scalar.activation(ssq if h == 0 else sq[h % 2], bank[5 + h % 2][:, SEQ:2 * SEQ],
                                     ACT.Square).then_inc(S["d_sq"], 1)

            def dturn(b, front, back):
                if front:
                    d_front(b, back, range(1, 8))
                if back:
                    d_back(b - 1, front)
                if front:
                    d_silu(b, 0)
                    for h in range(H1):
                        d_refill(b, h, back)
                        if 0 < h <= OUT_SPLIT:
                            d_high_gated(b, h - 1)
                        if h + 1 < H1:
                            d_silu(b, h + 1)
                        if h + 1 == H1 - 1 and not (isinstance(b, int) and b == LASTB):
                            d_high3(b + 1)
                        if h == H1 - 1 and not (isinstance(b, int) and b == LASTB):
                            d_front(b + 1, True, range(1))
                        d_square(b, h)

            act.wait_ge(S["l1_loaded"], 16 * W1_PIECES)
            for i in range(2):
                split_weights(0, V_USE + i)
            act.wait_ge(S["w1o_scaled"], 1)
            d_high3(0)
            d_front(0, False, range(1))
            dturn(0, True, False)
            dturn(1, True, True)
            with act.Fori(2, LASTB) as b:
                dturn(b, True, True)
            dturn(LASTB, True, True)
            dturn(NB, False, True)

        @block.vector
        def _(dve):
            nc.vector.memset(vz, 0.0).then_inc(S["cleared_v"], 1)
            nc.vector.memset(seen_b[:], 0.0)

            def decay(dst, ready, done, groups):
                for g in groups:
                    hs = slice(4 * g, 4 * g + 4)
                    dve.wait_ge(S[ready], g + 1)
                    nc.vector.tensor_tensor(dst[:, hs, :], dst[:, hs, :],
                                            causal.unsqueeze(1).broadcast_to([P, 4, SEQ]),
                                            ALU.mult).then_inc(S[done], 1)

            def variances(src, bn_, mv_, var_, steps_sem, per, turn, var_done):
                st = Steps(dve, S[steps_sem], per, turn)
                for t in range(TB):
                    st.done(nc.vector.bn_stats(bn_[:, t, :], src(t)))
                st.settled(S["dve_carrier"])
                for t in range(TB):
                    st.done(nc.vector.bn_aggr(mv_[:, t, :], bn_[:, t, :]))
                st.settled()
                st.end()
                nc.vector.tensor_scalar(var_[:], mv_[:, :, 1], EPS_LN, None, ALU.add).then_inc(S[var_done], 1)

            def scale_rows(src, dst, mv_, rstd_, turn, rstd_done, free, done):
                for name, n in free:
                    after(dve, name, n)
                dve.wait_ge(S[rstd_done], turn + 1)
                for t in range(TB):
                    ins = nc.vector.tensor_scalar(dst[:, t, :], src(t), mv_[:, t, 0:1], rstd_[:, t:t + 1],
                                                  ALU.subtract, ALU.mult)
                ins.then_inc(S[done], 1)

            def normalize(src, dst, bn_, mv_, var_, rstd_, steps_sem, per, turn, var_done, rstd_done, free, done):
                variances(src, bn_, mv_, var_, steps_sem, per, turn, var_done)
                scale_rows(src, dst, mv_, rstd_, turn, rstd_done, free, done)

            def xtile(b, t):
                return X[:, b * TB + t, :] if isinstance(b, int) else \
                    X[:, bass.ds(b * TB + t, 1), :].rearrange("p a d -> p (a d)")

            def a_stats(b):
                variances(lambda t: xtile(b, t), bn, mv, var, "a_ln_steps", 4, b, "a_var")

            def a_norm(b):
                scale_rows(lambda t: xtile(b, t), xhA, mv, rstd, b, "a_rstd", (("a_xT_ps", b),), "a_xhat")

            def low_part(dst, src, hi):
                return nc.vector.tensor_tensor(dst, src, hi.bitcast(F32), ALU.subtract)

            def a_xlo(b):
                dve.wait_ge(S["a_xT"], b + 1)
                after(dve, "a_v_ps", b)
                low_part(xAlo, bank[0][:, :].rearrange("p (a b) -> p a b", a=DC), xAhi).then_inc(S["a_xlo"], 1)

            def a_qrest(b):
                dve.wait_ge(S["a_qhi"], b + 1)
                low_part(qrest, qf, qhi).then_inc(S["a_qrest"], 1)

            def a_klo(b):
                dve.wait_ge(S["a_k"], b + 1)
                for m in range(DC):
                    ins = nc.vector.scalar_tensor_tensor(
                        out=klo[:, m, :], in0=bank[3][:, m * SEQ:(m + 1) * SEQ], scalar=bqk[:, 2 + m:3 + m],
                        in1=khi[:, m, :].bitcast(F32), op0=ALU.add, op1=ALU.subtract)
                ins.then_inc(S["a_klo"], 1)

            def a_vals(b, m):
                dve.wait_ge(S["a_v_ps"], b + 1)
                after(dve, "a_pv_ps", (b - 1) * NG + 2 * m + 2)
                n = H0 // 2
                for t in range(TB):
                    dst = vz[:, t, m * n:(m + 1) * n, :].rearrange("p a b -> p (a b)")
                    dst = bass.AP(dst.tensor, dst.offset, [dst.ap[0], [P + HD0, n], [1, HD0]])
                    ins = nc.vector.tensor_tensor(
                        dst, bank[1][:, t * D + m * P:t * D + (m + 1) * P].rearrange("p (a b) -> p a b", a=n),
                        bv[:, m * P:(m + 1) * P].rearrange("p (a b) -> p a b", a=n), ALU.add)
                ins.then_inc(S["a_v"], 1)

            def a_mask(b, g):
                if isinstance(b, int) and b == 0:
                    if g > 0:
                        decay(D0, "decay0_exp", "decay0_ready", [g])
                    dve.wait_ge(S["decay0_ready"], g + 1)
                after(dve, "a_pv_ps", b * NG + g - 1)
                for n in range(3):
                    dve.wait_ge(S["a_sc_ps"], b * (3 * NG) + 3 * g + n + 1)
                    if n < 2:
                        h = g * G0 + 2 * n
                        o, s, d = PA[g % 2][:, n, :].rearrange("p (a b) -> p a b", a=2), \
                            bank[4 + n][:, :].rearrange("p (a b) -> p a b", a=2), D0[:, h:h + 2, :]
                    else:
                        o, s, d = PA[g % 2][:, n, :].rearrange("p (a b) -> p a b", a=G0), \
                            bank[4 + n][:, :].rearrange("p (a b) -> p a b", a=G0), D0[:, g * G0:g * G0 + G0, 0:P]
                    nc.vector.tensor_tensor(o, s, d, ALU.mult).then_inc(S["a_prob"], 1)

            def a_residual(b):
                dve.wait_ge(S["a_out_ps"], b + 1)
                nc.vector.tensor_tensor(x1, bank[2][:, :].rearrange("p (a b) -> p a b", a=TB),
                                        bo.unsqueeze(1).broadcast_to([P, TB, D]), ALU.add).then_inc(S["a_x1"], 1)
                dve.wait_ge(S["a_x1"], b + 1)
                for t in range(TB):
                    nc.vector.tensor_tensor(x1[:, t, :], x1[:, t, :], xtile(b, t), ALU.add).then_inc(S["a_x1sum"], 1)
                dve.wait_ge(S["a_x1sum"], 2 * b + 2)
                variances(lambda t: x1[:, t, :], bn2, mv2, var2, "a_ln2_steps", 4, b, "a_var2")

            def a_norm2(b):
                for t in range(TB):
                    nc.vector.tensor_scalar(xtile(b, t), x1[:, t, :], 1.0, None, ALU.mult)
                scale_rows(lambda t: x1[:, t, :], xh2, mv2, rstd2, b, "a_rstd2",
                           (("a_x2T_ps", b), ("a_stored", 16 * b)), "a_xh2")

            def a_select(b):
                st = Steps(dve, S["a_sel_steps"], SEL_STEPS, b)
                dve.wait_ge(S["a_log_ps"], b + 1)
                nc.vector.tensor_copy(logit, bank[3][:, 0:TB * E].rearrange("p (a b) -> p a b", a=TB)
                                      ).then_inc(S["a_logit"], 1)
                dve.wait_ge(S["a_logit"], b + 1)
                dve.sem_inc(S["dve_carrier"], 1)
                for t in range(TB):
                    st.done(nc.vector.max(top[:, t, :], logit[:, t, :]))
                st.settled()
                nc.vector.tensor_scalar(ntop, top[:, :, 0], -1.0, None, ALU.mult).then_inc(S["a_ntop"], 1)
                for t in range(TB):
                    st.done(nc.vector.match_replace(left[:, t, :], top[:, t, :], logit[:, t, :], LOWEST))
                st.settled()
                st.done(nc.vector.tensor_scalar(sel, left, LOWEST, None, ALU.is_le))
                st.settled()
                st.end()
                after(dve, "a_rank_ps", b)
                nc.vector.tensor_copy(sel_b[:], sel).then_inc(S["a_selb"], 1)
                nc.vector.tensor_tensor(seen_b[:, 1, :], seen_b[:, 0, :], sel[:, 0, :],
                                        ALU.add).then_inc(S["a_selb"], 1)

            def a_places(b):
                st = Steps(dve, S["a_pos_steps"], POS_STEPS, b)
                dve.wait_ge(S["a_rank_ps"], b + 1)
                pos = bank[0][:, 0:TB * E].rearrange("p (a b) -> p a b", a=TB)
                st.done(nc.vector.tensor_tensor(seen_b[:, 0, :], seen_b[:, 1, :], sel[:, 1, :], ALU.add))
                st.done(nc.vector.tensor_scalar(keep, pos, float(CAP), None, ALU.is_lt))
                st.done(nc.vector.scalar_tensor_tensor(
                    out=key, in0=pos, scalar=float(CAP - 1),
                    in1=slot0.unsqueeze(1).broadcast_to([P, TB, E]), op0=ALU.min, op1=ALU.add))
                st.settled()
                st.done(nc.vector.tensor_tensor(key, key, sel, ALU.mult))
                st.done(nc.vector.tensor_tensor(keep, keep, sel, ALU.mult))
                st.end()

            def a_slots1(b):
                st = Steps(dve, S["a_slot_steps"], SLOT_STEPS, b)
                dve.wait_ge(S["a_exp"], b + 1)
                st.done(nc.vector.reciprocal(rsum, psumx))
                dve.wait_ge(S["a_pos_steps"], (b + 1) * POS_STEPS)
                st.settled(S["dve_carrier"])
                for t in range(TB):
                    st.done(nc.vector.max(slotf[:, t, :], key[:, t, :]))
                    st.done(nc.vector.scalar_tensor_tensor(out=prob[:, t, :], in0=prob[:, t, :],
                                                           scalar=rsum[:, t:t + 1], in1=keep[:, t, :],
                                                           op0=ALU.mult, op1=ALU.mult))
                st.settled()
                st.done(nc.vector.tensor_tensor(eq, key.unsqueeze(2).broadcast_to([P, TB, TOPK, E]),
                                                slotf.unsqueeze(3).broadcast_to([P, TB, TOPK, E]), ALU.is_equal))
                assert st.n == SLOT1_STEPS

            def a_slots2(b):
                st = Steps(dve, S["a_slot_steps"], SLOT_STEPS, b)
                st.n = SLOT1_STEPS
                st.settled()
                st.done(nc.vector.tensor_tensor(eq, eq, prob.unsqueeze(2).broadcast_to([P, TB, TOPK, E]), ALU.mult))
                st.settled()
                st.done(nc.vector.tensor_reduce(wsum, eq.rearrange("p a b c -> p (a b) c"), AX, ALU.add))
                st.settled()
                flat = slotf.rearrange("p a b -> p (a b)")

                def of_batch(tensor):
                    return tensor[:, b, :] if isinstance(b, int) else \
                        tensor[:, bass.ds(b, 1), :].rearrange("p a n -> p (a n)")

                st.done(nc.vector.tensor_scalar(of_batch(WGT), wsum, 1.0, None, ALU.mult))
                st.done(nc.vector.tensor_scalar(of_batch(SLOT), flat, -1.0, None, ALU.add))
                st.done(nc.vector.tensor_scalar(wsum, wsum, 0.0, DROPPED, ALU.is_le, ALU.mult))
                st.settled()
                st.done(nc.vector.scalar_tensor_tensor(out=wsum, in0=flat, scalar=-1.0, in1=wsum,
                                                       op0=ALU.add, op1=ALU.add))
                st.end()

            def a_slots3(b):
                dve.wait_ge(S["a_slot_steps"], (b + 1) * SLOT_STEPS)
                if not own(b):
                    after(dve, "a_ids", b * (16 * TB * TOPK))
                nc.vector.tensor_copy(scat[own(b)], wsum).then_inc(S["a_scat"], 1)

            def turn(b, stats, front, ahead, back, back2):
                if front:
                    a_vals(b, 1)
                    a_mask(b, 0)
                if back2 and not ahead:
                    a_slots2(b - 2)
                    a_slots3(b - 2)
                if back:
                    a_residual(b - 1)
                if ahead:
                    a_norm(b + 1)
                if back:
                    a_norm2(b - 1)
                if front:
                    a_mask(b, 1)
                if ahead:
                    a_xlo(b + 1)
                if back2 and ahead:
                    a_slots2(b - 2)
                    a_slots3(b - 2)
                if front:
                    a_mask(b, 2)
                    a_mask(b, 3)
                if ahead:
                    a_qrest(b + 1)
                if back:
                    a_select(b - 1)
                if ahead:
                    a_klo(b + 1)
                    a_vals(b + 1, 0)
                if stats:
                    a_stats(b + 2)
                if back:
                    a_places(b - 1)
                    a_slots1(b - 1)
                    if not ahead:
                        a_slots2(b - 1)
                        if not front:
                            a_slots3(b - 1)

            dve.wait_ge(S["x_first"], 16)
            a_stats(0)
            a_norm(0)
            dve.wait_ge(S["small_loaded"], 16 * NSMALL)
            nc.vector.tensor_scalar(nslope[:], slope[:], -1.0, None, ALU.mult).then_inc(S["nslope_ready"], 1)
            dve.wait_ge(S["consts_loaded"], 16)

            nc.vector.tensor_copy(ones_b[:], ones).then_inc(S["bf_ready"], 1)
            nc.vector.tensor_copy(before_b[:], const("before")).then_inc(S["bf_ready"], 1)
            dve.wait_ge(S["w0_loaded"], 16)
            for i in range(3):
                cols = slice(i * D, (i + 1) * D)
                dve.wait_ge(S["a_w0hi"], i + 1)
                low_part(W0lo[:, :, cols], W0[:, :, cols], W0hi[:, :, cols]).then_inc(S["a_w0lo"], 1)
                if i == 0:
                    a_xlo(0)
            a_qrest(0)
            a_klo(0)
            decay(D0, "decay0_exp", "decay0_ready", range(1))
            dve.wait_ge(S["cleared_v"], 1)
            a_vals(0, 0)
            dve.wait_ge(S["x_loaded"], 16)
            a_stats(1)
            turn(0, True, True, True, False, False)
            turn(1, True, True, True, True, False)
            turn(2, True, True, True, True, True)
            with dve.Fori(3, LASTB - 1) as b:
                turn(b, True, True, True, True, True)
            turn(LASTB - 1, False, True, True, True, True)
            turn(LASTB, False, True, False, True, True)
            a_slots3(LASTB - 1)
            turn(NB, False, False, False, True, False)
            decay(D1, "decay1_exp", "decay1_ready", range(4))
            dve.wait_ge(S["a_ids"], 16 * NB * TB * TOPK)
            dve.wait_ge(S["a_stored"], 16 * NB)

            def b_copy(e, s):
                after(dve, "b_gu_ps", 2 * e - 2)
                for c in range(DC):
                    dve.wait_ge(S["b_xhi"], 2 * e + c + 1)
                    nc.vector.tensor_tensor(xlo[s][:, c, :], bank[c][:, :], xhi[s][:, c, :].bitcast(F32),
                                            ALU.subtract).then_inc(S["b_xlo"], 1)

            def b_gate_up(e, s):
                dve.wait_ge(S["b_whi"], e + 1)
                after(dve, "b_gu_ps", 2 * e - 2)
                nc.vector.tensor_tensor(Wlo[s][:, 0:WE], Wraw[s][:, 0:WE], Whi[s][:, 0:WE].bitcast(F32),
                                        ALU.subtract).then_inc(S["b_wlo"], 1)

            def b_down(e, s):
                dve.wait_ge(S["b_dhi"], e + 1)
                after(dve, "b_y_ps", 2 * e - 2)
                nc.vector.tensor_tensor(Wlo[s][0:FE, WE:], Wraw[s][0:FE, WE:], Whi[s][0:FE, WE:].bitcast(F32),
                                        ALU.subtract).then_inc(S["b_dlo"], 1)

            def b_mul(e, s):
                dve.wait_ge(S["b_silu"], e + 1)
                dve.wait_ge(S["b_gu_ps"], 2 * e + 2)
                nc.vector.tensor_tensor(hB[s][0:FE, :], hB[s][0:FE, :], bank[3 + 2 * s][0:FE, :],
                                        ALU.mult).then_inc(S["b_h"], 1)

            def b_rest(e, s):
                dve.wait_ge(S["b_hhi"], e + 1)
                after(dve, "b_y_ps", 2 * e - 2)
                nc.vector.tensor_tensor(hlo[s][0:FE, :], hB[s][0:FE, :], hhi[s][0:FE, :].bitcast(F32),
                                        ALU.subtract).then_inc(S["b_hlo"], 1)

            def b_result(e, s):
                if not isinstance(e, int) or e >= 2:
                    dve.wait_ge(b_stored[s], (e - s) * 8)
                dve.wait_ge(S["b_y_ps"], 2 * e + 2)
                nc.vector.tensor_copy(yo[s][:, 2:4, :], bank[7][:, :].rearrange("p (a b) -> p a b", a=2)
                                      ).then_inc(S["b_yb"], 1)

            def b_pair(i):
                for s in (1, 0):
                    e = i * 2 + (1 if s else 2)
                    b_copy(e + 1, 1 - s)
                    b_gate_up(e + 1, 1 - s)
                    b_mul(e, s)
                    b_rest(e, s)
                    b_result(e - 1, 1 - s)
                    b_down(e + 1, 1 - s)

            for s in range(2):
                ins = nc.vector.memset(xg[s], 0.0)
            ins.then_inc(S["xg_cleared"], 1)
            for e in range(2):
                b_gate_up(e, e)
                b_down(e, e)
            for e in range(2):
                b_copy(e, e)
            b_mul(0, 0)
            b_rest(0, 0)

            b_pair(0)
            with dve.Fori(1, E // B2 - 1) as i:
                b_pair(i)
            b_mul(E - 1, 1)
            b_rest(E - 1, 1)
            b_result(E - 2, 0)
            b_result(E - 1, 1)
            for s in range(2):
                dve.wait_ge(b_stored[s], 16 * E // 2)
            dve.wait_ge(S["b_ya"], E)



            def split_weights(turn, i):
                W = raw_weights(i)
                dve.wait_ge(S["d_whi"], use_number(turn, i) + 1)
                low_part(Wlo1[i % 2][:, 0:W.shape[1]], W, Whi1[i % 2][:, 0:W.shape[1]]).then_inc(S["d_wlo"], 1)

            def refill(turn, i, front, back):
                if two_ahead(turn, i, front, back):
                    split_weights(*two_ahead(turn, i, front, back))

            def d_low3(b):
                after(dve, "d_g_ps", b * H1)
                dve.wait_ge(S["d_x3T"], b + 1)
                low_part(x3lo, bank[0][:, :].rearrange("p (a b) -> p a b", a=DC), x3hi).then_inc(S["d_x3lo"], 1)

            def d_low4(b):
                after(dve, "d_h_ps", b * HJ)
                dve.wait_ge(S["d_x4T"], b + 1)
                low_part(x4lo, bank[0][:, :].rearrange("p (a b) -> p a b", a=DC), x4hi).then_inc(S["d_x4lo"], 1)

            dve.wait_ge(S["l1_loaded"], 16 * W1_PIECES)
            for i in range(2):
                split_weights(0, V_USE + i)
            dve.wait_ge(S["norm_loaded"], 16)
            for h in range(H1):
                ins = nc.vector.tensor_scalar(out_weights(h), out_weights(h), nrm[:, h:h + 1], 0.5,
                                              ALU.mult, ALU.mult)
            ins.then_inc(S["w1o_scaled"], 1)

            def d_combine(b, k):
                for t in range(TB):
                    c = t * TOPK + k
                    dve.wait_ge(d_row[c], b * 16 + 16)
                if k:
                    dve.wait_ge(S["d_comb_steps"], b * COMB_STEPS + TB * k)
                for t in range(TB):
                    c = t * TOPK + k
                    nc.vector.scalar_tensor_tensor(
                        out=xtile(b, t), in0=rows[:, row_at(t, k), :], scalar=wcur[:, c:c + 1],
                        in1=xtile(b, t), op0=ALU.mult, op1=ALU.add).then_inc(S["d_comb_steps"], 1)

            def d_weights(b):
                after(dve, "d_comb_steps", b * COMB_STEPS)
                nc.vector.tensor_scalar(wcur[:], WGT[:, b, :] if isinstance(b, int) else
                                        WGT[:, bass.ds(b, 1), :].rearrange("p a n -> p (a n)"),
                                        1.0, None, ALU.mult).then_inc(S["d_wcur"], 1)
                dve.wait_ge(S["d_wcur"], b + 1)

            def d_norm3(b):
                dve.wait_ge(S["d_comb_steps"], (b + 1) * COMB_STEPS)
                dve.sem_inc(S["dve_carrier"], 1)
                normalize(lambda t: xtile(b, t), xh3, bn, mv, var, rstd, "d_ln3_steps", 4, b, "d_var3",
                          "d_rstd3", (("d_x4T_ps", b - 1), ("d_x3T_ps", b)), "d_xh3")

            def d_mask(b, h):
                dve.wait_ge(S["d_s_ps"], b * H1 + h + 1)
                after(dve, "d_o_ps", b * H1 + h - 1)
                s = bank[3 + h % 2]
                nc.vector.tensor_tensor(PD[h % 2][:, 0:2, :].rearrange("p a b -> p (a b)"), s[:, 0:SEQ],
                                        D1[:, h, :], ALU.mult)
                nc.vector.tensor_tensor(PD[h % 2][:, 2, :], s[:, SEQ:SEQ + P], D1[:, h, 0:P],
                                        ALU.mult).then_inc(S["d_p"], 1)

            def d_gate(b, h):
                dve.wait_ge(S["d_sq"], b * H1 + h + 1)
                nc.vector.scalar_tensor_tensor(out=gD[h % 2], in0=gD[h % 2], scalar=1.0,
                                               in1=bank[5 + h % 2][:, SEQ:2 * SEQ], op0=ALU.add,
                                               op1=ALU.mult).then_inc(S["d_go"], 1)

            def d_mean_square(b):
                dve.wait_ge(S["d_ssq_ps"], b + 1)
                nc.vector.tensor_scalar(var2[:], bank[0][:, 0:TB], 1.0 / C1, EPS_RMS, ALU.mult,
                                        ALU.add).then_inc(S["d_var"], 1)

            def d_residual(b):
                dve.wait_ge(S["d_rms"], b + 1)
                after(dve, "d_stored", b * 16)
                for t in range(TB):
                    ins = nc.vector.scalar_tensor_tensor(out=x3[:, t, :], in0=bank[7][:, t * D:(t + 1) * D],
                                                         scalar=rstd2[:, t:t + 1], in1=xtile(b, t),
                                                         op0=ALU.mult, op1=ALU.add)
                ins.then_inc(S["d_x3"], 1)
                dve.wait_ge(S["d_x3"], b + 1)
                normalize(lambda t: x3[:, t, :], xh4, bn2, mv2, var2, rstd2, "d_ln4_steps", 4, b, "d_var4",
                          "d_rstd4", (("d_x3T_ps", b + 2 if not isinstance(b, int) or b < LASTB else NB),), "d_xh4")

            def d_ffn(b, front):
                for j in range(HJ):
                    dve.wait_ge(S["d_sg"], b * HJ + j + 1)
                    nc.vector.tensor_tensor(sgF[j % 2], sgF[j % 2], bank[1 + j % 4][:, SEQ:2 * SEQ],
                                            ALU.mult).then_inc(S["d_h"], 1)
                    refill(b + 1, F_USE + j, front, True)
                    dve.wait_ge(S["d_hhi"], b * HJ + j + 1)
                    low_part(glo[j % 2], sgF[j % 2], ghi[j % 2]).then_inc(S["d_hlo"], 1)

            def d_result(b):
                dve.wait_ge(S["d_down"], (b + 1) * HJ)
                nc.vector.tensor_tensor(x3, bank[0][:, :].rearrange("p (a b) -> p a b", a=TB), x3,
                                        ALU.add).then_inc(S["d_out"], 1)

            def dturn(b, ahead, front, back):
                if back:
                    d_mean_square(b - 1)
                if front:
                    refill(b, V_USE, True, back)
                if back:
                    d_residual(b - 1)
                if front:
                    for g in range(1, VG - 1):
                        refill(b, V_USE + g, True, back)
                if back:
                    d_low4(b - 1)
                if front:
                    refill(b, V_USE + VG - 1, True, back)
                if back:
                    d_ffn(b - 1, front)
                    if not front:
                        d_result(b - 1)
                if front:
                    for h in range(H1):
                        d_mask(b, h)
                        if 0 < h <= OUT_SPLIT:
                            dve.wait_ge(S["d_ghi"], b * OUT_SPLIT + h)
                            low_part(glo[(h - 1) % 2], gD[(h - 1) % 2], ghi[(h - 1) % 2]).then_inc(S["d_glo"], 1)
                        refill(b, H_USE + h, True, back)
                        if back and h == 0:
                            d_result(b - 1)
                        if ahead and h == 1:
                            d_weights(b + 1)
                        if ahead and 2 <= h < 2 + TOPK:
                            d_combine(b + 1, h - 2)
                        if ahead and h == 11:
                            d_norm3(b + 1)
                        if ahead and h == H1 - 2:
                            d_low3(b + 1)
                        d_gate(b, h)

            d_weights(0)
            for k in range(TOPK):
                d_combine(0, k)
            d_norm3(0)
            d_low3(0)
            dturn(0, True, True, False)
            dturn(1, True, True, True)
            with dve.Fori(2, LASTB) as b:
                dturn(b, True, True, True)
            dturn(LASTB, False, True, True)
            dturn(NB, False, False, True)


SLOT1_STEPS, SLOT_STEPS = 6, 12
POS_STEPS = 5
SEL_STEPS = 5
COMB_STEPS = TB * TOPK


def _chunks(a):
    return np.ascontiguousarray(a.reshape(-1, P, a.shape[1]).transpose(1, 0, 2))


def kernel(**inputs):
    import concourse.bacc as _bacc
    from concourse.bass_utils import run_bass_kernel_spmd as _run

    a = {k: np.asarray(v) for k, v in inputs.items()}
    w_qkv = a["L1_attn_w_qkv"].reshape(H1, 3, HD1, D)
    w_v = w_qkv[:, 2].reshape(VG, 512, DC, P).transpose(3, 0, 2, 1)
    w_head = np.concatenate([w_qkv[:, :2], a["L1_attn_w_gate"].reshape(H1, 1, HD1, D)], 1)
    w_head = w_head.reshape(H1, 3, HD1, DC, P).transpose(4, 0, 3, 1, 2)
    w_out, w_down = _chunks(a["L1_attn_w_out"].T), _chunks(a["L1_ffn_w_down"].T)
    w_ffn = np.stack([a["L1_ffn_w_gate"], a["L1_ffn_w_up"]])
    w_ffn = w_ffn.reshape(2, HJ, P, DC, P).transpose(4, 1, 3, 0, 2)
    bqkv = a["L0_attn_bqkv"]
    gu = np.stack([a["L0_ffn_w_gate"], a["L0_ffn_w_up"]], 1)
    gu = gu.reshape(E, 2, FE, DC, P).transpose(0, 4, 3, 1, 2).reshape(E, P, -1)
    ins = {
        "x": a["L0_attn_x"].reshape(T // P, P, D).transpose(1, 0, 2),
        "consts": shape_constants(),
        "ids": np.arange(T, dtype=np.int32).reshape(T // P, P).T,
        "w0": _chunks(a["L0_attn_Wqkv"]),
        "b0qk": bqkv[:2 * D].reshape(4, P).T,
        "b0v": bqkv[2 * D:],
        "w0out": _chunks(a["L0_attn_Wout"]),
        "b0out": a["L0_attn_bout"],
        "slopes0": a["L0_attn_slopes"],
        "gatew": _chunks(a["L0_ffn_gate_w"].T),
        "moe_in": gu,
        "moe_down": a["L0_ffn_w_down"].transpose(0, 2, 1),
        "slopes1": a["L1_attn_slope_rate"].reshape(H1),
        "w1": np.concatenate([v.reshape(P, -1) for v in (
            w_v,
            np.concatenate([w_head.reshape(P, H1, -1), np.concatenate([w_down[:, -2:], w_out[:, :-2]], 1)], 2),
            np.concatenate([w_ffn.reshape(P, HJ, -1), np.concatenate([w_out[:, -2:], w_down[:, :-2]], 1)], 2),
            )], 1),
        "norm1": a["L1_attn_norm_w"].reshape(H1, P).T,
        "identity": np.eye(P, dtype=np.float32),
    }
    nc = _bacc.Bacc("TRN2", target_bir_lowering=False, num_devices=1)
    arrays, args = {}, []
    for name, v in ins.items():
        v = np.ascontiguousarray(v)
        arrays[f"in_{name}"] = v
        args.append(nc.dram_tensor(f"in_{name}", v.shape, mybir.dt.from_np(v.dtype), kind="ExternalInput").ap())
    args.append(nc.dram_tensor("out_0", (T, D), F32, kind="ExternalOutput").ap())
    args.append(nc.dram_tensor("xhat_rows", (T, D), F32, kind="Internal").ap())
    args.append(nc.dram_tensor("slot_ids", (E * CAP, 1), I32, kind="Internal").ap())
    args.append(nc.dram_tensor("y_rows", (E * CAP, D), F32, kind="Internal").ap())
    build(nc, *args)
    r = _run(nc, [arrays], core_ids=[0])
    return r.results[0]["out_0"].reshape(NB, SEQ, D)
```
